# Optimizing a Trainium2 kernel written in Bass

```python
import numpy as np
import jax
import jax.numpy as jnp

def _softmax(x, axis=-1):
    return jax.nn.softmax(x, axis=axis)

def _gelu(x):
    return jax.nn.gelu(x, approximate=True)

def _silu(x):
    return jax.nn.silu(x)

def _sigmoid(x):
    return jax.nn.sigmoid(x)

def _layernorm(x, axis=-1, eps=1e-05):
    m = jnp.mean(x, axis=axis, keepdims=True)
    v = jnp.var(x, axis=axis, keepdims=True)
    return (x - m) / jnp.sqrt(v + eps)

def _scatter_add(tgt, idx, src, axis=0):
    return tgt.at[idx].add(src)

def _segment_sum(src, seg, n):
    return jax.ops.segment_sum(src, seg, n)
kernel_name = 'mk_gnn_preln_d2_gnn_r8_27dfb2'

def setup_inputs(seed: int=0):
    np.random.seed(seed)
    _w = jnp.asarray

    def _rec_inputs():
        import jax
        import jax.numpy as jnp
        _gk = jax.random.key(seed)
        x = -0.0002117 + 1 * jax.random.normal(jax.random.fold_in(_gk, 1), (6250, 512), jnp.float32)
        src = jax.random.randint(jax.random.fold_in(_gk, 2), (100000,), 0, 6250, jnp.int32)
        dst = jnp.minimum((6250 * jax.random.uniform(jax.random.fold_in(_gk, 3), (100000,)) ** 2.0).astype(jnp.int32), 49999)
        _o = jnp.argsort(dst, stable=True)
        src = src[_o]
        dst = dst[_o]
        return (x, src, dst)
    x, src, dst = _rec_inputs()

    def _L0_gnn_setup():
        import jax, jax.numpy as jnp
        import numpy as np
        N = 6250
        E = 50000
        IN_FEATS = 512
        HEADS = 8
        OUT_FEATS = 64
        NEG_SLOPE = 0.2
        key = jax.random.key(seed)
        ks = jax.random.split(key, 12)
        HF = HEADS * OUT_FEATS
        s = 1.0 / np.sqrt(IN_FEATS)
        inp = {'feat': jax.random.normal(ks[0], (N, IN_FEATS), dtype=jnp.float32), 'src': jax.random.randint(ks[1], (E,), 0, N, dtype=jnp.int32), 'dst': jax.random.randint(ks[2], (E,), 0, N, dtype=jnp.int32), 'W_src': jax.random.normal(ks[3], (IN_FEATS, HF), dtype=jnp.float32) * s, 'b_src': jax.random.normal(ks[4], (HF,), dtype=jnp.float32) * 0.01, 'W_dst': jax.random.normal(ks[5], (IN_FEATS, HF), dtype=jnp.float32) * s, 'b_dst': jax.random.normal(ks[6], (HF,), dtype=jnp.float32) * 0.01, 'W_val': jax.random.normal(ks[7], (IN_FEATS, HF), dtype=jnp.float32) * s, 'b_val': jax.random.normal(ks[8], (HF,), dtype=jnp.float32) * 0.01, 'attn_l': jax.random.normal(ks[9], (HEADS, OUT_FEATS), dtype=jnp.float32) * 0.1, 'attn_r': jax.random.normal(ks[10], (HEADS, OUT_FEATS), dtype=jnp.float32) * 0.1}
        return inp
    _L0_gnn_all = _L0_gnn_setup()
    _L0_gnn_in = {k: v for k, v in _L0_gnn_all.items() if k in ('W_src', 'b_src', 'W_dst', 'b_dst', 'W_val', 'b_val', 'attn_l', 'attn_r')}
    del _L0_gnn_all

    def _L1_gnn_setup():
        import jax, jax.numpy as jnp
        import numpy as np
        N_NODES = 6250
        N_EDGES = 50000
        D = 512
        SELF_LOOP_W = 2.0

        def _gcn_layer(x, W, b, src, dst, n_nodes):
            h = x @ W
            ones = jnp.ones(src.shape[0], dtype=h.dtype)
            deg = jax.ops.segment_sum(ones, dst, num_segments=n_nodes) + SELF_LOOP_W
            dinv = jnp.where(deg > 0, jax.lax.rsqrt(deg), 0.0)
            norm = dinv[src] * dinv[dst]
            msgs = h[src] * norm[:, None]
            agg = jax.ops.segment_sum(msgs, dst, num_segments=n_nodes)
            agg = agg + h * (SELF_LOOP_W * dinv * dinv)[:, None]
            return agg + b
        key = jax.random.key(seed)
        k0, k1, k2, k3 = jax.random.split(key, 4)
        t_rep = jax.random.normal(k0, (N_NODES, D), dtype=jnp.float32)
        edge_index = jax.random.randint(k1, (2, N_EDGES), 0, N_NODES, dtype=jnp.int64)
        W1 = jax.random.normal(k2, (D, D), dtype=jnp.float32) / np.sqrt(D).astype(np.float32)
        b1 = jnp.zeros((D,), jnp.float32)
        W2 = jax.random.normal(k3, (D, D), dtype=jnp.float32) / np.sqrt(D).astype(np.float32)
        b2 = jnp.zeros((D,), jnp.float32)
        return {'t_rep': t_rep, 'edge_index': edge_index, 'W1': W1, 'b1': b1, 'W2': W2, 'b2': b2}
    _L1_gnn_all = _L1_gnn_setup()
    _L1_gnn_in = {k: v for k, v in _L1_gnn_all.items() if k in ('W1', 'b1', 'W2', 'b2')}
    del _L1_gnn_all
    return {'x': x, 'src': src, 'dst': dst, 'L0_gnn_W_src': _L0_gnn_in['W_src'], 'L0_gnn_b_src': _L0_gnn_in['b_src'], 'L0_gnn_W_dst': _L0_gnn_in['W_dst'], 'L0_gnn_b_dst': _L0_gnn_in['b_dst'], 'L0_gnn_W_val': _L0_gnn_in['W_val'], 'L0_gnn_b_val': _L0_gnn_in['b_val'], 'L0_gnn_attn_l': _L0_gnn_in['attn_l'], 'L0_gnn_attn_r': _L0_gnn_in['attn_r'], 'L1_gnn_W1': _L1_gnn_in['W1'], 'L1_gnn_b1': _L1_gnn_in['b1'], 'L1_gnn_W2': _L1_gnn_in['W2'], 'L1_gnn_b2': _L1_gnn_in['b2']}

def reference(x, src, dst, L0_gnn_W_src, L0_gnn_b_src, L0_gnn_W_dst, L0_gnn_b_dst, L0_gnn_W_val, L0_gnn_b_val, L0_gnn_attn_l, L0_gnn_attn_r, L1_gnn_W1, L1_gnn_b1, L1_gnn_W2, L1_gnn_b2):
    import jax
    import jax.numpy as jnp

    def _L0_gnn_ref(feat, src, dst, W_src, b_src, W_dst, b_dst, W_val, b_val, attn_l, attn_r):
        import jax, jax.numpy as jnp
        import numpy as np
        N = 6250
        E = 50000
        IN_FEATS = 512
        HEADS = 8
        OUT_FEATS = 64
        NEG_SLOPE = 0.2
        feat_src = (feat @ W_src + b_src).reshape(N, HEADS, OUT_FEATS)
        feat_dst = (feat @ W_dst + b_dst).reshape(N, HEADS, OUT_FEATS)
        feat_v = (feat @ W_val + b_val).reshape(N, HEADS, OUT_FEATS)
        el = jnp.einsum('nhf,hf->nh', feat_src, attn_l)
        er = jnp.einsum('nhf,hf->nh', feat_dst, attn_r)
        e = el[src] + er[dst]
        e = jnp.where(e >= 0, e, NEG_SLOPE * e)
        e_max = jax.ops.segment_max(e, dst, num_segments=N)
        e_max = jnp.where(jnp.isfinite(e_max), e_max, 0.0)
        exp_e = jnp.exp(e - e_max[dst])
        denom = jax.ops.segment_sum(exp_e, dst, num_segments=N)
        a = exp_e / jnp.maximum(denom[dst], 1e-16)
        msg = feat_v[src] * a[:, :, None]
        rst = jax.ops.segment_sum(msg, dst, num_segments=N)
        return rst.reshape(N, HEADS * OUT_FEATS)

    def _L1_gnn_ref(t_rep, edge_index, W1, b1, W2, b2):
        import jax, jax.numpy as jnp
        import numpy as np
        N_NODES = 6250
        N_EDGES = 50000
        D = 512
        SELF_LOOP_W = 2.0

        def _gcn_layer(x, W, b, src, dst, n_nodes):
            h = x @ W
            ones = jnp.ones(src.shape[0], dtype=h.dtype)
            deg = jax.ops.segment_sum(ones, dst, num_segments=n_nodes) + SELF_LOOP_W
            dinv = jnp.where(deg > 0, jax.lax.rsqrt(deg), 0.0)
            norm = dinv[src] * dinv[dst]
            msgs = h[src] * norm[:, None]
            agg = jax.ops.segment_sum(msgs, dst, num_segments=n_nodes)
            agg = agg + h * (SELF_LOOP_W * dinv * dinv)[:, None]
            return agg + b
        src, dst = (edge_index[0], edge_index[1])
        x = _gcn_layer(t_rep, W1, b1, src, dst, N_NODES)
        x = jax.nn.relu(x)
        x = _gcn_layer(x, W2, b2, src, dst, N_NODES)
        x = jax.nn.relu(x)
        return x
    edge_index = jnp.stack([src, dst])
    h = jnp.maximum(_layernorm(x, axis=-1), 0.0)
    x = x + _L0_gnn_ref(h, src, dst, L0_gnn_W_src, L0_gnn_b_src, L0_gnn_W_dst, L0_gnn_b_dst, L0_gnn_W_val, L0_gnn_b_val, L0_gnn_attn_l, L0_gnn_attn_r)
    h = jnp.maximum(_layernorm(x, axis=-1), 0.0)
    x = x + _L1_gnn_ref(h, edge_index, L1_gnn_W1, L1_gnn_b1, L1_gnn_W2, L1_gnn_b2)
    return x

_drawn_inputs = setup_inputs


def setup_inputs(seed=0):
    import zlib

    import numpy as np

    out = dict(_drawn_inputs(seed))
    spreads = {'L1_gnn_b1': (0.0, 0.1), 'L1_gnn_b2': (0.0, 0.1)}
    factors = {'L0_gnn_b_src': 8.0,
     'L0_gnn_W_dst': 2.978,
     'L0_gnn_b_dst': 8.0,
     'L0_gnn_b_val': 6.481,
     'L0_gnn_attn_r': 2.827}
    for name, (base, spread) in spreads.items():
        noise = np.random.default_rng([zlib.crc32(name.encode()), seed]).standard_normal(out[name].shape)
        drawn = base * np.exp(spread * noise) if base else spread * noise
        out[name] = jnp.asarray(drawn.astype(out[name].dtype))
    for name, factor in factors.items():
        out[name] = (out[name] * factor).astype(out[name].dtype)
    return out
```

```python
import numpy as np
import concourse.bass as bass
from concourse import mybir
from contextlib import ExitStack

F32 = mybir.dt.float32
BF16 = mybir.dt.bfloat16
F16 = mybir.dt.float16
I32 = mybir.dt.int32
ALU = mybir.AluOpType
ACT = mybir.ActivationFunctionType
AX = mybir.AxisListType
ds = bass.ds

P = 128
N, E, D, H = 6250, 100000, 512, 8
F = D // H
KC = D // P
TILES = -(-N // P)
NP = TILES * P
LAST = N - (TILES - 1) * P
J = -(-E // P)
EP = J * P
GE = 2 * P
GROUPS = EP // GE
STEPS = GROUPS + TILES - 1
U = 4
SP = -(-STEPS // U) * U
BLOCKS = -(-SP // P)
AW = D + H
XL = 8
OS = 8
LAG = 2
JB = 23
HB = J // JB
EB = 17
EL_BATCHES = 22
J0 = EL_BATCHES * EB
PCOLS = J - J0
Q = 4
KT = 4
NA = -(-TILES // KT)
EARLY = 16
SB = 7
BIG = 1e38
EPS = 1e-5
SLOPE = 0.2


class Step:

    def __init__(self, k, j, count, inner, turn=None):
        self.k, self.j, self.count, self.inner, self.turn = k, j, count, inner, turn

    def live(self, lag=0):
        return self.inner or 0 <= self.k - lag < self.count

    def past(self, n, lag=0):
        return self.inner or self.k - lag >= n


def pipelined(eng, count, unroll, lag, body, tail=0):
    lo = -(-(lag + unroll) // unroll) * unroll
    hi = lo + (count - tail - lo) // unroll * unroll
    for k in range(lo):
        body(Step(k, k % unroll, count, False, k // unroll))
    with eng.Fori(0, (hi - lo) // unroll) as i:
        for j in range(unroll):
            body(Step(i * unroll + (lo + j), j, count, True, i + lo // unroll))
    for k in range(hi, count + lag):
        body(Step(k, k % unroll, count, False, k // unroll))


def build(nc, x, src, dst, W_src, b_src, W_dst, b_dst, W_val, b_val, attn_l, attn_r, W1, b1, W2, b2, out):
    ctx = ExitStack()
    with ctx:
        def sb(name, shape, dt=F32):
            return ctx.enter_context(nc.sbuf_tensor(name, shape, dt))

        def ps(name, shape):
            return ctx.enter_context(nc.psum_tensor(name, shape, F32))

        def sem(name):
            return ctx.enter_context(nc.semaphore(name))

        def dram(name, shape, dt=F32):
            return nc.dram_tensor(name, shape, dt, kind="Internal").ap()

        src_rows = dram("src_rows", [GROUPS, GE], I32)
        dst_rows = dram("dst_rows", [GROUPS, GE], I32)
        el_tab = dram("el_tab", [NP, H])
        er_tab = dram("er_tab", [EP + NP, H])
        w_tab = dram("w_tab", [GROUPS, GE * H])
        low_tab = dram("low_tab", [PCOLS, P], F16)
        v_tab = dram("v_tab", [NP, D])
        x1_tab = dram("x1_tab", [NP, D])
        h2_tab = dram("h2_tab", [NP, D])
        h3_tab = dram("h3_tab", [NP, D])

        big = sb("big", [P, TILES * AW])
        edge = sb("edge", [P, 2 * J * H])
        rows = sb("rows", [P, 2 * U, D])
        wmat = sb("wmat", [P, KC, D])
        bias = sb("bias", [P, D])
        ident = sb("ident", [P, P])
        ones = sb("ones", [P, P])
        tri = sb("tri", [P, P])
        iota_i = sb("iota_i", [P, P], I32)
        iota = sb("iota", [P, P])
        node_i = sb("node_i", [P, TILES], I32)
        low_i4 = sb("low_i4", [P, KT], I32)
        low_id = sb("low_id", [P, KT])
        a_hot = sb("a_hot", [P, Q, NA])
        step_i = sb("step_i", [P, BLOCKS], I32)
        stepf = sb("stepf", [P, BLOCKS])
        pad_i = sb("pad_i", [1, 2, EP - E], I32)
        onehot = sb("onehot", [P, 2, 2, P])
        dist = sb("dist", [P, 2, P])
        wlr = sb("wlr", [P, KC, 2 * H])
        blr = sb("blr", [P, 2 * H])
        stat = sb("stat", [P, TILES, 6])
        ln = sb("ln", [P, 4, TILES])
        mv = sb("mv", [P, 2, 2])
        std = sb("std", [P, 2])
        rstd = sb("rstd", [P, 2])
        nmr = sb("nmr", [P, 2])
        epsc = sb("epsc", [P, 1])
        twoc = sb("twoc", [P, 1])
        eler = sb("eler", [P, TILES, 2 * H])
        src_flat = sb("src_flat", [P, J], I32)
        src_step = sb("src_step", [P, SP, 2], I32)
        ndrel = sb("ndrel", [P, SP, 2])
        slot_i = sb("slot_i", [1, 8 + BLOCKS * P], I32)
        hist = sb("hist", [P, TILES])
        dinv = sb("dinv", [P, TILES])
        small = sb("small", [P, 8, TILES])
        er_idx = sb("er_idx", [P, TILES], I32)
        el_idx = sb("el_idx", [P, 2, EB], I32)
        el_rows = sb("el_rows", [P, 2, EB * H])
        sc_rows = sb("sc_rows", [P, SB, H])
        sc_idx = sb("sc_idx", [P, SB], I32)
        row_idx = sb("row_idx", [P, 2, U, 2], I32)
        edgecols_i = sb("edgecols_i", [P, 2], I32)
        edgecols = sb("edgecols", [P, 2])
        stepcols = sb("stepcols", [P, 8, BLOCKS])
        gidx = sb("gidx", [P, BLOCKS], I32)
        tail_st = sb("tail_st", [P, 2, H])
        carry = sb("carry", [P, H])
        carry_row = sb("carry_row", [H, 3, P + 1])
        rden = sb("rden", [P, TILES, H])

        el = edge[:, 0:J * H].rearrange("p (j h) -> p j h", h=H)
        top = edge[:, J * H:2 * J * H].rearrange("p (j h) -> p j h", h=H)
        w_step = edge[:, 0:SP * 2 * H].rearrange("p (w q) -> p w q", q=2 * H)
        w_rows = edge[:, SP * 2 * H:SP * 2 * H + 2 * GE * H].rearrange("p (b n) -> p b n", b=2)
        W_src_sb = edge[:, 0:2048].rearrange("p (k n) -> p k n", k=KC)
        W_dst_sb = edge[:, 2048:4096].rearrange("p (k n) -> p k n", k=KC)
        fold = edge[:, 4096:8192].rearrange("p (s k n) -> p s k n", s=2, k=KC)
        attn_sb = edge[:, 8192:9216].rearrange("p (s n) -> p s n", s=2)
        bsd_sb = edge[:, 9216:10240].rearrange("p (s n) -> p s n", s=2)
        bfold = edge[:, 10240:11264].rearrange("p (s n) -> p s n", s=2)

        at = [0]

        def in_big(n):
            at[0] += n
            return big[:, at[0] - n:at[0]]
        er = in_big(J * H).rearrange("p (j h) -> p j h", h=H)
        dst_i = in_big(J).bitcast(I32)
        dst_f = in_big(J)
        blk_i = in_big(J).bitcast(I32)
        blk_f = in_big(J)
        low_i = in_big(J).bitcast(I32)
        low_f = in_big(J)
        cont = in_big(J + 1)
        pen = in_big(J + 1)
        scan = in_big(J)
        hot_low = in_big(JB * P).bitcast(BF16).rearrange("p (b j n) -> p b j n", b=2, j=JB)
        hot_blk = in_big(JB * TILES + 1)[:, 0:JB * TILES].bitcast(BF16).rearrange("p (b j n) -> p b j n", b=2, j=JB)
        g_i = in_big(2 * GROUPS).bitcast(I32).rearrange("p (s g) -> p s g", s=2)
        g_t = in_big(2 * GROUPS).rearrange("p (s g) -> p s g", s=2)
        g_c = in_big(2 * GROUPS).rearrange("p (s g) -> p s g", s=2)
        g_b = in_big(2 * GROUPS).rearrange("p (s g) -> p s g", s=2)
        g_m = in_big(3 * GROUPS).rearrange("p (s g) -> p s g", s=3)
        b_i = in_big(BLOCKS * 2 * GE).bitcast(I32).rearrange("p (b s e) -> p b s e", b=BLOCKS, s=2)
        b_f = in_big(2 * 2 * GE).rearrange("p (b s e) -> p b s e", b=2, s=2)
        el_parts = in_big(3 * NA * KT * H // 2).bitcast(BF16).rearrange("p (s t h) -> p s t h", s=3, h=H)
        el_rest = g_c.rearrange("p s g -> p (s g)")[:, 0:TILES * H].rearrange("p (t h) -> p t h", h=H)
        low_T = g_b.rearrange("p s g -> p (s g)")[:, 0:2 * P].bitcast(F16).rearrange("p (b n) -> p b n", n=P)
        hot2 = hot_low.rearrange("p b j n -> p (b j n)")
        src_hot = hot2[:, 0:2 * KT * Q * P].rearrange("p (b k n) -> p b k n", b=2, k=KT)
        picked = hot2[:, 2 * KT * Q * P:2 * KT * Q * P + 2 * Q * NA * H].bitcast(F32).rearrange(
            "p (q a h) -> p q a h", q=Q, h=H)
        low_all = hot_blk.rearrange("p b j n -> p (b j n)")[:, 0:4 * Q * P].bitcast(F16).rearrange("p (b n) -> p b n", b=4)
        assert at[0] <= TILES * AW

        def acc(t):
            return big[:, ds(t * AW, D)]

        def first(t):
            return big[:, ds(t * D, D)]

        mm = [ps("mm0", [P, D]), ps("mm1", [P, D])]
        tr = [ps("tr0", [P, D]), ps("tr1", [P, D])]
        sm = [ps("sm0", [P, D]), ps("sm1", [P, D])]
        hist_ps = ps("hist_ps", [P, D])
        misc = ps("misc", [P, D])
        sum_ps, den_ps = mm + tr, sm + [hist_ps, misc]

        pad_set, const_set, ident_set, edges_kept, fold_in, edges_in, firsts_in = map(sem, (
            "pad_set", "const_set", "ident_set", "edges_kept", "fold_in", "edges_in", "firsts_in"))
        dve_setup, folded = sem("dve_setup"), sem("folded")
        x_in = [sem(f"x_in{c}") for c in range(TILES // XL + 1)]
        stat_set, ln_set, std_set, h_set, h_turned, hT_set, hT_kept, eler_sum, eler_set = map(sem, (
            "stat_set", "ln_set", "std_set", "h_set", "h_turned", "hT_set", "hT_kept", "eler_sum", "eler_set"))
        el_kept, er_zeroed, wval_in, hT_copied, v_sum, v_set = map(sem, (
            "el_kept", "er_zeroed", "wval_in", "hT_copied", "v_sum", "v_set"))
        v_kept = [sem("v_kept0"), sem("v_kept1")]
        el_in = [sem("el_in0"), sem("el_in1")]
        er_scattered, er_in, srcdst_in, w_kept, el_idx_set, sc_idx_set = map(sem, (
            "er_scattered", "er_in", "srcdst_in", "w_kept", "el_idx_set", "sc_idx_set"))
        el_placed = sem("el_placed")
        w_in = [sem(f"w_in{k}") for k in range(BLOCKS)]
        dve_prep, pe_prep, hot_set, hot_used, std_deg, gidx_set, er_idx_set, w_exp, lin_set = map(sem, (
            "dve_prep", "pe_prep", "hot_set", "hot_used", "std_deg", "gidx_set", "er_idx_set", "w_exp", "lin_set"))
        w_turned, w_placed = sem("w_turned"), sem("w_placed")
        low_kept, src_hot_set, el_summed, el_chain, el_picked = map(sem, (
            "low_kept", "src_hot_set", "el_summed", "el_chain", "el_picked"))
        low_in = [sem(f"low_in{b}") for b in range(4)]
        agg = []
        for n in ("gat", "gcn1", "gcn2"):
            agg.append(dict(
                rows_in=[sem(f"{n}_rows_in{u}") for u in range(U)],
                idx_set=sem(f"{n}_idx_set"), dist_set=sem(f"{n}_dist_set"), onehot_set=sem(f"{n}_onehot_set"), msg_set=sem(f"{n}_msg_set"),
                step_sum=sem(f"{n}_step_sum"), acc_added=sem(f"{n}_acc_added")))
        rden_set, xr_scaled, x1_set, x1_stat, x1_var, x1_std, x1_rstd, x1_nmr = map(sem, (
            "rden_set", "xr_scaled", "x1_set", "x1_stat", "x1_var", "x1_std", "x1_rstd", "x1_nmr"))
        xr_in = [sem("xr_in0"), sem("xr_in1")]
        x1_kept = [sem("x1_kept0"), sem("x1_kept1")]
        mids = []
        for n in ("gcn1", "gcn2"):
            mids.append(dict(
                w_in=sem(f"{n}_w_in"), y_set=sem(f"{n}_y_set"), h_set=sem(f"{n}_h_set"), turned=sem(f"{n}_turned"),
                hT_set=sem(f"{n}_hT_set"), summed=sem(f"{n}_summed"), tab_set=sem(f"{n}_tab_set"),
                seeded=sem(f"{n}_seeded"), kept=[sem(f"{n}_kept0"), sem(f"{n}_kept1")]))
        b_in = [sem("b1_in"), sem("b2_in")]
        y_set, out_set = sem("y_set"), sem("out_set")
        x1_in = [sem(f"x1_in{n}") for n in range(OS)]
        out_kept = [sem(f"out_kept{n}") for n in range(OS)]

        def slot_total(t, par, per=16):
            return (t - par) * (per // 2) + per

        def all_kept(eng, pair, per=16):
            eng.wait_ge(pair[0], per * ((TILES + 1) // 2))
            eng.wait_ge(pair[1], per * (TILES // 2))

        waits_passed = {eng: sem(f"waits_passed_{eng}") for eng in ("pool", "dve")}

        def wait_alone(name, eng, which, value):
            eng.wait_ge(which, value)
            eng.sem_inc(waits_passed[name], 1)

        def on_all(vec):
            return vec.rearrange("(a n) -> a n", a=1).broadcast_to([P, D])

        block = ctx.enter_context(nc.Block())

        prep = [0]
        marks = {}

        @block.vector
        def _(dve):
            def did(ins):
                prep[0] += 1
                ins.then_inc(dve_prep, 1)
                dve.wait_ge(dve_prep, prep[0])

            dve.wait_ge(fold_in, 96)
            n = 0
            for s, w in enumerate((W_src_sb, W_dst_sb)):
                dve.tensor_tensor(fold[:, s, :, :], w, attn_sb[:, s, :].unsqueeze(1).to_broadcast([P, KC, D]),
                                  ALU.mult).then_inc(dve_setup, 1)
                dve.tensor_tensor(bfold[:, s, :], bsd_sb[:, s, :], attn_sb[:, s, :], ALU.mult).then_inc(dve_setup, 1)
                n += 2
                dve.wait_ge(dve_setup, n)
                for k in range(KC):
                    dve.tensor_reduce(wlr[:, k, s * H:(s + 1) * H], fold[:, s, k, :].rearrange("p (h f) -> p h f", f=F),
                                      AX.X, ALU.add).then_inc(folded, 1)
                dve.tensor_reduce(blr[:, s * H:(s + 1) * H], bfold[:, s, :].rearrange("p (h f) -> p h f", f=F),
                                  AX.X, ALU.add).then_inc(folded, 1)
            dve.wait_ge(folded, 10)

            for c in range(TILES // XL):
                dve.wait_ge(x_in[c], 16)
                with dve.Fori(0, 2) as i:
                    for n in range(XL // 2):
                        t = i * (XL // 2) + (c * XL + n)
                        dve.bn_stats(stat[:, t, :], first(t)).then_inc(stat_set, 1)
            dve.wait_ge(x_in[TILES // XL], 16)
            dve.bn_stats(stat[:, TILES - 1, :], first(TILES - 1)).then_inc(stat_set, 1)
            dve.wait_ge(stat_set, TILES)
            dve.tensor_tensor(ln[:, 0, :], stat[:, :, 1], stat[:, :, 4], ALU.add).then_inc(ln_set, 1)
            dve.tensor_tensor(ln[:, 1, :], stat[:, :, 1], stat[:, :, 4], ALU.subtract).then_inc(ln_set, 1)
            dve.tensor_tensor(ln[:, 2, :], stat[:, :, 2], stat[:, :, 5], ALU.add).then_inc(ln_set, 1)
            dve.wait_ge(ln_set, 3)
            dve.tensor_tensor(ln[:, 3, :], ln[:, 1, :], ln[:, 1, :], ALU.mult).then_inc(ln_set, 1)
            dve.tensor_scalar(ln[:, 0, :], ln[:, 0, :], 0.5, None, ALU.mult).then_inc(ln_set, 1)
            dve.tensor_scalar(ln[:, 2, :], ln[:, 2, :], 1.0 / D, None, ALU.mult).then_inc(ln_set, 1)
            dve.wait_ge(ln_set, 6)
            dve.scalar_tensor_tensor(ln[:, 1, :], ln[:, 3, :], 0.25, ln[:, 2, :], ALU.mult, ALU.add).then_inc(ln_set, 1)
            dve.wait_ge(std_set, 1)
            dve.reciprocal(ln[:, 2, :], ln[:, 3, :]).then_inc(ln_set, 1)
            dve.wait_ge(ln_set, 8)
            dve.scalar_tensor_tensor(ln[:, 1, :], ln[:, 0, :], -1.0, ln[:, 2, :], ALU.mult, ALU.mult).then_inc(ln_set, 1)

            def first_layer(s):
                if s.live():
                    t, par = s.k, s.j
                    dve.wait_ge(h_turned, t + 1)
                    if s.past(2):
                        dve.wait_ge(eler_sum, t - 1)
                        dve.wait_ge(hT_kept, t - 1)
                    dve.tensor_copy(rows[:, 4 + par, :], tr[par][:, :]).then_inc(hT_set, 1)
                if s.live(1):
                    t, par = s.k - 1, (s.j - 1) % 2
                    dve.wait_ge(eler_sum, t + 1)
                    dve.tensor_tensor(eler[:, t, :], sm[par][:, 0:2 * H], blr[:, :], ALU.add).then_inc(eler_set, 1)
            pipelined(dve, TILES, 2, 1, first_layer)

            dve.wait_ge(wval_in, 32)

            def make_v(s):
                t, par = s.k, s.j
                dve.wait_ge(v_sum, t + 1)
                if s.past(2):
                    dve.wait_ge(v_kept[par], slot_total(t - 2, par))
                dve.tensor_tensor(rows[:, par, :], mm[par][:, :], bias[:, :], ALU.add).then_inc(v_set, 1)
            pipelined(dve, TILES, 2, 0, make_v)

            did(dve.memset(er.rearrange("p j h -> p (j h)"), 0.0))
            dve.memset(edgecols_i[:, :], -1).then_inc(lin_set, 1)
            did(dve.tensor_copy(iota[:, :], iota_i[:, :]))
            did(dve.tensor_copy(stepf[:, :], step_i[:, :]))
            did(dve.tensor_copy(low_id[:, :], low_i4[:, :]))

            dve.wait_ge(firsts_in, 80)
            did(dve.tensor_scalar(g_i[0:1, :, :], g_i[0:1, :, :], 7, None, ALU.arith_shift_right))
            did(dve.tensor_copy(g_t[0:1, :, :], g_i[0:1, :, :]))
            did(dve.tensor_tensor(g_c[0:1, 0, :], g_t[0:1, 1, :], g_t[0:1, 0, :], ALU.subtract))
            did(dve.tensor_scalar(g_c[0:1, 0, :], g_c[0:1, 0, :], 1.0, None, ALU.add))
            did(dve.memset(g_m[0:1, 0, :], 1.0))
            did(dve.tensor_tensor_scan(g_c[0:1, 1, :], g_m[0:1, 0, :], g_c[0:1, 0, :], 0.0, ALU.mult, ALU.add))
            did(dve.tensor_tensor(g_t[0:1, 1, :], g_c[0:1, 1, :], g_c[0:1, 0, :], ALU.subtract))
            marks["groups"] = prep[0]
            dve.wait_ge(pe_prep, 1)
            did(dve.tensor_copy(g_b[:, 0, :], misc[:, 0:GROUPS]))
            dve.wait_ge(pe_prep, 2)
            did(dve.tensor_copy(g_b[:, 1, :], sm[0][:, 0:GROUPS]))
            for b in range(BLOCKS):
                did(dve.tensor_scalar(g_m[:, 0, :], g_b[:, 1, :], stepf[:, b:b + 1], None, ALU.is_le))
                did(dve.tensor_tensor(g_m[:, 1:3, :], g_b[:, :, :], g_m[:, 0:1, :].to_broadcast([P, 2, GROUPS]), ALU.mult))
                did(dve.tensor_reduce(stepcols[:, 0, b:b + 1], g_m[:, 0, :], AX.X, ALU.add))
                did(dve.tensor_reduce(stepcols[:, 1, b:b + 1], g_m[:, 1, :], AX.X, ALU.max))
                did(dve.tensor_reduce(stepcols[:, 2, b:b + 1], g_m[:, 2, :], AX.X, ALU.max))
            did(dve.tensor_tensor(stepcols[:, 3, :], stepcols[:, 1, :], stepcols[:, 2, :], ALU.subtract))
            did(dve.tensor_tensor(stepcols[:, 4, :], stepcols[:, 3, :], stepf[:, :], ALU.add))
            did(dve.tensor_scalar(stepcols[:, 5, :], stepcols[:, 4, :], float(P), None, ALU.mult))
            did(dve.tensor_scalar(stepcols[:, 6, :], stepcols[:, 4, :], float(TILES - 1), float(AW), ALU.min, ALU.mult))
            marks["slots"] = prep[0]
            dve.tensor_scalar(gidx[:, :], stepcols[:, 0, :], -1.0, None, ALU.add).then_inc(gidx_set, 1)
            dve.wait_ge(pe_prep, 3)
            did(dve.memset(slot_i[0:1, 0:LAG], 0))
            did(dve.tensor_copy(slot_i[0:1, LAG:LAG + BLOCKS * P], misc[0:1, 0:BLOCKS * P]))

            did(dve.tensor_scalar(blk_i, dst_i, 7, None, ALU.arith_shift_right))
            did(dve.tensor_scalar(low_i, dst_i, P - 1, None, ALU.bitwise_and))
            did(dve.tensor_copy(blk_f, blk_i))
            did(dve.tensor_copy(low_f, low_i))

            def hot(s):
                b, par = s.k, s.j
                if s.past(2):
                    dve.wait_ge(hot_used, b - 1)
                dve.tensor_tensor(hot_low[:, par, :, :], low_f[:, ds(b * JB, JB)].unsqueeze(2).to_broadcast([P, JB, P]),
                                  iota[:, :].unsqueeze(1).to_broadcast([P, JB, P]), ALU.is_equal).then_inc(hot_set, 1)
                dve.tensor_tensor(hot_blk[:, par, :, :], blk_f[:, ds(b * JB, JB)].unsqueeze(2).to_broadcast([P, JB, TILES]),
                                  iota[:, 0:TILES].unsqueeze(1).to_broadcast([P, JB, TILES]), ALU.is_equal).then_inc(hot_set, 1)
            pipelined(dve, HB, 2, 0, hot, tail=2)
            dve.wait_ge(hot_used, HB)
            did(dve.tensor_copy(hist[:, :], hist_ps[:, 0:TILES]))
            marks["hist"] = prep[0]
            did(dve.tensor_copy(small[:, 0, :], node_i[:, :]))
            dve.wait_ge(pe_prep, 5)
            did(dve.tensor_copy(small[:, 1, :], misc[:, 0:TILES]))
            did(dve.tensor_tensor_scan(small[:, 2, :], ones[:, 0:TILES], small[:, 1, :], 0.0, ALU.mult, ALU.add))
            did(dve.tensor_tensor(small[:, 3, :], small[:, 2, :], small[:, 1, :], ALU.subtract))
            did(dve.tensor_tensor(small[:, 4, :], small[:, 3, :], sm[0][:, 0:TILES], ALU.add))
            did(dve.tensor_tensor(small[:, 3, :], small[:, 4, :], small[:, 0, :], ALU.subtract))
            did(dve.scalar_tensor_tensor(small[:, 5, :], hist[:, :], 0.0, small[:, 3, :], ALU.is_gt, ALU.mult))
            dve.tensor_tensor(er_idx[:, :], small[:, 5, :], small[:, 0, :], ALU.add).then_inc(er_idx_set, 1)
            dve.wait_ge(std_deg, 1)
            did(dve.reciprocal(dinv[:, :], small[:, 6, :]))

            did(dve.tensor_scalar(low_i[:, 0:PCOLS], src_flat[:, J0:J], KT * P - 1, None, ALU.bitwise_and))
            did(dve.tensor_scalar(blk_i[:, 0:PCOLS], src_flat[:, J0:J], 9, None, ALU.arith_shift_right))
            did(dve.tensor_copy(low_f[:, 0:PCOLS], low_i[:, 0:PCOLS]))
            did(dve.tensor_copy(blk_f[:, 0:PCOLS], blk_i[:, 0:PCOLS]))
            marks["low"] = prep[0]
            did(dve.memset(el_parts[:, :, TILES:, :], 0.0))
            did(dve.tensor_copy(el_parts[:, 0, 0:TILES, :], eler[:, :, 0:H]))
            did(dve.tensor_tensor(el_rest, eler[:, :, 0:H], el_parts[:, 0, 0:TILES, :], ALU.subtract))
            did(dve.tensor_copy(el_parts[:, 1, 0:TILES, :], el_rest))
            did(dve.tensor_tensor(el_rest, el_rest, el_parts[:, 1, 0:TILES, :], ALU.subtract))
            did(dve.tensor_copy(el_parts[:, 2, 0:TILES, :], el_rest))
            marks["parts"] = prep[0]
            dve.wait_ge(pe_prep, 6)
            full, left = divmod(PCOLS, P)
            did(dve.tensor_copy(low_T[:, 0:full, :], misc[:, 0:full * P].rearrange("p (b n) -> p b n", n=P)))
            did(dve.tensor_copy(low_T[0:left, full, :], misc[0:left, full * P:(full + 1) * P]))
            marks["low_T"] = prep[0]

            dve.wait_ge(srcdst_in, 16 * 2 * BLOCKS)
            turned = 6
            for b in range(BLOCKS):
                n_w = min(P, SP - b * P)
                did(dve.tensor_copy(b_f[:, b % 2, 0, :], b_i[:, b, 0, :]))
                did(dve.tensor_scalar(b_f[:, b % 2, 1, :], b_i[:, b, 1, :], stepcols[:, 5, b:b + 1], -1.0,
                                      ALU.subtract, ALU.mult))
                marks[f"block{b}"] = prep[0]
                turned += 1
                dve.wait_ge(pe_prep, turned)
                got = tr[b % 2][:, :].rearrange("p (s c w) -> p s w c", s=2, c=2)
                did(dve.tensor_copy(src_step[:, b * P:b * P + n_w, :], got[:, 0, 0:n_w, :]))
                did(dve.tensor_copy(ndrel[:, b * P:b * P + n_w, :], got[:, 1, 0:n_w, :]))
                marks[f"unblock{b}"] = prep[0]
            marks["tables"] = prep[0]

            did(dve.tensor_copy(dst_f, dst_i))
            did(dve.tensor_copy(edgecols[:, :], edgecols_i[:, :]))
            did(dve.tensor_tensor(cont[:, 1:J], dst_f[:, 1:J], dst_f[:, 0:J - 1], ALU.is_equal))
            did(dve.tensor_tensor(cont[:, 0:1], dst_f[:, 0:1], edgecols[:, 0:1], ALU.is_equal))
            did(dve.tensor_tensor(cont[:, J:J + 1], dst_f[:, J - 1:J], edgecols[:, 1:2], ALU.is_equal))
            did(dve.tensor_scalar(pen, cont, -1.0, BIG, ALU.add, ALU.mult))

            def pick(s):
                if s.live():
                    g, par = s.k, s.j % 2
                    dve.wait_ge(low_in[s.j], (g - s.j) * 4 + 16)
                    if s.past(2):
                        dve.wait_ge(el_summed, g - 1)
                    for kt in range(KT):
                        dve.tensor_scalar(src_hot[:, par, kt, :], low_all[:, s.j, :], low_id[:, kt:kt + 1], None,
                                          ALU.is_equal).then_inc(src_hot_set, 1)
                if s.live(1):
                    g, par = s.k - 1, (s.j - 1) % 2
                    dve.tensor_tensor(a_hot[:, :, :], blk_f[:, ds(g * Q, Q)].unsqueeze(2).to_broadcast([P, Q, NA]),
                                      iota[:, 0:NA].unsqueeze(1).to_broadcast([P, Q, NA]), ALU.is_equal).then_inc(el_chain, 1)
                    dve.wait_ge(el_chain, 2 * g + 1)
                    dve.wait_ge(el_summed, g + 1)
                    dve.tensor_tensor(picked[:, :, :, :],
                                      mm[par][:, 0:Q * NA * H].rearrange("p (q a h) -> p q a h", q=Q, h=H),
                                      a_hot[:, :, :].unsqueeze(3).to_broadcast([P, Q, NA, H]), ALU.mult).then_inc(el_chain, 1)
                    dve.wait_ge(el_chain, 2 * g + 2)
                    dve.tensor_reduce(edge[:, ds(g * (Q * H) + J0 * H, Q * H)].rearrange("p (q h) -> p q h", h=H),
                                      picked[:, :, :, :].rearrange("p q a h -> p q h a"), AX.X, ALU.add).then_inc(el_picked, 1)
            pipelined(dve, PCOLS // Q, 4, 1, pick)
            dve.wait_ge(el_picked, PCOLS // Q)

            turns = [turned]

            def carries(local, is_max, back):
                flags = cont[:, 1:J + 1] if back else cont[:, 0:J]
                for h in range(H):
                    local(h)
                did(dve.tensor_reduce(carry[:, 0:1], flags, AX.X, ALU.min))
                if is_max:
                    did(dve.tensor_scalar(carry[:, 0:1], carry[:, 0:1], -1.0, BIG, ALU.add, ALU.mult))
                did(dve.tensor_copy(tail_st[:, 1, :], carry[:, 0:1].to_broadcast([P, H])))
                marks.setdefault("ends", []).append(prep[0])
                turns[0] += 1
                dve.wait_ge(pe_prep, turns[0])
                did(dve.tensor_copy(carry_row[:, 0:2, 0:P], misc[0:H, 0:2 * P].rearrange("p (s n) -> p s n", s=2)))
                start = -BIG if is_max else 0.0
                edge_col = P if back else 0
                did(dve.memset(carry_row[:, 2, edge_col:edge_col + 1], start))
                ops = (ALU.add, ALU.max) if is_max else (ALU.mult, ALU.add)
                if back:
                    did(dve.tensor_tensor_scan(carry_row[:, 2, 0:P][:, ::-1], carry_row[:, 1, 0:P][:, ::-1],
                                               carry_row[:, 0, 0:P][:, ::-1], start, *ops))
                else:
                    did(dve.tensor_tensor_scan(carry_row[:, 2, 1:P + 1], carry_row[:, 1, 0:P],
                                               carry_row[:, 0, 0:P], start, *ops))
                marks.setdefault("carried", []).append(prep[0])
                turns[0] += 1
                dve.wait_ge(pe_prep, turns[0])
                did(dve.tensor_copy(carry[:, :], sm[1][:, 0:H]))

            dve.wait_ge(er_in, 16)

            def er_local(h):
                did(dve.tensor_tensor_scan(scan[:, :], cont[:, 0:J], er[:, :, h], 0.0, ALU.mult, ALU.add))
                did(dve.tensor_copy(tail_st[:, 0, h:h + 1], scan[:, J - 1:J]))
            carries(er_local, False, False)
            for h in range(H):
                did(dve.tensor_tensor_scan(scan[:, :], cont[:, 0:J], er[:, :, h], carry[:, h:h + 1], ALU.mult, ALU.add))
                did(dve.tensor_copy(er[:, :, h], scan[:, :]))

            dve.wait_ge(el_placed, EL_BATCHES)

            def top_local(h):
                did(dve.tensor_tensor_scan(scan[:, :], pen[:, 0:J], el[:, :, h], -BIG, ALU.add, ALU.max))
                did(dve.tensor_copy(tail_st[:, 0, h:h + 1], scan[:, J - 1:J]))
            carries(top_local, True, False)
            for h in range(H):
                did(dve.tensor_tensor_scan(top[:, :, h], pen[:, 0:J], el[:, :, h], carry[:, h:h + 1], ALU.add, ALU.max))
            did(dve.tensor_tensor(el, el, er, ALU.add))

            def back_local(h):
                did(dve.tensor_tensor_scan(scan[:, ::-1], pen[:, 1:J + 1][:, ::-1], top[:, ::-1, h], -BIG,
                                           ALU.add, ALU.max))
                did(dve.tensor_copy(tail_st[:, 0, h:h + 1], scan[:, 0:1]))
            carries(back_local, True, True)
            for h in range(H):
                did(dve.tensor_tensor_scan(scan[:, ::-1], pen[:, 1:J + 1][:, ::-1], top[:, ::-1, h],
                                           carry[:, h:h + 1], ALU.add, ALU.max))
                did(dve.tensor_tensor(top[:, :, h], scan[:, :], er[:, :, h], ALU.add))
            did(dve.scalar_tensor_tensor(el, el, SLOPE, el, ALU.mult, ALU.max))
            did(dve.scalar_tensor_tensor(top, top, SLOPE, top, ALU.mult, ALU.max))
            did(dve.tensor_tensor(el, el, top, ALU.subtract))
            marks["arg"] = prep[0]
            did(dve.memset(big[:, :], 0.0))
            dve.wait_ge(w_kept, 16)
            for b in range(BLOCKS):
                n_w = min(P, SP - b * P)
                for q in range(4):
                    i = 4 * b + q
                    dve.wait_ge(w_turned, i + 1)
                    dve.tensor_copy(w_step[:, b * P:b * P + n_w, 4 * q:4 * q + 4],
                                    tr[i % 2][:, :].rearrange("p (q w) -> p w q", q=4)[:, 0:n_w, :]).then_inc(w_placed, 1)
            dve.wait_ge(w_placed, 4 * BLOCKS)

            def aggregate(a, weighted):
                per = 2 if weighted else 1
                offs = [None]

                def step(s):
                    if weighted and s.live():
                        w, u = s.k, s.j % U
                        dve.wait_ge(a["rows_in"][u], (w - u) * 8 + 32)
                        view = rows[:, 2 * u:2 * u + 2, :].rearrange("p c (h f) -> p (c h) f", f=F)
                        dve.tensor_tensor(view, view, w_step[:, w, :].unsqueeze(2).to_broadcast([P, 2 * H, F]),
                                          ALU.mult).then_inc(a["msg_set"], 1)
                    if s.j % U == 0:
                        _, offs[0] = nc.values_load_multi_w_load_instructions(
                            slot_i[0:1, ds(s.k, U)], engines=(mybir.EngineType.DVE,), min_val=0,
                            max_val=(TILES - 1) * AW, skip_runtime_bounds_check_because="clamped when the table is made")
                    if s.live(LAG):
                        w, bank = s.k - LAG, (s.j - LAG) % U
                        dve.wait_ge(a["step_sum"], w + 1)
                        if s.past(1, LAG):
                            dve.wait_ge(a["acc_added"], per * w)
                        o = offs[0][s.j % U]
                        dve.tensor_tensor(big[:, ds(o, D)], big[:, ds(o, D)], sum_ps[bank][:, :], ALU.add).then_inc(a["acc_added"], 1)
                        if weighted:
                            den = big[:, ds(o + D, H)]
                            dve.tensor_tensor(den, den, den_ps[bank][:, 0:H], ALU.add).then_inc(a["acc_added"], 1)
                pipelined(dve, SP, 2 * U, LAG, step)
            aggregate(agg[0], True)

            def bank_out(m, s, lag):
                if s.live(lag):
                    t, par = s.k - lag, (s.j - lag) % 2
                    dve.wait_ge(m["turned"], t + 1)
                    if s.past(2, lag):
                        dve.wait_ge(m["summed"], t - 1)
                    dve.tensor_copy(rows[:, 4 + par, :], tr[par][:, :]).then_inc(m["hT_set"], 1)

            dve.wait_ge(agg[0]["acc_added"], 2 * SP)
            den = big[:, :].rearrange("p (t n) -> p t n", n=AW)[:, :, D:AW]
            dve.tensor_scalar(rden[:, :, :], den, 1e-16, None, ALU.max).then_inc(rden_set, 1)
            dve.wait_ge(rden_set, 1)
            dve.reciprocal(rden[:, :, :], rden[:, :, :]).then_inc(rden_set, 1)
            dve.wait_ge(rden_set, 2)

            def residual(s):
                if s.live():
                    t = s.k
                    a_t = acc(t).rearrange("p (h f) -> p h f", f=F)
                    dve.tensor_tensor(a_t, a_t, rden[:, t, :].unsqueeze(2).to_broadcast([P, H, F]),
                                      ALU.mult).then_inc(xr_scaled, 1)
                if s.live(2):
                    t, par = s.k - 2, s.j
                    dve.wait_ge(x1_set, t + 1)
                    dve.bn_stats(stat[:, par, :], acc(t)).then_inc(x1_stat, 1)
                    wait_alone("dve", dve, x1_stat, t + 1)
                    dve.bn_aggr(mv[:, par, :], stat[:, par, :]).then_inc(x1_var, 1)
                if s.live(3):
                    t, par = s.k - 3, (s.j - 1) % 2
                    dve.wait_ge(x1_std, t + 1)
                    if s.past(2, 3):
                        dve.wait_ge(mids[0]["h_set"], t - 1)
                    dve.reciprocal(small[:, 7, par:par + 1], std[:, par:par + 1]).then_inc(x1_rstd, 1)
                    dve.wait_ge(x1_rstd, 2 * t + 1)
                    dve.tensor_tensor(rstd[:, par:par + 1], small[:, 7, par:par + 1], dinv[:, ds(t, 1)],
                                      ALU.mult).then_inc(x1_rstd, 1)
                    dve.wait_ge(x1_rstd, 2 * t + 2)
                    dve.tensor_scalar(nmr[:, par:par + 1], mv[:, par, 0:1], rstd[:, par:par + 1], -1.0,
                                      ALU.mult, ALU.mult).then_inc(x1_nmr, 1)
                bank_out(mids[0], s, 4)
            pipelined(dve, TILES, 2, 4, residual)

            dve.wait_ge(mids[0]["seeded"], TILES)
            aggregate(agg[1], False)

            dve.wait_ge(b_in[0], 16)
            dve.wait_ge(agg[1]["acc_added"], SP)

            def between(s):
                if s.live():
                    t = s.k
                    dve.scalar_tensor_tensor(acc(t), acc(t), dinv[:, ds(t, 1)], bias[:, :],
                                             ALU.mult, ALU.add).then_inc(mids[1]["y_set"], 1)
                bank_out(mids[1], s, 2)
            pipelined(dve, TILES, 2, 2, between)

            dve.wait_ge(mids[1]["seeded"], TILES)
            aggregate(agg[2], False)

            dve.wait_ge(b_in[1], 16)
            dve.wait_ge(agg[2]["acc_added"], SP)

            def finish(s):
                if s.live():
                    t = s.k
                    dve.scalar_tensor_tensor(acc(t), acc(t), dinv[:, ds(t, 1)], bias[:, :],
                                             ALU.mult, ALU.add).then_inc(y_set, 1)
                if s.live(1):
                    t, slot = s.k - 1, (s.j - 1) % OS
                    dve.wait_ge(y_set, t + 1)
                    dve.wait_ge(x1_in[slot], (t - slot) * (16 // OS) + 16)
                    dve.scalar_tensor_tensor(rows[:, slot, :], acc(t), 0.0, rows[:, slot, :],
                                             ALU.max, ALU.add).then_inc(out_set, 1)
            pipelined(dve, TILES, OS, 1, finish)

        @block.sync
        def _(sp):
            sp.dma_start(src_rows.rearrange("g e -> (g e)")[0:E].rearrange("(a n) -> a n", a=16),
                         src.rearrange("(a n) -> a n", a=16)).then_inc(edges_kept, 16)
            sp.dma_start(dst_rows.rearrange("g e -> (g e)")[0:E].rearrange("(a n) -> a n", a=16),
                         dst.rearrange("(a n) -> a n", a=16)).then_inc(edges_kept, 16)
            sp.wait_ge(pad_set, 2)
            sp.dma_start(src_rows.rearrange("g e -> (g e)")[E:EP].rearrange("(a n) -> a n", a=1),
                         pad_i[:, 0, :]).then_inc(edges_kept, 16)
            sp.dma_start(dst_rows.rearrange("g e -> (g e)")[E:EP].rearrange("(a n) -> a n", a=1),
                         pad_i[:, 1, :]).then_inc(edges_kept, 16)
            sp.dma_start(W_src_sb, W_src.rearrange("(k p) n -> p k n", p=P)).then_inc(fold_in, 16)
            sp.dma_start(W_dst_sb, W_dst.rearrange("(k p) n -> p k n", p=P)).then_inc(fold_in, 16)
            sp.dma_start(attn_sb[:, 0, :], on_all(attn_l.rearrange("h f -> (h f)"))).then_inc(fold_in, 16)
            sp.dma_start(attn_sb[:, 1, :], on_all(attn_r.rearrange("h f -> (h f)"))).then_inc(fold_in, 16)
            sp.dma_start(bsd_sb[:, 0, :], on_all(b_src)).then_inc(fold_in, 16)
            sp.dma_start(bsd_sb[:, 1, :], on_all(b_dst)).then_inc(fold_in, 16)
            sp.dma_start(wmat[:, :, :], W_val.rearrange("(k p) n -> p k n", p=P)).then_inc(wval_in, 16)
            sp.dma_start(bias[:, :], on_all(b_val)).then_inc(wval_in, 16)

            sp.wait_ge(pad_set, 3)
            for c in range(TILES // XL):
                sp.dma_start(big[:, c * XL * D:(c + 1) * XL * D].rearrange("p (t d) -> p t d", d=D),
                             x[c * XL * P:(c + 1) * XL * P, :].rearrange("(t p) d -> p t d", p=P)).then_inc(x_in[c], 16)
            sp.dma_start(first(TILES - 1)[0:LAST, :], x[(TILES - 1) * P:N, :]).then_inc(x_in[TILES // XL], 16)
            sp.wait_ge(edges_kept, 64)
            sp.dma_start(src_flat[:, :], src_rows.rearrange("g e -> (g e)").rearrange("(p j) -> p j", j=J)).then_inc(edges_in, 16)
            sp.wait_ge(eler_set, TILES)
            sp.dma_start(el_tab.rearrange("(t p) h -> p t h", p=P), eler[:, :, 0:H]).then_inc(el_kept, 16)

            def keep_v(s):
                t, par = s.k, s.j
                sp.wait_ge(v_set, t + 1)
                sp.dma_start(v_tab[ds(t * P, P), :], rows[:, par, :]).then_inc(v_kept[par], 16)
            pipelined(sp, TILES, 2, 0, keep_v)

            sp.wait_ge(v_set, TILES)
            sp.dma_start(wmat[:, :, :], W1.rearrange("(k p) n -> p k n", p=P)).then_inc(mids[0]["w_in"], 16)
            sp.dma_start(bias[:, :], on_all(b1)).then_inc(b_in[0], 16)
            sp.wait_ge(lin_set, 1)
            dst_flat = dst_rows.rearrange("g e -> (g e)").rearrange("(p j) -> p j", j=J)
            sp.dma_start(dst_i, dst_flat).then_inc(firsts_in, 16)
            with nc.allow_non_contiguous_dma(reason="single dst at the borders of partitions and groups"):
                sp.dma_start(edgecols_i[1:P, 0:1], dst_flat[0:P - 1, J - 1:J]).then_inc(firsts_in, 16)
                sp.dma_start(edgecols_i[0:P - 1, 1:2], dst_flat[1:P, 0:1]).then_inc(firsts_in, 16)
                for s in range(2):
                    sp.dma_start(g_i[0:1, s, :],
                                 dst_rows[:, s * (GE - 1):s * (GE - 1) + 1].rearrange("g e -> e g")).then_inc(firsts_in, 16)
            sp.dma_start(er_tab[0:EP, :].rearrange("(p j) h -> p (j h)", j=J),
                         er.rearrange("p j h -> p (j h)")).then_inc(er_zeroed, 16)
            sp.wait_ge(dve_prep, marks["low_T"])
            full, left = divmod(PCOLS, P)
            sp.dma_start(low_tab[0:full * P, :].rearrange("(b r) n -> r b n", r=P), low_T[:, 0:full, :]).then_inc(low_kept, 16)
            sp.dma_start(low_tab[full * P:PCOLS, :], low_T[0:left, full, :]).then_inc(low_kept, 16)
            sp.wait_ge(low_kept, 32)

            def load_low(s):
                if s.past(4):
                    sp.wait_ge(src_hot_set, (s.k - 3) * KT)
                sp.dma_start(low_all[:, s.j, :], low_tab[ds(s.k * Q, Q), :].rearrange("q n -> (q n)").rearrange(
                    "(a n) -> a n", a=1).broadcast_to([P, Q * P])).then_inc(low_in[s.j], 16)
            pipelined(sp, PCOLS // Q, 4, 0, load_low)
            sp.wait_ge(er_scattered, 16 * TILES)
            sp.dma_start(er.rearrange("p j h -> p (j h)"),
                         er_tab[0:EP, :].rearrange("(p j) h -> p (j h)", j=J)).then_inc(er_in, 16)
            sp.wait_ge(w_exp, 1)
            sp.dma_start(w_tab.rearrange("g n -> (g n)").rearrange("(p n) -> p n", p=P),
                         edge[:, 0:J * H]).then_inc(w_kept, 16)

            sp.wait_ge(rden_set, 2)

            def keep_table(m, tab, s, lag):
                if s.live(lag):
                    t, par = s.k - lag, (s.j - lag) % 2
                    sp.wait_ge(m["tab_set"], t + 1)
                    sp.dma_start(tab[ds(t * P, P), :], rows[:, 6 + par, :]).then_inc(m["kept"][par], 16)

            def residual(s):
                t, par = s.k, s.j
                if s.live():
                    if s.past(2):
                        sp.wait_ge(x1_set, t - 1)
                    if s.inner or t < TILES - 1:
                        sp.dma_start(rows[:, par, :], x[ds(t * P, P), :]).then_inc(xr_in[par], 16)
                    else:
                        sp.dma_start(rows[0:LAST, par, :], x[t * P:N, :]).then_inc(xr_in[par], 16)
                if s.live(2):
                    t = s.k - 2
                    sp.wait_ge(x1_set, t + 1)
                    sp.dma_start(x1_tab[ds(t * P, P), :], acc(t)).then_inc(x1_kept[par], 16)
                keep_table(mids[0], h2_tab, s, 6)
            pipelined(sp, TILES, 2, 6, residual, tail=1)
            sp.wait_ge(mids[0]["summed"], TILES)
            sp.dma_start(wmat[:, :, :], W2.rearrange("(k p) n -> p k n", p=P)).then_inc(mids[1]["w_in"], 16)

            def between(s):
                keep_table(mids[1], h3_tab, s, 0)
            pipelined(sp, TILES, 2, 0, between)
            sp.wait_ge(mids[1]["y_set"], TILES)
            sp.dma_start(bias[:, :], on_all(b2)).then_inc(b_in[1], 16)

            sp.wait_ge(agg[2]["acc_added"], SP)

            def finish(s):
                if s.live():
                    t, slot = s.k, s.j
                    if s.past(OS):
                        sp.wait_ge(out_kept[slot], (t - slot) * (16 // OS))
                    sp.dma_start(rows[:, slot, :], x1_tab[ds(t * P, P), :]).then_inc(x1_in[slot], 16)
                if s.live(4):
                    t, slot = s.k - 4, (s.j - 4) % OS
                    sp.wait_ge(out_set, t + 1)
                    if s.inner or t < TILES - 1:
                        sp.dma_start(out[ds(t * P, P), :], rows[:, slot, :]).then_inc(out_kept[slot], 16)
                    else:
                        sp.dma_start(out[t * P:N, :], rows[0:LAST, slot, :]).then_inc(out_kept[slot], 16)
            pipelined(sp, TILES, OS, 4, finish, tail=1)
            for slot in range(OS):
                sp.wait_ge(out_kept[slot], 16 * len(range(slot, TILES, OS)))

        @block.gpsimd
        def _(pool):
            pool.memset(pad_i[:, 0, :], 0).then_inc(pad_set, 1)
            pool.memset(pad_i[:, 1, :], NP - 1).then_inc(pad_set, 1)
            pool.memset(first(TILES - 1), 0.0).then_inc(pad_set, 1)
            pool.memset(ident[:, :], 0.0).then_inc(const_set, 1)
            pool.memset(ones[:, :], 1.0).then_inc(const_set, 1)
            pool.memset(tri[:, :], 1.0).then_inc(const_set, 1)
            pool.memset(epsc[:, :], EPS).then_inc(const_set, 1)
            pool.memset(twoc[:, :], 2.0).then_inc(const_set, 1)
            pool.iota(iota_i[:, :], pattern=[[1, P]], base=0, channel_multiplier=0).then_inc(const_set, 1)
            pool.iota(node_i[:, :], pattern=[[P, TILES]], base=EP, channel_multiplier=1).then_inc(const_set, 1)
            pool.iota(low_i4[:, :], pattern=[[P, KT]], base=0, channel_multiplier=1).then_inc(const_set, 1)
            pool.iota(step_i[:, :], pattern=[[P, BLOCKS]], base=0, channel_multiplier=1).then_inc(const_set, 1)
            pool.wait_ge(const_set, 5)
            pool.affine_select(out=ident[:, :], in_=ident[:, :], compare_op=ALU.not_equal, fill=1.0, base=0,
                               pattern=[[-1, P]], channel_multiplier=1).then_inc(ident_set, 1)
            pool.affine_select(out=tri[:, :], in_=tri[:, :], compare_op=ALU.is_gt, fill=0.0, base=0,
                               pattern=[[1, P]], channel_multiplier=-1).then_inc(ident_set, 1)

            def keep_hT(s):
                t, par = s.k, s.j
                wait_alone("pool", pool, hT_set, t + 1)
                pool.tensor_copy(big[:, ds(t * D, D)], rows[:, 4 + par, :]).then_inc(hT_kept, 1)
            pipelined(pool, TILES, 2, 0, keep_hT)

            pool.wait_ge(el_kept, 16)
            pool.wait_ge(edges_in, 16)

            def batch(s):
                g, b = s.k, s.j
                if s.live():
                    pool.tensor_copy(el_idx[:, b, :], src_flat[:, ds(g * EB, EB)]).then_inc(el_idx_set, 1)
                    wait_alone("pool", pool, el_idx_set, g + 1)
                    for n in range(EB):
                        pool.indirect_dma_start(
                            el_rows[:, b, n * H:(n + 1) * H], None, el_tab,
                            bass.IndirectOffsetOnAxis(ap=el_idx[:, b, n:n + 1], axis=0)).then_inc(el_in[b], 16)
                if s.live(1):
                    g, b = s.k - 1, (s.j - 1) % 2
                    wait_alone("pool", pool, el_in[b], (g - b) * (8 * EB) + 16 * EB)
                    pool.tensor_copy(edge[:, ds(g * (EB * H), EB * H)], el_rows[:, b, :]).then_inc(el_placed, 1)
                    wait_alone("pool", pool, el_placed, g + 1)
            for k in range(2):
                batch(Step(k, k, EL_BATCHES, False))
            with pool.Fori(0, (EARLY - 2) // 2) as i:
                for j in range(2):
                    batch(Step(i * 2 + (2 + j), j, EL_BATCHES, True))
            pool.wait_ge(gidx_set, 1)
            for b in range(BLOCKS):
                for s, tab in enumerate((src_rows, dst_rows)):
                    pool.indirect_dma_start(b_i[:, b, s, :], None, tab,
                                            bass.IndirectOffsetOnAxis(ap=gidx[:, b:b + 1], axis=0)).then_inc(srcdst_in, 16)
            pool.wait_ge(er_idx_set, 1)
            pool.wait_ge(er_zeroed, 16)
            with pool.Fori(0, TILES // SB) as i:
                pool.tensor_copy(sc_idx[:, :], er_idx[:, ds(i * SB, SB)]).then_inc(sc_idx_set, 1)
                pool.tensor_copy(sc_rows[:, :, :], eler[:, ds(i * SB, SB), H:2 * H]).then_inc(sc_idx_set, 1)
                wait_alone("pool", pool, sc_idx_set, i * 2 + 2)
                for n in range(SB):
                    pool.indirect_dma_start(er_tab, bass.IndirectOffsetOnAxis(ap=sc_idx[:, n:n + 1], axis=0),
                                            sc_rows[:, n, :], None).then_inc(er_scattered, 16)
                wait_alone("pool", pool, er_scattered, (i + 1) * (16 * SB))
            with pool.Fori(0, (EL_BATCHES - EARLY) // 2) as i:
                for j in range(2):
                    batch(Step(i * 2 + (EARLY + j), j, EL_BATCHES, True))
            batch(Step(EL_BATCHES, 0, EL_BATCHES, False))
            pool.wait_ge(w_kept, 16)
            for b in range(BLOCKS):
                if b >= 2:
                    pool.wait_ge(w_turned, 4 * (b - 1))
                pool.indirect_dma_start(w_rows[:, b % 2, :], None, w_tab,
                                        bass.IndirectOffsetOnAxis(ap=gidx[:, b:b + 1], axis=0)).then_inc(w_in[b], 16)

            def gather(tab, a):
                def step(s):
                    w, u, b = s.k, s.j % U, s.j // U
                    if s.past(U):
                        wait_alone("pool", pool, a["step_sum"], w - U + 1)
                    if u == 0:
                        pool.tensor_copy(row_idx[:, b, :, :], src_step[:, ds(w, U), :]).then_inc(a["idx_set"], 1)
                        wait_alone("pool", pool, a["idx_set"], s.turn * 2 + (b + 1))
                    for c in range(2):
                        pool.indirect_dma_start(
                            rows[:, 2 * u + c, :], None, tab,
                            bass.IndirectOffsetOnAxis(ap=row_idx[:, b, u, c:c + 1], axis=0)).then_inc(a["rows_in"][u], 16)
                pipelined(pool, SP, 2 * U, 0, step)

            pool.wait_ge(dve_prep, marks["tables"])
            all_kept(pool, v_kept)
            gather(v_tab, agg[0])

            def seed(m, s, lag):
                if s.live(lag):
                    t, par = s.k - lag, (s.j - lag) % 2
                    wait_alone("pool", pool, m["tab_set"], t + 1)
                    pool.tensor_tensor(acc(t), rows[:, 6 + par, :], rows[:, 6 + par, :], ALU.add).then_inc(m["seeded"], 1)

            def residual(s):
                if s.live():
                    t, par = s.k, s.j
                    wait_alone("pool", pool, xr_scaled, t + 1)
                    wait_alone("pool", pool, xr_in[par], slot_total(t, par))
                    pool.tensor_tensor(acc(t), acc(t), rows[:, par, :], ALU.add).then_inc(x1_set, 1)
                if s.live(5):
                    t, par = s.k - 5, (s.j - 5) % 2
                    wait_alone("pool", pool, x1_kept[par], slot_total(t, par))
                seed(mids[0], s, 5)
            pipelined(pool, TILES, 2, 5, residual)
            all_kept(pool, mids[0]["kept"])
            all_kept(pool, x1_kept)
            gather(h2_tab, agg[1])

            def between(s):
                seed(mids[1], s, 3)
            pipelined(pool, TILES, 2, 3, between)
            all_kept(pool, mids[1]["kept"])
            gather(h3_tab, agg[2])

        @block.scalar
        def _(act):
            act.wait_ge(const_set, 9)

            act.wait_ge(ln_set, 7)
            act.activation(ln[:, 3, :], ln[:, 1, :], ACT.Sqrt, bias=epsc[:, 0:1]).then_inc(std_set, 1)
            act.wait_ge(ln_set, 9)

            def normalise(s):
                t, par = s.k, s.j
                if s.past(2):
                    act.wait_ge(h_turned, t - 1)
                act.activation(rows[:, 2 + par, :], first(t), ACT.Relu,
                               bias=ln[:, 1, ds(t, 1)], scale=ln[:, 2, ds(t, 1)]).then_inc(h_set, 1)
            pipelined(act, TILES, 2, 0, normalise)

            def fetch_hT(s):
                t, par = s.k, s.j
                act.wait_ge(hT_kept, t + 1)
                if s.past(2):
                    act.wait_ge(v_sum, t - 1)
                act.activation(rows[:, 6 + par, :], first(t), ACT.Copy).then_inc(hT_copied, 1)
            pipelined(act, TILES, 2, 0, fetch_hT)

            act.wait_ge(dve_prep, marks["hist"])
            act.activation(small[:, 6, :], hist[:, :], ACT.Sqrt, bias=twoc[:, 0:1]).then_inc(std_deg, 1)
            act.wait_ge(dve_prep, marks["arg"])
            act.activation(edge[:, 0:J * H], edge[:, 0:J * H], ACT.Exp).then_inc(w_exp, 1)

            def make_onehots(a):
                def step(s):
                    w = s.k
                    if s.past(1):
                        act.wait_ge(a["onehot_set"], w)
                    for c in range(2):
                        act.activation(dist[:, c, :], iota[:, :], ACT.Abs,
                                       bias=ndrel[:, w, c:c + 1]).then_inc(a["dist_set"], 1)
                    act.wait_ge(a["dist_set"], 2 * w + 2)
                    if s.past(2):
                        act.wait_ge(a["step_sum"], w - 1)
                    act.activation(onehot[:, s.j % 2, :, :], dist[:, :, :], ACT.Relu,
                                   bias=ones[:, 0:1], scale=-1.0).then_inc(a["onehot_set"], 1)
                pipelined(act, SP, U, 0, step)

            act.wait_ge(dve_prep, marks["tables"])
            make_onehots(agg[0])

            def table_out(m, s, lag):
                if s.live(lag):
                    t, par = s.k - lag, (s.j - lag) % 2
                    act.wait_ge(m["summed"], t + 1)
                    if s.past(2, lag):
                        act.wait_ge(m["seeded"], t - 1)
                        act.wait_ge(m["kept"][par], slot_total(t - 2, par))
                    act.activation(rows[:, 6 + par, :], mm[par][:, :], ACT.Copy).then_inc(m["tab_set"], 1)

            def residual(s):
                if s.live(2):
                    t, par = s.k - 2, s.j
                    act.wait_ge(x1_var, t + 1)
                    act.activation(std[:, par:par + 1], mv[:, par, 1:2], ACT.Sqrt, bias=epsc[:, 0:1]).then_inc(x1_std, 1)
                if s.live(3):
                    t, par = s.k - 3, (s.j - 3) % 2
                    act.wait_ge(x1_nmr, t + 1)
                    if s.past(2, 3):
                        act.wait_ge(mids[0]["turned"], t - 1)
                    act.activation(rows[:, 2 + par, :], acc(t), ACT.Relu,
                                   bias=nmr[:, par:par + 1], scale=rstd[:, par:par + 1]).then_inc(mids[0]["h_set"], 1)
                table_out(mids[0], s, 5)
            pipelined(act, TILES, 2, 5, residual)

            make_onehots(agg[1])

            def between(s):
                if s.live(1):
                    t, par = s.k - 1, (s.j - 1) % 2
                    act.wait_ge(mids[1]["y_set"], t + 1)
                    if s.past(2, 1):
                        act.wait_ge(mids[1]["turned"], t - 1)
                    act.activation(rows[:, 2 + par, :], acc(t), ACT.Relu,
                                   scale=dinv[:, ds(t, 1)]).then_inc(mids[1]["h_set"], 1)
                table_out(mids[1], s, 3)
            pipelined(act, TILES, 2, 3, between)
            make_onehots(agg[2])

        @block.tensor
        def _(pe):
            pe.wait_ge(ident_set, 2)
            pe.wait_ge(folded, 10)

            def turn(bank, slot, done):
                for k in range(KC):
                    last = nc.tensor.transpose(bank[:, k * P:(k + 1) * P], rows[:, slot, k * P:(k + 1) * P], ident[:, :])
                last.then_inc(done, 1)

            def product(bank, slot, rhs, done):
                for k in range(KC):
                    last = nc.tensor.matmul(bank, rows[:, slot, k * P:(k + 1) * P], rhs(k), start=(k == 0), stop=(k == KC - 1))
                last.then_inc(done, 1)

            def first_layer(s):
                if s.live():
                    t, par = s.k, s.j
                    pe.wait_ge(h_set, t + 1)
                    if s.past(2):
                        pe.wait_ge(hT_set, t - 1)
                    turn(tr[par], 2 + par, h_turned)
                if s.live(1):
                    t, par = s.k - 1, (s.j - 1) % 2
                    pe.wait_ge(hT_set, t + 1)
                    if s.past(2, 1):
                        pe.wait_ge(eler_set, t - 1)
                    product(sm[par][:, 0:2 * H], 4 + par, lambda k: wlr[:, k, :], eler_sum)
            pipelined(pe, TILES, 2, 1, first_layer)

            pe.wait_ge(wval_in, 32)

            def make_v(s):
                t, par = s.k, s.j
                pe.wait_ge(hT_copied, t + 1)
                if s.past(2):
                    pe.wait_ge(v_set, t - 1)
                product(mm[par][:, :], 6 + par, lambda k: wmat[:, k, :], v_sum)
            pipelined(pe, TILES, 2, 0, make_v)

            pe.wait_ge(dve_prep, marks["groups"])
            pe.matmul(misc[:, 0:GROUPS], ones[0:1, :], g_t[0:1, 0, :], start=True, stop=True).then_inc(pe_prep, 1)
            pe.matmul(sm[0][:, 0:GROUPS], ones[0:1, :], g_t[0:1, 1, :], start=True, stop=True).then_inc(pe_prep, 1)
            pe.wait_ge(dve_prep, marks["slots"])
            for b in range(BLOCKS):
                last = pe.matmul(misc[0:1, b * P:(b + 1) * P], stepcols[:, 6, b:b + 1], ident[:, :], start=True, stop=True)
            last.then_inc(pe_prep, 1)

            def count(s):
                b, par = s.k, s.j
                pe.wait_ge(hot_set, 2 * b + 2)
                for j in range(JB):
                    last = pe.matmul(hist_ps[:, 0:TILES], hot_low[:, par, j, :], hot_blk[:, par, j, :],
                                     start=(not s.inner and b == 0 and j == 0),
                                     stop=(not s.inner and b == HB - 1 and j == JB - 1))
                last.then_inc(hot_used, 1)
            pipelined(pe, HB, 2, 0, count, tail=2)
            pe.wait_ge(dve_prep, marks["hist"])
            pe.matmul(misc[:, 0:TILES], ones[:, :], hist[:, :], start=True, stop=True).then_inc(pe_prep, 1)
            pe.matmul(sm[0][:, 0:TILES], tri[:, :], hist[:, :], start=True, stop=True).then_inc(pe_prep, 1)

            pe.wait_ge(dve_prep, marks["low"])
            for b in range(-(-PCOLS // P)):
                n = min(P, PCOLS - b * P)
                last = pe.transpose(misc[0:n, b * P:(b + 1) * P], low_f[:, b * P:b * P + n], ident[:, :])
            last.then_inc(pe_prep, 1)

            for b in range(BLOCKS):
                pe.wait_ge(dve_prep, marks[f"block{b}"])
                for s in range(2):
                    for c in range(2):
                        last = pe.transpose(tr[b % 2][:, (2 * s + c) * P:(2 * s + c + 1) * P],
                                            b_f[:, b % 2, s, c * P:(c + 1) * P], ident[:, :])
                last.then_inc(pe_prep, 1)
            def pick(s):
                g, par = s.k, s.j
                pe.wait_ge(src_hot_set, (g + 1) * KT)
                if s.past(2):
                    pe.wait_ge(el_picked, g - 1)
                for q in range(Q):
                    for kt in range(KT):
                        for part in range(3):
                            last = pe.matmul(mm[par][:, q * NA * H:(q + 1) * NA * H], src_hot[:, par, kt, q * P:(q + 1) * P],
                                             el_parts[:, part, kt::KT, :], start=(kt == 0 and part == 0),
                                             stop=(kt == KT - 1 and part == 2))
                last.then_inc(el_summed, 1)
            pipelined(pe, PCOLS // Q, 2, 0, pick)

            for n in range(3):
                pe.wait_ge(dve_prep, marks["ends"][n])
                for i in range(2):
                    last = pe.transpose(misc[0:H, i * P:(i + 1) * P], tail_st[:, i, :], ident[:, :])
                last.then_inc(pe_prep, 1)
                pe.wait_ge(dve_prep, marks["carried"][n])
                lo = 1 if n == 2 else 0
                pe.transpose(sm[1][:, 0:H], carry_row[:, 2, lo:lo + P], ident[0:H, 0:H]).then_inc(pe_prep, 1)

            for b in range(BLOCKS):
                pe.wait_ge(w_in[b], 16)
                halves = w_rows[:, b % 2, :].rearrange("p (c e h) -> p c h e", c=2, h=H)
                for q in range(4):
                    i = 4 * b + q
                    if i >= 2:
                        pe.wait_ge(w_placed, i - 1)
                    for n in range(4):
                        c, h = divmod(4 * q + n, H)
                        last = pe.transpose(tr[i % 2][:, n * P:(n + 1) * P], halves[:, c, h, :], ident[:, :])
                    last.then_inc(w_turned, 1)

            def aggregate(a, weighted):
                def step(s):
                    w, u, par = s.k, s.j % U, s.j % 2
                    pe.wait_ge(a["onehot_set"], w + 1)
                    if weighted:
                        pe.wait_ge(a["msg_set"], w + 1)
                    else:
                        pe.wait_ge(a["rows_in"][u], (w - u) * 8 + 32)
                    if s.past(U):
                        pe.wait_ge(a["acc_added"], (2 if weighted else 1) * (w - U + 1))
                    for c in range(2):
                        if weighted:
                            pe.matmul(den_ps[u][:, 0:H], onehot[:, par, c, :], w_step[:, w, c * H:(c + 1) * H],
                                      start=(c == 0), stop=(c == 1))
                    for c in range(2):
                        last = pe.matmul(sum_ps[u][:, :], onehot[:, par, c, :], rows[:, 2 * u + c, :],
                                         start=(c == 0), stop=(c == 1))
                    last.then_inc(a["step_sum"], 1)
                pipelined(pe, SP, 2 * U, 0, step)

            pe.wait_ge(w_placed, 4 * BLOCKS)
            aggregate(agg[0], True)

            def dense_layer(m, lag):
                pe.wait_ge(m["w_in"], 16)

                def step(s):
                    if s.live(lag):
                        t, par = s.k - lag, (s.j - lag) % 2
                        pe.wait_ge(m["h_set"], t + 1)
                        if s.past(2, lag):
                            pe.wait_ge(m["hT_set"], t - 1)
                        turn(tr[par], 2 + par, m["turned"])
                    if s.live(lag + 1):
                        t, par = s.k - lag - 1, (s.j - lag - 1) % 2
                        pe.wait_ge(m["hT_set"], t + 1)
                        if s.past(2, lag + 1):
                            pe.wait_ge(m["tab_set"], t - 1)
                        product(mm[par][:, :], 4 + par, lambda k: wmat[:, k, :], m["summed"])
                pipelined(pe, TILES, 2, lag + 1, step)
            dense_layer(mids[0], 0)
            aggregate(agg[1], False)
            dense_layer(mids[1], 0)
            aggregate(agg[2], False)


_INS = ["x", "src", "dst", "L0_gnn_W_src", "L0_gnn_b_src", "L0_gnn_W_dst", "L0_gnn_b_dst", "L0_gnn_W_val", "L0_gnn_b_val",
        "L0_gnn_attn_l", "L0_gnn_attn_r", "L1_gnn_W1", "L1_gnn_b1", "L1_gnn_W2", "L1_gnn_b2"]


def kernel(**inputs):
    import concourse.bacc as bacc
    from concourse.bass_utils import run_bass_kernel_spmd as run

    nc = bacc.Bacc("TRN2", target_bir_lowering=False, num_devices=1)
    arrays, args = {}, []
    for name in _INS:
        a = np.ascontiguousarray(inputs[name])
        arrays[name] = a
        args.append(nc.dram_tensor(name, a.shape, mybir.dt.from_np(a.dtype), kind="ExternalInput").ap())
    out = nc.dram_tensor("out", [N, D], F32, kind="ExternalOutput").ap()
    build(nc, *args, out)
    return run(nc, [arrays], core_ids=[0]).results[0]["out"]
```

```python
import numpy as np
import concourse.bass as bass
from concourse import mybir
from contextlib import ExitStack

F32 = mybir.dt.float32
BF16 = mybir.dt.bfloat16
F16 = mybir.dt.float16
I32 = mybir.dt.int32
ALU = mybir.AluOpType
ACT = mybir.ActivationFunctionType
AX = mybir.AxisListType
ds = bass.ds

P = 128
N, E, D, H = 6250, 100000, 512, 8
F = D // H
KC = D // P
TILES = -(-N // P)
NP = TILES * P
LAST = N - (TILES - 1) * P
J = -(-E // P)
EP = J * P
SLOTS = 8
BANKS = 4
AW = D + H


class Cut:

    def __init__(self, chunks):
        self.chunks = chunks
        self.edges = chunks * P
        self.groups = EP // self.edges
        self.slots = SLOTS // chunks
        unroll = 2 * self.slots
        self.steps = -(-(self.groups + TILES - 1) // unroll) * unroll
        self.blocks = -(-self.steps // P)


GAT, GCN = Cut(2), Cut(1)
GE = GAT.edges
GROUPS = GAT.groups
SP = GAT.steps
XL = 8
OS = 8
LAG = 2
JB = 17
HB = J // JB
EB = 17
EL_BATCHES = 18
J0 = EL_BATCHES * EB
PCOLS = J - J0
Q = 4
KT = 4
NA = -(-TILES // KT)
EARLY = 4
SB = 7
BIG = 1e38
EPS = 1e-5
SLOPE = 0.2


class Step:

    def __init__(self, k, j, count, inner, turn=None):
        self.k, self.j, self.count, self.inner, self.turn = k, j, count, inner, turn

    def live(self, lag=0):
        return self.inner or 0 <= self.k - lag < self.count

    def past(self, n, lag=0):
        return self.inner or self.k - lag >= n


def pipelined(eng, count, unroll, lag, body, tail=0):
    lo = -(-(lag + unroll) // unroll) * unroll
    hi = lo + (count - tail - lo) // unroll * unroll
    for k in range(lo):
        body(Step(k, k % unroll, count, False, k // unroll))
    with eng.Fori(0, (hi - lo) // unroll) as i:
        for j in range(unroll):
            body(Step(i * unroll + (lo + j), j, count, True, i + lo // unroll))
    for k in range(hi, count + lag):
        body(Step(k, k % unroll, count, False, k // unroll))


def build(nc, x, src, dst, W_src, b_src, W_dst, b_dst, W_val, b_val, attn_l, attn_r, W1, b1, W2, b2, out):
    ctx = ExitStack()
    with ctx:
        def sb(name, shape, dt=F32):
            return ctx.enter_context(nc.sbuf_tensor(name, shape, dt))

        def ps(name, shape):
            return ctx.enter_context(nc.psum_tensor(name, shape, F32))

        def sem(name):
            return ctx.enter_context(nc.semaphore(name))

        def dram(name, shape, dt=F32):
            return nc.dram_tensor(name, shape, dt, kind="Internal").ap()

        src_rows = dram("src_rows", [GROUPS, GE], I32)
        dst_rows = dram("dst_rows", [GROUPS, GE], I32)
        el_tab = dram("el_tab", [NP, H])
        er_tab = dram("er_tab", [EP + NP, H])
        w_tab = dram("w_tab", [GROUPS, GE * H])
        low_tab = dram("low_tab", [PCOLS, P], F16)
        v_tab = dram("v_tab", [NP, D])
        x1_tab = dram("x1_tab", [NP, D])
        h2_tab = dram("h2_tab", [NP, D])
        h3_tab = dram("h3_tab", [NP, D])

        big = sb("big", [P, TILES * AW])
        edge = sb("edge", [P, 2 * J * H])
        rows = sb("rows", [P, SLOTS, D])
        wmat = sb("wmat", [P, KC, D])
        bias = sb("bias", [P, D])
        ident = sb("ident", [P, P])
        ones = sb("ones", [P, P])
        tri = sb("tri", [P, P])
        iota = sb("iota", [P, P])
        node_i = sb("node_i", [P, TILES], I32)
        low_i4 = sb("low_i4", [P, KT], I32)
        low_id = sb("low_id", [P, KT])
        a_hot = sb("a_hot", [P, Q, NA])
        step_i = sb("step_i", [P, GCN.blocks], I32)
        stepf = sb("stepf", [P, GCN.blocks])
        gidx = [sb(f"gidx{c.chunks}", [P, c.blocks], I32) for c in (GAT, GCN)]
        tile0 = [sb(f"tile0_{c.chunks}", [P, c.blocks]) for c in (GAT, GCN)]
        pad_i = sb("pad_i", [1, 2, EP - E], I32)
        wlr = sb("wlr", [P, KC, 2 * H])
        blr = sb("blr", [P, 2 * H])
        x1_stats = sb("x1_stats", [P, 2, 6])
        mv = sb("mv", [P, 2, 2])
        std = sb("std", [P, 2])
        rstd = sb("rstd", [P, 2])
        nmr = sb("nmr", [P, 2])
        epsc = sb("epsc", [P, 1])
        twoc = sb("twoc", [P, 1])
        eler_hots = sb("eler_hots", [P, TILES * 2 * H])
        src_flat = sb("src_flat", [P, J], I32)
        src_step = [sb(f"src_step{c.chunks}", [P, c.steps * c.chunks], I32) for c in (GAT, GCN)]
        ndrel = [sb(f"ndrel{c.chunks}", [P, c.steps * c.chunks]) for c in (GAT, GCN)]
        slot_i = [sb(f"slot_i{c.chunks}", [1, 8 + c.blocks * P], I32) for c in (GAT, GCN)]
        hist = sb("hist", [P, TILES])
        dinv = sb("dinv", [P, TILES])
        ind = sb("ind", [P, TILES])
        small = sb("small", [P, 8, TILES])
        er_idx = sb("er_idx", [P, TILES], I32)
        el_idx = sb("el_idx", [P, 2, EB], I32)
        el_rows = sb("el_rows", [P, 2, EB * H])
        sc_rows = sb("sc_rows", [P, SB, H])
        sc_idx = sb("sc_idx", [P, SB], I32)
        row_idx = sb("row_idx", [P, 2, SLOTS], I32)
        edgecols_i = sb("edgecols_i", [P, 2], I32)
        edgecols = sb("edgecols", [P, 2])
        stepcols = [sb(f"stepcols{c.chunks}", [P, 6, c.blocks]) for c in (GAT, GCN)]
        tail_st = sb("tail_st", [P, 2, H])
        carry = sb("carry", [P, H])

        el = edge[:, 0:J * H].rearrange("p (j h) -> p j h", h=H)
        top = edge[:, J * H:2 * J * H].rearrange("p (j h) -> p j h", h=H)
        w_step = edge[:, 0:SP * 2 * H].rearrange("p (w q) -> p w q", q=2 * H)
        w_rows = edge[:, SP * 2 * H:SP * 2 * H + 2 * GE * H].rearrange("p (b n) -> p b n", b=2)
        rden = edge[:, SP * 2 * H + 2 * GE * H:SP * 2 * H + 2 * GE * H + TILES * H].rearrange("p (t h) -> p t h", h=H)
        eler = eler_hots[:, :].rearrange("p (t q) -> p t q", q=2 * H)
        onehot = eler_hots[:, 0:4 * P].rearrange("p (b c n) -> p b c n", b=2, c=2)
        dist = eler_hots[:, 4 * P:6 * P].rearrange("p (c n) -> p c n", c=2)
        stat = big[:, TILES * D:TILES * (D + 6)].rearrange("p (t s) -> p t s", s=6)
        ln = small[:, 0:4, :]
        iota_i = small[:, 4:7, :].rearrange("p s t -> p (s t)")[:, 0:P].bitcast(I32)
        W_src_sb = wmat
        W_dst_sb = rows[:, 0:KC, :]
        attn_sb = rows[:, KC:KC + 2, :]
        bsd_sb = rows[:, KC + 2:KC + 4, :]

        class Region:

            def __init__(self, ap):
                self.ap, self.at = ap, 0

            def __call__(self, n):
                self.at += n
                assert self.at <= self.ap.shape[1]
                return self.ap[:, self.at - n:self.at]

        part = Region(edge[:, :])
        fold = part(KC * D).rearrange("p (k n) -> p k n", k=KC)
        bfold = part(2 * D).rearrange("p (s n) -> p s n", s=2)
        g_i = [[src_step[1][0:1, 0:GAT.groups], src_step[1][0:1, GAT.groups:2 * GAT.groups]],
               [src_step[0][0:1, 0:GCN.groups], ndrel[0][0:1, 0:GCN.groups].bitcast(I32)]]
        g_row = [part(2 * c.blocks * P)[0:1, :].rearrange("p (s g) -> p s g", s=2) for c in (GAT, GCN)]
        assert part.at <= J * H
        flat_rows = rows[:, :, :].rearrange("p s n -> p (s n)")
        step_of = flat_rows[:, 0:GCN.blocks * P].bitcast(I32)
        g_from = [a.bitcast(BF16).rearrange("p (g n) -> p g n", n=c.blocks * P) for a, c in (
            (edge[:, 0:GAT.blocks ** 2 * P // 2], GAT),
            (flat_rows[:, GCN.blocks * P:GCN.blocks * P + GCN.blocks ** 2 * P // 2], GCN))]
        g_first = [a[:, 2, :] for a in stepcols]
        g_val = [a[:, 3, :].bitcast(BF16).rearrange("p (g v) -> p g v", v=2) for a in stepcols]
        part = Region(edge[:, J * H:2 * J * H])
        dst_i = part(J).bitcast(I32)
        blk_i = part(J).bitcast(I32)
        blk_f = part(J)
        low_i = part(J).bitcast(I32)
        low_f = part(J)
        hot_flat = part(JB * P).bitcast(BF16)
        hot_low = hot_flat.rearrange("p (b j n) -> p b j n", b=2, j=JB)
        src_hot = hot_flat[:, 0:2 * KT * Q * P].rearrange("p (b k n) -> p b k n", b=2, k=KT)
        part = Region(rows[:, 2:6, :].rearrange("p s n -> p (s n)"))
        b_f = part(2 * 2 * GE).rearrange("p (b s e) -> p b s e", b=2, s=2)
        part = Region(rows[:, 6:8, :].rearrange("p s n -> p (s n)"))
        hot_blk = part(JB * TILES).bitcast(BF16).rearrange("p (b j n) -> p b j n", b=2, j=JB)
        part = Region(rows[:, 2:6, :].rearrange("p s n -> p (s n)"))
        low_all = part(4 * Q * P // 2).bitcast(F16).rearrange("p (b n) -> p b n", b=4)
        picked = part(Q * NA * H).rearrange("p (q a h) -> p q a h", q=Q, h=H)
        part = Region(big[:, :])
        er = part(J * H).rearrange("p (j h) -> p j h", h=H)
        dst_f = part(J)
        cont = part(J + 1)
        pen = part(J + 1)
        scan = part(J)
        b_i = [part(c.blocks * 2 * c.edges).bitcast(I32).rearrange("p (b s e) -> p b s e", b=c.blocks, s=2)
               for c in (GAT, GCN)]
        el_parts = part(3 * NA * KT * H // 2).bitcast(BF16).rearrange("p (s t h) -> p s t h", s=3, h=H)
        el_rest = part(TILES * H).rearrange("p (t h) -> p t h", h=H)
        carry_row = part(3 * (P + 1))[0:H, :].rearrange("p (s n) -> p s n", s=3)
        low_T = part(2 * P).bitcast(F16).rearrange("p (b n) -> p b n", n=P)

        def acc(t):
            return big[:, ds(t * AW, D)]

        def first(t):
            return big[:, ds(t * D, D)]

        mm = [ps("mm0", [P, D]), ps("mm1", [P, D])]
        tr = [ps("tr0", [P, D]), ps("tr1", [P, D])]
        sm = [ps("sm0", [P, D]), ps("sm1", [P, D])]
        hist_ps = ps("hist_ps", [P, D])
        misc = ps("misc", [P, D])
        sum_ps, den_ps = mm + tr, sm + [hist_ps, misc]

        pad_set, const_set, ident_set, edges_kept, fold_in, edges_in, dst_in = map(sem, (
            "pad_set", "const_set", "ident_set", "edges_kept", "fold_in", "edges_in", "dst_in"))
        firsts_in = [sem("firsts_in0"), sem("firsts_in1")]
        borders_in, bval_in = sem("borders_in"), sem("bval_in")
        dve_setup, folded = sem("dve_setup"), sem("folded")
        x_in = [sem(f"x_in{c}") for c in range(TILES // XL + 1)]
        stat_set, ln_set, std_set, h_set, h_turned, hT_set, eler_sum, eler_set = map(sem, (
            "stat_set", "ln_set", "std_set", "h_set", "h_turned", "hT_set", "eler_sum", "eler_set"))
        el_kept, er_zeroed, wval_in, v_sum, v_set, step_of_set = map(sem, (
            "el_kept", "er_zeroed", "wval_in", "v_sum", "v_set", "step_of_set"))
        v_kept = [sem("v_kept0"), sem("v_kept1")]
        el_in = [sem("el_in0"), sem("el_in1")]
        srcdst_in = [sem("srcdst_in0"), sem("srcdst_in1")]
        er_scattered, er_in, w_kept, el_idx_set, sc_idx_set = map(sem, (
            "er_scattered", "er_in", "w_kept", "el_idx_set", "sc_idx_set"))
        el_placed = sem("el_placed")
        w_in = [sem(f"w_in{k}") for k in range(GAT.blocks)]
        dve_prep, pe_prep, hot_set, hot_used, std_deg, er_idx_set, w_exp = map(sem, (
            "dve_prep", "pe_prep", "hot_set", "hot_used", "std_deg", "er_idx_set", "w_exp"))
        w_turned, w_placed = sem("w_turned"), sem("w_placed")
        low_kept, src_hot_set, el_summed, el_chain, el_picked = map(sem, (
            "low_kept", "src_hot_set", "el_summed", "el_chain", "el_picked"))
        low_in = [sem(f"low_in{b}") for b in range(4)]
        agg = []
        for n, c in (("gat", 0), ("gcn1", 1), ("gcn2", 1)):
            agg.append(dict(
                cut=(GAT, GCN)[c], src=src_step[c], ndrel=ndrel[c], slot=slot_i[c],
                rows_in=[sem(f"{n}_rows_in{u}") for u in range((GAT, GCN)[c].slots)],
                idx_set=sem(f"{n}_idx_set"), dist_set=sem(f"{n}_dist_set"), onehot_set=sem(f"{n}_onehot_set"),
                msg_set=sem(f"{n}_msg_set"), step_sum=sem(f"{n}_step_sum"), acc_added=sem(f"{n}_acc_added")))
        xb_set = sem("xb_set")
        rden_set, xr_scaled, x1_set, x1_stat, x1_var, x1_std, x1_rstd, x1_nmr = map(sem, (
            "rden_set", "xr_scaled", "x1_set", "x1_stat", "x1_var", "x1_std", "x1_rstd", "x1_nmr"))
        xr_in = [sem("xr_in0"), sem("xr_in1")]
        x1_kept = [sem("x1_kept0"), sem("x1_kept1")]
        mids = []
        for n in ("gcn1", "gcn2"):
            mids.append(dict(
                w_in=sem(f"{n}_w_in"), y_set=sem(f"{n}_y_set"), h_set=sem(f"{n}_h_set"), turned=sem(f"{n}_turned"),
                hT_set=sem(f"{n}_hT_set"), summed=sem(f"{n}_summed"), tab_set=sem(f"{n}_tab_set"),
                seeded=sem(f"{n}_seeded"), kept=[sem(f"{n}_kept0"), sem(f"{n}_kept1")]))
        b_in = [sem("b1_in"), sem("b2_in")]
        y_set, out_set = sem("y_set"), sem("out_set")
        x1_in_out_kept = [sem(f"x1_in_out_kept{n}") for n in range(OS)]

        def slot_total(t, par, per=16):
            return (t - par) * (per // 2) + per

        def all_kept(eng, pair, per=16):
            eng.wait_ge(pair[0], per * ((TILES + 1) // 2))
            eng.wait_ge(pair[1], per * (TILES // 2))

        waits_passed = {eng: sem(f"waits_passed_{eng}") for eng in ("pool", "dve")}

        def wait_alone(name, eng, which, value):
            eng.wait_ge(which, value)
            eng.sem_inc(waits_passed[name], 1)

        def on_all(vec):
            return vec.rearrange("(a n) -> a n", a=1).broadcast_to([P, D])

        block = ctx.enter_context(nc.Block())

        prep, pe_steps, b_turn = [0], [0], [0]
        marks = {}

        @block.vector
        def _(dve):
            def did(ins):
                prep[0] += 1
                ins.then_inc(dve_prep, 1)
                dve.wait_ge(dve_prep, prep[0])

            def turned():
                pe_steps[0] += 1
                dve.wait_ge(pe_prep, pe_steps[0])

            dve.wait_ge(const_set, 9)
            did(dve.tensor_copy(iota[:, :], iota_i[:, :]))
            did(dve.tensor_copy(stepf[:, :], step_i[:, :]))
            did(dve.tensor_copy(low_id[:, :], low_i4[:, :]))

            for n, c in enumerate((GAT, GCN)):
                dve.wait_ge(firsts_in[n], 32)
                G = c.groups
                (first_i, last_i), row = g_i[n], g_row[n]
                counted, summed = first_i.bitcast(F32), last_i.bitcast(F32)
                did(dve.memset(row[:, 0, :], 1e6))
                did(dve.memset(row[:, 1, :], 0.0))
                did(dve.tensor_scalar(first_i, first_i, 7, None, ALU.arith_shift_right))
                did(dve.tensor_scalar(last_i, last_i, 7, None, ALU.arith_shift_right))
                did(dve.tensor_copy(row[:, 1, 0:G], first_i))
                did(dve.tensor_copy(row[:, 0, 0:G], last_i))
                did(dve.scalar_tensor_tensor(counted, row[:, 0, 0:G], 1.0, row[:, 1, 0:G], ALU.add, ALU.subtract))
                did(dve.tensor_tensor_scan(summed, ones[0:1, 0:1].to_broadcast([1, G]), counted, 0.0, ALU.mult, ALU.add))
                did(dve.tensor_tensor(row[:, 0, 0:G], summed, counted, ALU.subtract))
                did(dve.tensor_tensor(summed, row[:, 1, 0:G], row[:, 0, 0:G], ALU.subtract))
                did(dve.tensor_copy(row[:, 1, 0:1], summed[:, 0:1]))
                did(dve.tensor_tensor(row[:, 1, 1:G], summed[:, 1:G], summed[:, 0:G - 1], ALU.subtract))
                marks[f"groups{n}"] = prep[0]

            dve.wait_ge(fold_in, 96)
            for s, w in enumerate((W_src_sb, W_dst_sb)):
                if s:
                    dve.wait_ge(folded, 5)
                dve.tensor_tensor(fold, w[:, :, :], attn_sb[:, s, :].unsqueeze(1).to_broadcast([P, KC, D]),
                                  ALU.mult).then_inc(dve_setup, 1)
                dve.tensor_tensor(bfold[:, s, :], bsd_sb[:, s, :], attn_sb[:, s, :], ALU.mult).then_inc(dve_setup, 1)
                dve.wait_ge(dve_setup, 2 * s + 2)
                for k in range(KC):
                    dve.tensor_reduce(wlr[:, k, s * H:(s + 1) * H], fold[:, k, :].rearrange("p (h f) -> p h f", f=F),
                                      AX.X, ALU.add).then_inc(folded, 1)
                dve.tensor_reduce(blr[:, s * H:(s + 1) * H], bfold[:, s, :].rearrange("p (h f) -> p h f", f=F),
                                  AX.X, ALU.add).then_inc(folded, 1)
            dve.wait_ge(folded, 10)

            dve.wait_ge(step_of_set, 1)
            for n, c in enumerate((GAT, GCN)):
                turned()
                did(dve.memset(g_val[n], 1.0))
                did(dve.tensor_copy(g_first[n], sm[0][:, 0:c.blocks]))
                did(dve.tensor_copy(g_val[n][:, :, 1], sm[0][:, c.blocks:2 * c.blocks]))
                for g in range(c.blocks):
                    did(dve.tensor_scalar(g_from[n][:, g, :], step_of[:, 0:c.blocks * P], g_first[n][:, g:g + 1], None, ALU.is_ge))
                marks[f"from{n}"] = prep[0]
                turned()
                cols = stepcols[n][:, :, :]
                did(dve.tensor_copy(cols[:, 0:2, :], sm[1][:, 0:2 * c.blocks].rearrange("p (b v) -> p v b", v=2)))
                did(dve.tensor_scalar(gidx[n][:, :], cols[:, 0, :], -1.0, None, ALU.add))
                marks[f"gidx{n}"] = prep[0]
                did(dve.tensor_tensor(cols[:, 4, :], cols[:, 1, :], stepf[:, 0:c.blocks], ALU.add))
                did(dve.tensor_scalar(tile0[n][:, :], cols[:, 4, :], float(P), None, ALU.mult))
                did(dve.tensor_scalar(cols[:, 5, :], cols[:, 4, :], float(TILES - 1), float(AW), ALU.min, ALU.mult))
                marks[f"slots{n}"] = prep[0]
                turned()
                did(dve.memset(slot_i[n][0:1, 0:LAG], 0))
                for lo in range(0, c.blocks * P, D):
                    hi = min(lo + D, c.blocks * P)
                    did(dve.tensor_copy(slot_i[n][0:1, LAG + lo:LAG + hi], mm[lo // D][0:1, 0:hi - lo]))
                marks[f"slots_out{n}"] = prep[0]

            for c in range(TILES // XL):
                dve.wait_ge(x_in[c], 16)
                with dve.Fori(0, 2) as i:
                    for n in range(XL // 2):
                        t = i * (XL // 2) + (c * XL + n)
                        dve.bn_stats(stat[:, t, :], first(t)).then_inc(stat_set, 1)
            dve.wait_ge(x_in[TILES // XL], 16)
            dve.bn_stats(stat[:, TILES - 1, :], first(TILES - 1)).then_inc(stat_set, 1)
            dve.wait_ge(stat_set, TILES)
            dve.tensor_tensor(ln[:, 0, :], stat[:, :, 1], stat[:, :, 4], ALU.add).then_inc(ln_set, 1)
            dve.tensor_tensor(ln[:, 1, :], stat[:, :, 1], stat[:, :, 4], ALU.subtract).then_inc(ln_set, 1)
            dve.tensor_tensor(ln[:, 2, :], stat[:, :, 2], stat[:, :, 5], ALU.add).then_inc(ln_set, 1)
            dve.wait_ge(ln_set, 3)
            dve.tensor_tensor(ln[:, 3, :], ln[:, 1, :], ln[:, 1, :], ALU.mult).then_inc(ln_set, 1)
            dve.tensor_scalar(ln[:, 0, :], ln[:, 0, :], 0.5, None, ALU.mult).then_inc(ln_set, 1)
            dve.tensor_scalar(ln[:, 2, :], ln[:, 2, :], 1.0 / D, None, ALU.mult).then_inc(ln_set, 1)
            dve.wait_ge(ln_set, 6)
            dve.scalar_tensor_tensor(ln[:, 1, :], ln[:, 3, :], 0.25, ln[:, 2, :], ALU.mult, ALU.add).then_inc(ln_set, 1)
            dve.wait_ge(std_set, 1)
            dve.reciprocal(ln[:, 2, :], ln[:, 3, :]).then_inc(ln_set, 1)
            dve.wait_ge(ln_set, 8)
            dve.scalar_tensor_tensor(ln[:, 1, :], ln[:, 0, :], -1.0, ln[:, 2, :], ALU.mult, ALU.mult).then_inc(ln_set, 1)

            dve.wait_ge(dst_in, 16)
            did(dve.tensor_scalar(blk_i, dst_i, 7, None, ALU.arith_shift_right))
            did(dve.tensor_scalar(low_i, dst_i, P - 1, None, ALU.bitwise_and))
            did(dve.tensor_copy(blk_f, blk_i))
            did(dve.tensor_copy(low_f, low_i))

            def first_layer(s):
                if s.live():
                    t, par = s.k, s.j
                    dve.wait_ge(h_turned, t + 1)
                    if s.past(2):
                        dve.wait_ge(eler_sum, t - 1)
                    dve.tensor_copy(rows[:, 4 + par, :], tr[par][:, :]).then_inc(hT_set, 1)
                    if s.inner or t < HB:
                        b = t
                        if s.past(2):
                            dve.wait_ge(hot_used, b - 1)
                        dve.tensor_tensor(hot_low[:, par, :, :],
                                          low_f[:, ds(b * JB, JB)].unsqueeze(2).to_broadcast([P, JB, P]),
                                          iota[:, :].unsqueeze(1).to_broadcast([P, JB, P]), ALU.is_equal).then_inc(hot_set, 1)
                        dve.tensor_tensor(hot_blk[:, par, :, :],
                                          blk_f[:, ds(b * JB, JB)].unsqueeze(2).to_broadcast([P, JB, TILES]),
                                          iota[:, 0:TILES].unsqueeze(1).to_broadcast([P, JB, TILES]),
                                          ALU.is_equal).then_inc(hot_set, 1)
                if s.live(1):
                    t, par = s.k - 1, (s.j - 1) % 2
                    dve.wait_ge(eler_sum, t + 1)
                    dve.tensor_tensor(eler[:, t, :], sm[par][:, 0:2 * H], blr[:, :], ALU.add).then_inc(eler_set, 1)
            pipelined(dve, TILES, 2, 1, first_layer, tail=4)

            dve.wait_ge(hot_used, HB)
            did(dve.tensor_copy(hist[:, :], hist_ps[:, 0:TILES]))
            marks["hist"] = prep[0]
            did(dve.tensor_copy(small[:, 0, :], node_i[:, :]))
            turned()
            did(dve.tensor_copy(small[:, 1, :], misc[:, 0:TILES]))
            did(dve.tensor_tensor_scan(small[:, 2, :], ones[:, 0:TILES], small[:, 1, :], 0.0, ALU.mult, ALU.add))
            did(dve.tensor_tensor(small[:, 3, :], small[:, 2, :], small[:, 1, :], ALU.subtract))
            did(dve.tensor_tensor(small[:, 4, :], small[:, 3, :], sm[0][:, 0:TILES], ALU.add))
            did(dve.tensor_tensor(small[:, 3, :], small[:, 4, :], small[:, 0, :], ALU.subtract))
            did(dve.scalar_tensor_tensor(small[:, 5, :], hist[:, :], 0.0, small[:, 3, :], ALU.is_gt, ALU.mult))
            dve.tensor_tensor(er_idx[:, :], small[:, 5, :], small[:, 0, :], ALU.add).then_inc(er_idx_set, 1)
            dve.wait_ge(std_deg, 1)
            did(dve.reciprocal(dinv[:, :], small[:, 6, :]))
            did(dve.tensor_scalar(ind[:, :], hist[:, :], 0.0, None, ALU.is_gt))

            dve.wait_ge(h_set, TILES)
            did(dve.memset(er.rearrange("p j h -> p (j h)"), 0.0))
            marks["er_zero"] = prep[0]
            did(dve.tensor_copy(dst_f, dst_i))

            did(dve.tensor_scalar(low_i[:, 0:PCOLS], src_flat[:, J0:J], KT * P - 1, None, ALU.bitwise_and))
            did(dve.tensor_scalar(blk_i[:, 0:PCOLS], src_flat[:, J0:J], 9, None, ALU.arith_shift_right))
            did(dve.tensor_copy(low_f[:, 0:PCOLS], low_i[:, 0:PCOLS]))
            did(dve.tensor_copy(blk_f[:, 0:PCOLS], blk_i[:, 0:PCOLS]))
            marks["low"] = prep[0]
            did(dve.memset(el_parts[:, :, TILES:, :], 0.0))
            did(dve.tensor_copy(el_parts[:, 0, 0:TILES, :], eler[:, :, 0:H]))
            did(dve.tensor_tensor(el_rest, eler[:, :, 0:H], el_parts[:, 0, 0:TILES, :], ALU.subtract))
            did(dve.tensor_copy(el_parts[:, 1, 0:TILES, :], el_rest))
            did(dve.tensor_tensor(el_rest, el_rest, el_parts[:, 1, 0:TILES, :], ALU.subtract))
            did(dve.tensor_copy(el_parts[:, 2, 0:TILES, :], el_rest))
            marks["parts"] = prep[0]
            turned()
            full, left = divmod(PCOLS, P)
            did(dve.tensor_copy(low_T[:, 0:full, :], misc[:, 0:full * P].rearrange("p (b n) -> p b n", n=P)))
            did(dve.tensor_copy(low_T[0:left, full, :], misc[0:left, full * P:(full + 1) * P]))
            marks["low_T"] = prep[0]

            for n, c in enumerate((GAT, GCN)):
                dve.wait_ge(srcdst_in[n], 16 * 2 * c.blocks)
                for b in range(c.blocks):
                    i = b_turn[0]
                    b_turn[0] += 1
                    n_w = min(P, c.steps - b * P)
                    half = b_f[:, i % 2, :, 0:c.edges]
                    did(dve.tensor_copy(half[:, 0, :], b_i[n][:, b, 0, :]))
                    did(dve.tensor_scalar(half[:, 1, :], b_i[n][:, b, 1, :], tile0[n][:, b:b + 1], -1.0,
                                          ALU.subtract, ALU.mult))
                    marks[f"block{i}"] = prep[0]
                    turned()
                    got = tr[i % 2][:, 0:2 * c.edges].rearrange("p (s c w) -> p s w c", s=2, c=c.chunks)
                    at = slice(b * P * c.chunks, (b * P + n_w) * c.chunks)
                    did(dve.tensor_copy(src_step[n][:, at].rearrange("p (w c) -> p w c", c=c.chunks), got[:, 0, 0:n_w, :]))
                    did(dve.tensor_copy(ndrel[n][:, at].rearrange("p (w c) -> p w c", c=c.chunks), got[:, 1, 0:n_w, :]))
            marks["tables"] = prep[0]

            dve.wait_ge(borders_in, 32)
            did(dve.tensor_copy(edgecols[:, :], edgecols_i[:, :]))
            did(dve.tensor_tensor(cont[:, 1:J], dst_f[:, 1:J], dst_f[:, 0:J - 1], ALU.is_equal))
            did(dve.tensor_tensor(cont[:, 0:1], dst_f[:, 0:1], edgecols[:, 0:1], ALU.is_equal))
            did(dve.tensor_tensor(cont[:, J:J + 1], dst_f[:, J - 1:J], edgecols[:, 1:2], ALU.is_equal))
            did(dve.tensor_scalar(pen, cont, -1.0, BIG, ALU.add, ALU.mult))

            def pick(s):
                if s.live():
                    g, par = s.k, s.j % 2
                    dve.wait_ge(low_in[s.j], (g - s.j) * 4 + 16)
                    if s.past(2):
                        dve.wait_ge(el_summed, g - 1)
                    for kt in range(KT):
                        dve.tensor_scalar(src_hot[:, par, kt, :], low_all[:, s.j, :], low_id[:, kt:kt + 1], None,
                                          ALU.is_equal).then_inc(src_hot_set, 1)
                if s.live(1):
                    g, par = s.k - 1, (s.j - 1) % 2
                    dve.tensor_tensor(a_hot[:, :, :], blk_f[:, ds(g * Q, Q)].unsqueeze(2).to_broadcast([P, Q, NA]),
                                      iota[:, 0:NA].unsqueeze(1).to_broadcast([P, Q, NA]), ALU.is_equal).then_inc(el_chain, 1)
                    dve.wait_ge(el_chain, 2 * g + 1)
                    dve.wait_ge(el_summed, g + 1)
                    dve.tensor_tensor(picked[:, :, :, :],
                                      mm[par][:, 0:Q * NA * H].rearrange("p (q a h) -> p q a h", q=Q, h=H),
                                      a_hot[:, :, :].unsqueeze(3).to_broadcast([P, Q, NA, H]), ALU.mult).then_inc(el_chain, 1)
                    dve.wait_ge(el_chain, 2 * g + 2)
                    dve.tensor_reduce(edge[:, ds(g * (Q * H) + J0 * H, Q * H)].rearrange("p (q h) -> p q h", h=H),
                                      picked[:, :, :, :].rearrange("p q a h -> p q h a"), AX.X, ALU.add).then_inc(el_picked, 1)
            pipelined(dve, PCOLS // Q, 4, 1, pick)
            dve.wait_ge(el_picked, PCOLS // Q)

            def carries(local, is_max, back):
                flags = cont[:, 1:J + 1] if back else cont[:, 0:J]
                for h in range(H):
                    local(h)
                did(dve.tensor_reduce(carry[:, 0:1], flags, AX.X, ALU.min))
                if is_max:
                    did(dve.tensor_scalar(carry[:, 0:1], carry[:, 0:1], -1.0, BIG, ALU.add, ALU.mult))
                did(dve.tensor_copy(tail_st[:, 1, :], carry[:, 0:1].to_broadcast([P, H])))
                marks.setdefault("ends", []).append(prep[0])
                turned()
                did(dve.tensor_copy(carry_row[:, 0:2, 0:P], misc[0:H, 0:2 * P].rearrange("p (s n) -> p s n", s=2)))
                start = -BIG if is_max else 0.0
                edge_col = P if back else 0
                did(dve.memset(carry_row[:, 2, edge_col:edge_col + 1], start))
                ops = (ALU.add, ALU.max) if is_max else (ALU.mult, ALU.add)
                if back:
                    did(dve.tensor_tensor_scan(carry_row[:, 2, 0:P][:, ::-1], carry_row[:, 1, 0:P][:, ::-1],
                                               carry_row[:, 0, 0:P][:, ::-1], start, *ops))
                else:
                    did(dve.tensor_tensor_scan(carry_row[:, 2, 1:P + 1], carry_row[:, 1, 0:P],
                                               carry_row[:, 0, 0:P], start, *ops))
                marks.setdefault("carried", []).append(prep[0])
                turned()
                did(dve.tensor_copy(carry[:, :], sm[1][:, 0:H]))

            dve.wait_ge(er_in, 16)

            def er_local(h):
                did(dve.tensor_tensor_scan(scan[:, :], cont[:, 0:J], er[:, :, h], 0.0, ALU.mult, ALU.add))
                did(dve.tensor_copy(tail_st[:, 0, h:h + 1], scan[:, J - 1:J]))
            carries(er_local, False, False)
            for h in range(H):
                did(dve.tensor_tensor_scan(scan[:, :], cont[:, 0:J], er[:, :, h], carry[:, h:h + 1], ALU.mult, ALU.add))
                did(dve.tensor_copy(er[:, :, h], scan[:, :]))

            dve.wait_ge(el_placed, EL_BATCHES)

            def top_local(h):
                did(dve.tensor_tensor_scan(scan[:, :], pen[:, 0:J], el[:, :, h], -BIG, ALU.add, ALU.max))
                did(dve.tensor_copy(tail_st[:, 0, h:h + 1], scan[:, J - 1:J]))
            carries(top_local, True, False)
            for h in range(H):
                did(dve.tensor_tensor_scan(top[:, :, h], pen[:, 0:J], el[:, :, h], carry[:, h:h + 1], ALU.add, ALU.max))
            did(dve.tensor_tensor(el, el, er, ALU.add))

            def back_local(h):
                did(dve.tensor_tensor_scan(scan[:, ::-1], pen[:, 1:J + 1][:, ::-1], top[:, ::-1, h], -BIG,
                                           ALU.add, ALU.max))
                did(dve.tensor_copy(tail_st[:, 0, h:h + 1], scan[:, 0:1]))
            carries(back_local, True, True)
            for h in range(H):
                did(dve.tensor_tensor_scan(scan[:, ::-1], pen[:, 1:J + 1][:, ::-1], top[:, ::-1, h],
                                           carry[:, h:h + 1], ALU.add, ALU.max))
                did(dve.tensor_tensor(top[:, :, h], scan[:, :], er[:, :, h], ALU.add))
            did(dve.scalar_tensor_tensor(el, el, SLOPE, el, ALU.mult, ALU.max))
            did(dve.scalar_tensor_tensor(top, top, SLOPE, top, ALU.mult, ALU.max))
            did(dve.tensor_tensor(el, el, top, ALU.subtract))
            marks["arg"] = prep[0]
            did(dve.memset(big[:, :], 0.0))
            dve.wait_ge(w_kept, 16)
            for b in range(GAT.blocks):
                n_w = min(P, SP - b * P)
                for q in range(4):
                    i = 4 * b + q
                    dve.wait_ge(w_turned, i + 1)
                    dve.tensor_copy(w_step[:, b * P:b * P + n_w, 4 * q:4 * q + 4],
                                    tr[i % 2][:, :].rearrange("p (q w) -> p w q", q=4)[:, 0:n_w, :]).then_inc(w_placed, 1)
            dve.wait_ge(w_placed, 4 * GAT.blocks)

            def aggregate(a, weighted):
                per = 2 if weighted else 1
                c, offs = a["cut"], [None]

                def step(s):
                    if weighted and s.live():
                        w, u = s.k, s.j % c.slots
                        dve.wait_ge(a["rows_in"][u], (w - u) * 8 + 32)
                        view = rows[:, 2 * u:2 * u + 2, :].rearrange("p c (h f) -> p (c h) f", f=F)
                        dve.tensor_tensor(view, view, w_step[:, w, :].unsqueeze(2).to_broadcast([P, 2 * H, F]),
                                          ALU.mult).then_inc(a["msg_set"], 1)
                    if s.j % BANKS == 0:
                        _, offs[0] = nc.values_load_multi_w_load_instructions(
                            a["slot"][0:1, ds(s.k, BANKS)], engines=(mybir.EngineType.DVE,), min_val=0,
                            max_val=(TILES - 1) * AW, skip_runtime_bounds_check_because="clamped when the table is made")
                    if s.live(LAG):
                        w, bank = s.k - LAG, (s.j - LAG) % BANKS
                        dve.wait_ge(a["step_sum"], w + 1)
                        if s.past(1, LAG):
                            dve.wait_ge(a["acc_added"], per * w)
                        o = offs[0][s.j % BANKS]
                        dve.tensor_tensor(big[:, ds(o, D)], big[:, ds(o, D)], sum_ps[bank][:, :], ALU.add).then_inc(a["acc_added"], 1)
                        if weighted:
                            den = big[:, ds(o + D, H)]
                            dve.tensor_tensor(den, den, den_ps[bank][:, 0:H], ALU.add).then_inc(a["acc_added"], 1)
                pipelined(dve, c.steps, 2 * BANKS, LAG, step)
            aggregate(agg[0], True)

            def bank_out(m, s, lag):
                if s.live(lag):
                    t, par = s.k - lag, (s.j - lag) % 2
                    dve.wait_ge(m["turned"], t + 1)
                    if s.past(2, lag):
                        dve.wait_ge(m["summed"], t - 1)
                    dve.tensor_copy(rows[:, 4 + par, :], tr[par][:, :]).then_inc(m["hT_set"], 1)

            dve.wait_ge(bval_in, 16)
            dve.wait_ge(agg[0]["acc_added"], 2 * SP)
            den = big[:, :].rearrange("p (t n) -> p t n", n=AW)[:, :, D:AW]
            dve.tensor_scalar(rden[:, :, :], den, 1e-16, None, ALU.max).then_inc(rden_set, 1)
            dve.wait_ge(rden_set, 1)
            dve.reciprocal(rden[:, :, :], rden[:, :, :]).then_inc(rden_set, 1)
            dve.wait_ge(rden_set, 2)

            def residual(s):
                if s.live():
                    t = s.k
                    a_t = acc(t).rearrange("p (h f) -> p h f", f=F)
                    dve.tensor_tensor(a_t, a_t, rden[:, t, :].unsqueeze(2).to_broadcast([P, H, F]),
                                      ALU.mult).then_inc(xr_scaled, 1)
                    t, par = s.k, s.j
                    dve.wait_ge(xr_in[par], slot_total(t, par))
                    dve.scalar_tensor_tensor(rows[:, par, :], bias[:, :], ind[:, ds(t, 1)], rows[:, par, :],
                                             ALU.mult, ALU.add).then_inc(xb_set, 1)
                if s.live(2):
                    t, par = s.k - 2, s.j
                    dve.wait_ge(x1_set, t + 1)
                    dve.bn_stats(x1_stats[:, par, :], acc(t)).then_inc(x1_stat, 1)
                    wait_alone("dve", dve, x1_stat, t + 1)
                    dve.bn_aggr(mv[:, par, :], x1_stats[:, par, :]).then_inc(x1_var, 1)
                if s.live(3):
                    t, par = s.k - 3, (s.j - 1) % 2
                    dve.wait_ge(x1_std, t + 1)
                    if s.past(2, 3):
                        dve.wait_ge(mids[0]["h_set"], t - 1)
                    dve.reciprocal(small[:, 7, par:par + 1], std[:, par:par + 1]).then_inc(x1_rstd, 1)
                    dve.wait_ge(x1_rstd, 2 * t + 1)
                    dve.tensor_tensor(rstd[:, par:par + 1], small[:, 7, par:par + 1], dinv[:, ds(t, 1)],
                                      ALU.mult).then_inc(x1_rstd, 1)
                    dve.wait_ge(x1_rstd, 2 * t + 2)
                    dve.tensor_scalar(nmr[:, par:par + 1], mv[:, par, 0:1], rstd[:, par:par + 1], -1.0,
                                      ALU.mult, ALU.mult).then_inc(x1_nmr, 1)
                bank_out(mids[0], s, 4)
            pipelined(dve, TILES, 2, 4, residual)

            dve.wait_ge(mids[0]["seeded"], TILES)
            aggregate(agg[1], False)

            dve.wait_ge(b_in[0], 16)
            dve.wait_ge(agg[1]["acc_added"], GCN.steps)

            def between(s):
                if s.live():
                    t = s.k
                    dve.scalar_tensor_tensor(acc(t), acc(t), dinv[:, ds(t, 1)], bias[:, :],
                                             ALU.mult, ALU.add).then_inc(mids[1]["y_set"], 1)
                bank_out(mids[1], s, 2)
            pipelined(dve, TILES, 2, 2, between)

            dve.wait_ge(mids[1]["seeded"], TILES)
            aggregate(agg[2], False)

            dve.wait_ge(b_in[1], 16)
            dve.wait_ge(agg[2]["acc_added"], GCN.steps)

            def finish(s):
                if s.live():
                    t = s.k
                    dve.scalar_tensor_tensor(acc(t), acc(t), dinv[:, ds(t, 1)], bias[:, :],
                                             ALU.mult, ALU.add).then_inc(y_set, 1)
                if s.live(1):
                    t, slot = s.k - 1, (s.j - 1) % OS
                    dve.wait_ge(y_set, t + 1)
                    dve.wait_ge(x1_in_out_kept[slot], (t - slot) * (32 // OS) + 16)
                    dve.scalar_tensor_tensor(rows[:, slot, :], acc(t), 0.0, rows[:, slot, :],
                                             ALU.max, ALU.add).then_inc(out_set, 1)
            pipelined(dve, TILES, OS, 1, finish)

        @block.sync
        def _(sp):
            sp.dma_start(src_rows.rearrange("g e -> (g e)")[0:E].rearrange("(a n) -> a n", a=16),
                         src.rearrange("(a n) -> a n", a=16)).then_inc(edges_kept, 16)
            sp.dma_start(dst_rows.rearrange("g e -> (g e)")[0:E].rearrange("(a n) -> a n", a=16),
                         dst.rearrange("(a n) -> a n", a=16)).then_inc(edges_kept, 16)
            sp.wait_ge(pad_set, 2)
            sp.dma_start(src_rows.rearrange("g e -> (g e)")[E:EP].rearrange("(a n) -> a n", a=1),
                         pad_i[:, 0, :]).then_inc(edges_kept, 16)
            sp.dma_start(dst_rows.rearrange("g e -> (g e)")[E:EP].rearrange("(a n) -> a n", a=1),
                         pad_i[:, 1, :]).then_inc(edges_kept, 16)
            sp.wait_ge(edges_kept, 64)
            dst_line = dst_rows.rearrange("g e -> (g e)")

            def load_firsts(n, c):
                by_group = dst_line.rearrange("(g e) -> g e", e=c.edges)
                with nc.allow_non_contiguous_dma(reason="first and last dst of every group"):
                    for s in range(2):
                        sp.dma_start(g_i[n][s], by_group[:, s * (c.edges - 1):s * (c.edges - 1) + 1].rearrange(
                            "g e -> e g")).then_inc(firsts_in[n], 16)
            load_firsts(0, GAT)
            load_firsts(1, GCN)
            sp.dma_start(W_src_sb[:, :, :], W_src.rearrange("(k p) n -> p k n", p=P)).then_inc(fold_in, 16)
            sp.dma_start(W_dst_sb, W_dst.rearrange("(k p) n -> p k n", p=P)).then_inc(fold_in, 16)
            sp.dma_start(attn_sb[:, 0, :], on_all(attn_l.rearrange("h f -> (h f)"))).then_inc(fold_in, 16)
            sp.dma_start(attn_sb[:, 1, :], on_all(attn_r.rearrange("h f -> (h f)"))).then_inc(fold_in, 16)
            sp.dma_start(bsd_sb[:, 0, :], on_all(b_src)).then_inc(fold_in, 16)
            sp.dma_start(bsd_sb[:, 1, :], on_all(b_dst)).then_inc(fold_in, 16)
            sp.dma_start(bias[:, :], on_all(b_val)).then_inc(bval_in, 16)
            dst_flat = dst_line.rearrange("(p j) -> p j", j=J)
            sp.dma_start(dst_i, dst_flat).then_inc(dst_in, 16)
            sp.wait_ge(pad_set, 4)
            for c in range(TILES // XL):
                sp.dma_start(big[:, c * XL * D:(c + 1) * XL * D].rearrange("p (t d) -> p t d", d=D),
                             x[c * XL * P:(c + 1) * XL * P, :].rearrange("(t p) d -> p t d", p=P)).then_inc(x_in[c], 16)
            sp.dma_start(first(TILES - 1)[0:LAST, :], x[(TILES - 1) * P:N, :]).then_inc(x_in[TILES // XL], 16)
            sp.dma_start(src_flat[:, :], src_rows.rearrange("g e -> (g e)").rearrange("(p j) -> p j", j=J)).then_inc(edges_in, 16)
            sp.wait_ge(folded, 10)
            sp.dma_start(wmat[:, :, :], W_val.rearrange("(k p) n -> p k n", p=P)).then_inc(wval_in, 16)
            with nc.allow_non_contiguous_dma(reason="single dst at the borders of partitions"):
                sp.dma_start(edgecols_i[1:P, 0:1], dst_flat[0:P - 1, J - 1:J]).then_inc(borders_in, 16)
                sp.dma_start(edgecols_i[0:P - 1, 1:2], dst_flat[1:P, 0:1]).then_inc(borders_in, 16)
            def keep_v(s):
                t, par = s.k, s.j
                sp.wait_ge(v_set, t + 1)
                sp.dma_start(v_tab[ds(t * P, P), :], rows[:, par, :]).then_inc(v_kept[par], 16)
            pipelined(sp, TILES, 2, 0, keep_v)
            sp.wait_ge(eler_set, TILES)
            sp.dma_start(el_tab.rearrange("(t p) h -> p t h", p=P), eler[:, :, 0:H]).then_inc(el_kept, 16)
            sp.dma_start(wmat[:, :, :], W1.rearrange("(k p) n -> p k n", p=P)).then_inc(mids[0]["w_in"], 16)
            sp.wait_ge(dve_prep, marks["er_zero"])
            sp.dma_start(er_tab[0:EP, :].rearrange("(p j) h -> p (j h)", j=J),
                         er.rearrange("p j h -> p (j h)")).then_inc(er_zeroed, 16)
            sp.wait_ge(dve_prep, marks["low_T"])
            full, left = divmod(PCOLS, P)
            sp.dma_start(low_tab[0:full * P, :].rearrange("(b r) n -> r b n", r=P), low_T[:, 0:full, :]).then_inc(low_kept, 16)
            sp.dma_start(low_tab[full * P:PCOLS, :], low_T[0:left, full, :]).then_inc(low_kept, 16)
            sp.wait_ge(low_kept, 32)

            sp.wait_ge(dve_prep, marks["tables"])

            def load_low(s):
                if s.past(4):
                    sp.wait_ge(src_hot_set, (s.k - 3) * KT)
                sp.dma_start(low_all[:, s.j, :], low_tab[ds(s.k * Q, Q), :].rearrange("q n -> (q n)").rearrange(
                    "(a n) -> a n", a=1).broadcast_to([P, Q * P])).then_inc(low_in[s.j], 16)
            pipelined(sp, PCOLS // Q, 4, 0, load_low)
            sp.wait_ge(er_scattered, 16 * TILES)
            sp.dma_start(er.rearrange("p j h -> p (j h)"),
                         er_tab[0:EP, :].rearrange("(p j) h -> p (j h)", j=J)).then_inc(er_in, 16)
            sp.wait_ge(w_exp, 1)
            sp.dma_start(w_tab.rearrange("g n -> (g n)").rearrange("(p n) -> p n", p=P),
                         edge[:, 0:J * H]).then_inc(w_kept, 16)

            sp.wait_ge(rden_set, 2)

            def keep_table(m, tab, s, lag):
                if s.live(lag):
                    t, par = s.k - lag, (s.j - lag) % 2
                    sp.wait_ge(m["tab_set"], t + 1)
                    sp.dma_start(tab[ds(t * P, P), :], rows[:, 6 + par, :]).then_inc(m["kept"][par], 16)

            def residual(s):
                t, par = s.k, s.j
                if s.live():
                    if s.past(2):
                        sp.wait_ge(x1_set, t - 1)
                    if s.inner or t < TILES - 1:
                        sp.dma_start(rows[:, par, :], x[ds(t * P, P), :]).then_inc(xr_in[par], 16)
                    else:
                        sp.dma_start(rows[0:LAST, par, :], x[t * P:N, :]).then_inc(xr_in[par], 16)
                if s.live(2):
                    t = s.k - 2
                    sp.wait_ge(x1_set, t + 1)
                    sp.dma_start(x1_tab[ds(t * P, P), :], acc(t)).then_inc(x1_kept[par], 16)
                keep_table(mids[0], h2_tab, s, 6)
            pipelined(sp, TILES, 2, 6, residual, tail=1)
            sp.wait_ge(xb_set, TILES)
            sp.dma_start(bias[:, :], on_all(b1)).then_inc(b_in[0], 16)
            sp.wait_ge(mids[0]["summed"], TILES)
            sp.dma_start(wmat[:, :, :], W2.rearrange("(k p) n -> p k n", p=P)).then_inc(mids[1]["w_in"], 16)

            def between(s):
                keep_table(mids[1], h3_tab, s, 0)
            pipelined(sp, TILES, 2, 0, between)
            sp.wait_ge(mids[1]["y_set"], TILES)
            sp.dma_start(bias[:, :], on_all(b2)).then_inc(b_in[1], 16)

            sp.wait_ge(agg[2]["acc_added"], GCN.steps)

            def finish(s):
                if s.live():
                    t, slot = s.k, s.j
                    if s.past(OS):
                        sp.wait_ge(x1_in_out_kept[slot], (t - slot) * (32 // OS))
                    sp.dma_start(rows[:, slot, :], x1_tab[ds(t * P, P), :]).then_inc(x1_in_out_kept[slot], 16)
                if s.live(4):
                    t, slot = s.k - 4, (s.j - 4) % OS
                    sp.wait_ge(out_set, t + 1)
                    if s.inner or t < TILES - 1:
                        sp.dma_start(out[ds(t * P, P), :], rows[:, slot, :]).then_inc(x1_in_out_kept[slot], 16)
                    else:
                        sp.dma_start(out[t * P:N, :], rows[0:LAST, slot, :]).then_inc(x1_in_out_kept[slot], 16)
            pipelined(sp, TILES, OS, 4, finish, tail=1)
            for slot in range(OS):
                sp.wait_ge(x1_in_out_kept[slot], 32 * len(range(slot, TILES, OS)))

        @block.gpsimd
        def _(pool):
            pool.memset(pad_i[:, 0, :], 0).then_inc(pad_set, 1)
            pool.memset(pad_i[:, 1, :], NP - 1).then_inc(pad_set, 1)
            pool.memset(first(TILES - 1), 0.0).then_inc(pad_set, 1)
            pool.memset(edgecols_i[:, :], -1).then_inc(pad_set, 1)
            pool.memset(ident[:, :], 0.0).then_inc(const_set, 1)
            pool.memset(ones[:, :], 1.0).then_inc(const_set, 1)
            pool.memset(tri[:, :], 1.0).then_inc(const_set, 1)
            pool.memset(epsc[:, :], EPS).then_inc(const_set, 1)
            pool.memset(twoc[:, :], 2.0).then_inc(const_set, 1)
            pool.iota(iota_i[:, :], pattern=[[1, P]], base=0, channel_multiplier=0).then_inc(const_set, 1)
            pool.iota(node_i[:, :], pattern=[[P, TILES]], base=EP, channel_multiplier=1).then_inc(const_set, 1)
            pool.iota(low_i4[:, :], pattern=[[P, KT]], base=0, channel_multiplier=1).then_inc(const_set, 1)
            pool.iota(step_i[:, :], pattern=[[P, GCN.blocks]], base=0, channel_multiplier=1).then_inc(const_set, 1)
            pool.wait_ge(const_set, 5)
            pool.affine_select(out=ident[:, :], in_=ident[:, :], compare_op=ALU.not_equal, fill=1.0, base=0,
                               pattern=[[-1, P]], channel_multiplier=1).then_inc(ident_set, 1)
            pool.affine_select(out=tri[:, :], in_=tri[:, :], compare_op=ALU.is_gt, fill=0.0, base=0,
                               pattern=[[1, P]], channel_multiplier=-1).then_inc(ident_set, 1)

            pool.wait_ge(folded, 10)
            pool.iota(step_of, pattern=[[1, GCN.blocks * P]], base=0, channel_multiplier=0).then_inc(step_of_set, 1)

            pool.wait_ge(h_set, TILES)
            for n, c in enumerate((GAT, GCN)):
                pool.wait_ge(dve_prep, marks[f"gidx{n}"])
                for b in range(c.blocks):
                    for s, tab in enumerate((src_rows, dst_rows)):
                        by_group = tab if c.chunks == 2 else tab.rearrange("g (c e) -> (g c) e", e=c.edges)
                        pool.indirect_dma_start(b_i[n][:, b, s, :], None, by_group,
                                                bass.IndirectOffsetOnAxis(ap=gidx[n][:, b:b + 1], axis=0)).then_inc(srcdst_in[n], 16)

            pool.wait_ge(el_kept, 16)
            pool.wait_ge(edges_in, 16)

            def batch(s):
                g, b = s.k, s.j
                if s.live():
                    pool.tensor_copy(el_idx[:, b, :], src_flat[:, ds(g * EB, EB)]).then_inc(el_idx_set, 1)
                    wait_alone("pool", pool, el_idx_set, g + 1)
                    for n in range(EB):
                        pool.indirect_dma_start(
                            el_rows[:, b, n * H:(n + 1) * H], None, el_tab,
                            bass.IndirectOffsetOnAxis(ap=el_idx[:, b, n:n + 1], axis=0)).then_inc(el_in[b], 16)
                if s.live(1):
                    g, b = s.k - 1, (s.j - 1) % 2
                    wait_alone("pool", pool, el_in[b], (g - b) * (8 * EB) + 16 * EB)
                    pool.tensor_copy(edge[:, ds(g * (EB * H), EB * H)], el_rows[:, b, :]).then_inc(el_placed, 1)
                    wait_alone("pool", pool, el_placed, g + 1)
            for k in range(2):
                batch(Step(k, k, EL_BATCHES, False))
            with pool.Fori(0, (EARLY - 2) // 2) as i:
                for j in range(2):
                    batch(Step(i * 2 + (2 + j), j, EL_BATCHES, True))
            pool.wait_ge(er_idx_set, 1)
            pool.wait_ge(er_zeroed, 16)
            with pool.Fori(0, TILES // SB) as i:
                pool.tensor_copy(sc_idx[:, :], er_idx[:, ds(i * SB, SB)]).then_inc(sc_idx_set, 1)
                pool.tensor_copy(sc_rows[:, :, :], eler[:, ds(i * SB, SB), H:2 * H]).then_inc(sc_idx_set, 1)
                wait_alone("pool", pool, sc_idx_set, i * 2 + 2)
                for n in range(SB):
                    pool.indirect_dma_start(er_tab, bass.IndirectOffsetOnAxis(ap=sc_idx[:, n:n + 1], axis=0),
                                            sc_rows[:, n, :], None).then_inc(er_scattered, 16)
                wait_alone("pool", pool, er_scattered, (i + 1) * (16 * SB))
            with pool.Fori(0, (EL_BATCHES - EARLY) // 2) as i:
                for j in range(2):
                    batch(Step(i * 2 + (EARLY + j), j, EL_BATCHES, True))
            batch(Step(EL_BATCHES, 0, EL_BATCHES, False))
            pool.wait_ge(w_kept, 16)
            for b in range(GAT.blocks):
                if b >= 2:
                    pool.wait_ge(w_turned, 4 * (b - 1))
                pool.indirect_dma_start(w_rows[:, b % 2, :], None, w_tab,
                                        bass.IndirectOffsetOnAxis(ap=gidx[0][:, b:b + 1], axis=0)).then_inc(w_in[b], 16)

            def gather(tab, a):
                c = a["cut"]

                def step(s):
                    w, u, b = s.k, s.j % c.slots, s.j // c.slots
                    if s.past(c.slots):
                        wait_alone("pool", pool, a["step_sum"], w - c.slots + 1)
                    if u == 0:
                        pool.tensor_copy(row_idx[:, b, :], a["src"][:, ds(w * c.chunks, SLOTS)]).then_inc(a["idx_set"], 1)
                        wait_alone("pool", pool, a["idx_set"], s.turn * 2 + (b + 1))
                    for i in range(u * c.chunks, (u + 1) * c.chunks):
                        pool.indirect_dma_start(
                            rows[:, i, :], None, tab,
                            bass.IndirectOffsetOnAxis(ap=row_idx[:, b, i:i + 1], axis=0)).then_inc(a["rows_in"][u], 16)
                pipelined(pool, c.steps, 2 * c.slots, 0, step)

            pool.wait_ge(dve_prep, marks["tables"])
            all_kept(pool, v_kept)
            gather(v_tab, agg[0])

            def seed(m, s, lag):
                if s.live(lag):
                    t, par = s.k - lag, (s.j - lag) % 2
                    wait_alone("pool", pool, m["tab_set"], t + 1)
                    pool.tensor_tensor(acc(t), rows[:, 6 + par, :], rows[:, 6 + par, :], ALU.add).then_inc(m["seeded"], 1)

            def residual(s):
                if s.live():
                    t, par = s.k, s.j
                    wait_alone("pool", pool, xr_scaled, t + 1)
                    wait_alone("pool", pool, xb_set, t + 1)
                    pool.tensor_tensor(acc(t), acc(t), rows[:, par, :], ALU.add).then_inc(x1_set, 1)
                if s.live(5):
                    t, par = s.k - 5, (s.j - 5) % 2
                    wait_alone("pool", pool, x1_kept[par], slot_total(t, par))
                seed(mids[0], s, 5)
            pipelined(pool, TILES, 2, 5, residual)
            all_kept(pool, mids[0]["kept"])
            all_kept(pool, x1_kept)
            gather(h2_tab, agg[1])

            def between(s):
                seed(mids[1], s, 3)
            pipelined(pool, TILES, 2, 3, between)
            all_kept(pool, mids[1]["kept"])
            gather(h3_tab, agg[2])

        @block.scalar
        def _(act):
            act.wait_ge(const_set, 9)

            act.wait_ge(ln_set, 7)
            act.activation(ln[:, 3, :], ln[:, 1, :], ACT.Sqrt, bias=epsc[:, 0:1]).then_inc(std_set, 1)
            act.wait_ge(ln_set, 9)

            def first_layer(s):
                if s.live():
                    t, par = s.k, s.j
                    if s.past(2):
                        act.wait_ge(h_turned, t - 1)
                    act.activation(rows[:, 2 + par, :], first(t), ACT.Relu,
                                   bias=ln[:, 1, ds(t, 1)], scale=ln[:, 2, ds(t, 1)]).then_inc(h_set, 1)
                if s.live(2):
                    t, par = s.k - 2, s.j
                    act.wait_ge(v_sum, t + 1)
                    if s.past(2, 2):
                        act.wait_ge(v_kept[par], slot_total(t - 2, par))
                    act.activation(rows[:, par, :], mm[par][:, :], ACT.Copy).then_inc(v_set, 1)
            pipelined(act, TILES, 2, 2, first_layer)

            act.wait_ge(dve_prep, marks["hist"])
            act.activation(small[:, 6, :], hist[:, :], ACT.Sqrt, bias=twoc[:, 0:1]).then_inc(std_deg, 1)
            act.wait_ge(dve_prep, marks["arg"])
            act.activation(edge[:, 0:J * H], edge[:, 0:J * H], ACT.Exp).then_inc(w_exp, 1)

            def make_onehots(a):
                per = 2 // a["cut"].chunks

                def pair(s):
                    n = s.k
                    if s.past(1):
                        act.wait_ge(a["onehot_set"], n)
                    for c in range(2):
                        act.activation(dist[:, c, :], iota[:, :], ACT.Abs,
                                       bias=a["ndrel"][:, ds(n * 2 + c, 1)]).then_inc(a["dist_set"], 1)
                    act.wait_ge(a["dist_set"], 2 * n + 2)
                    if s.past(2):
                        act.wait_ge(a["step_sum"], per * (n - 1))
                    act.activation(onehot[:, s.j % 2, :, :], dist[:, :, :], ACT.Relu,
                                   bias=ones[:, 0:1], scale=-1.0).then_inc(a["onehot_set"], 1)
                pipelined(act, a["cut"].steps // per, 4, 0, pair)

            act.wait_ge(dve_prep, marks["tables"])
            make_onehots(agg[0])

            def table_out(m, s, lag):
                if s.live(lag):
                    t, par = s.k - lag, (s.j - lag) % 2
                    act.wait_ge(m["summed"], t + 1)
                    if s.past(2, lag):
                        act.wait_ge(m["seeded"], t - 1)
                        act.wait_ge(m["kept"][par], slot_total(t - 2, par))
                    act.activation(rows[:, 6 + par, :], mm[par][:, :], ACT.Copy).then_inc(m["tab_set"], 1)

            def residual(s):
                if s.live(2):
                    t, par = s.k - 2, s.j
                    act.wait_ge(x1_var, t + 1)
                    act.activation(std[:, par:par + 1], mv[:, par, 1:2], ACT.Sqrt, bias=epsc[:, 0:1]).then_inc(x1_std, 1)
                if s.live(3):
                    t, par = s.k - 3, (s.j - 3) % 2
                    act.wait_ge(x1_nmr, t + 1)
                    if s.past(2, 3):
                        act.wait_ge(mids[0]["turned"], t - 1)
                    act.activation(rows[:, 2 + par, :], acc(t), ACT.Relu,
                                   bias=nmr[:, par:par + 1], scale=rstd[:, par:par + 1]).then_inc(mids[0]["h_set"], 1)
                table_out(mids[0], s, 5)
            pipelined(act, TILES, 2, 5, residual)

            make_onehots(agg[1])

            def between(s):
                if s.live(1):
                    t, par = s.k - 1, (s.j - 1) % 2
                    act.wait_ge(mids[1]["y_set"], t + 1)
                    if s.past(2, 1):
                        act.wait_ge(mids[1]["turned"], t - 1)
                    act.activation(rows[:, 2 + par, :], acc(t), ACT.Relu,
                                   scale=dinv[:, ds(t, 1)]).then_inc(mids[1]["h_set"], 1)
                table_out(mids[1], s, 3)
            pipelined(act, TILES, 2, 3, between)
            make_onehots(agg[2])

        @block.tensor
        def _(pe):
            pe.wait_ge(ident_set, 2)
            pe.wait_ge(dve_prep, marks["groups1"])
            for n, c in enumerate((GAT, GCN)):
                for v in range(2):
                    for g in range(c.blocks):
                        last = pe.matmul(sm[0][:, v * c.blocks + g:v * c.blocks + g + 1], g_row[n][:, v, g * P:(g + 1) * P],
                                         ones[0:1, 0:1], start=True, stop=True)
                last.then_inc(pe_prep, 1)
                pe.wait_ge(dve_prep, marks[f"from{n}"])
                for b in range(c.blocks):
                    for g in range(c.blocks):
                        last = pe.matmul(sm[1][:, 2 * b:2 * b + 2], g_from[n][:, g, b * P:(b + 1) * P], g_val[n][:, g, :],
                                         start=(g == 0), stop=(g == c.blocks - 1))
                last.then_inc(pe_prep, 1)
                pe.wait_ge(dve_prep, marks[f"slots{n}"])
                for b in range(c.blocks):
                    last = pe.matmul(mm[b // BANKS][0:1, b % BANKS * P:(b % BANKS + 1) * P],
                                     stepcols[n][:, 5, b:b + 1], ident[:, :], start=True, stop=True)
                last.then_inc(pe_prep, 1)
            pe.wait_ge(dve_prep, marks["slots_out1"])
            pe.wait_ge(folded, 10)
            pe.wait_ge(wval_in, 16)

            def turn(bank, slot, done):
                for k in range(KC):
                    last = nc.tensor.transpose(bank[:, k * P:(k + 1) * P], rows[:, slot, k * P:(k + 1) * P], ident[:, :])
                last.then_inc(done, 1)

            def product(bank, slot, rhs, done):
                for k in range(KC):
                    last = nc.tensor.matmul(bank, rows[:, slot, k * P:(k + 1) * P], rhs(k), start=(k == 0), stop=(k == KC - 1))
                last.then_inc(done, 1)

            def first_layer(s):
                if s.live():
                    t, par = s.k, s.j
                    pe.wait_ge(h_set, t + 1)
                    if s.past(2):
                        pe.wait_ge(hT_set, t - 1)
                    turn(tr[par], 2 + par, h_turned)
                if s.live(1):
                    t, par = s.k - 1, (s.j - 1) % 2
                    pe.wait_ge(hT_set, t + 1)
                    if s.past(2, 1):
                        pe.wait_ge(eler_set, t - 1)
                        pe.wait_ge(v_set, t - 1)
                    for k in range(KC):
                        hT = rows[:, 4 + par, k * P:(k + 1) * P]
                        v_last = pe.matmul(mm[par][:, :], hT, wmat[:, k, :], start=(k == 0), stop=(k == KC - 1))
                        if k == KC - 1:
                            v_last.then_inc(v_sum, 1)
                        last = pe.matmul(sm[par][:, 0:2 * H], hT, wlr[:, k, :], start=(k == 0), stop=(k == KC - 1))
                    last.then_inc(eler_sum, 1)
                if s.inner or s.k < HB:
                    b, par = s.k, s.j
                    pe.wait_ge(hot_set, 2 * b + 2)
                    for j in range(JB):
                        last = pe.matmul(hist_ps[:, 0:TILES], hot_low[:, par, j, :], hot_blk[:, par, j, :],
                                         start=(not s.inner and b == 0 and j == 0),
                                         stop=(not s.inner and b == HB - 1 and j == JB - 1))
                    last.then_inc(hot_used, 1)
            pipelined(pe, TILES, 2, 1, first_layer, tail=4)

            pe.wait_ge(dve_prep, marks["hist"])
            pe.matmul(misc[:, 0:TILES], ones[:, :], hist[:, :], start=True, stop=True)
            pe.matmul(sm[0][:, 0:TILES], tri[:, :], hist[:, :], start=True, stop=True).then_inc(pe_prep, 1)

            pe.wait_ge(dve_prep, marks["low"])
            for b in range(-(-PCOLS // P)):
                n = min(P, PCOLS - b * P)
                last = pe.transpose(misc[0:n, b * P:(b + 1) * P], low_f[:, b * P:b * P + n], ident[:, :])
            last.then_inc(pe_prep, 1)

            i = 0
            for c in (GAT, GCN):
                for b in range(c.blocks):
                    pe.wait_ge(dve_prep, marks[f"block{i}"])
                    for s in range(2):
                        for h in range(c.chunks):
                            last = pe.transpose(tr[i % 2][:, (c.chunks * s + h) * P:(c.chunks * s + h + 1) * P],
                                                b_f[:, i % 2, s, h * P:(h + 1) * P], ident[:, :])
                    last.then_inc(pe_prep, 1)
                    i += 1

            def pick(s):
                g, par = s.k, s.j
                pe.wait_ge(src_hot_set, (g + 1) * KT)
                if s.past(2):
                    pe.wait_ge(el_picked, g - 1)
                for q in range(Q):
                    for kt in range(KT):
                        for part in range(3):
                            last = pe.matmul(mm[par][:, q * NA * H:(q + 1) * NA * H], src_hot[:, par, kt, q * P:(q + 1) * P],
                                             el_parts[:, part, kt::KT, :], start=(kt == 0 and part == 0),
                                             stop=(kt == KT - 1 and part == 2))
                last.then_inc(el_summed, 1)
            pipelined(pe, PCOLS // Q, 2, 0, pick)

            for n in range(3):
                pe.wait_ge(dve_prep, marks["ends"][n])
                for i in range(2):
                    last = pe.transpose(misc[0:H, i * P:(i + 1) * P], tail_st[:, i, :], ident[:, :])
                last.then_inc(pe_prep, 1)
                pe.wait_ge(dve_prep, marks["carried"][n])
                lo = 1 if n == 2 else 0
                pe.transpose(sm[1][:, 0:H], carry_row[:, 2, lo:lo + P], ident[0:H, 0:H]).then_inc(pe_prep, 1)

            for b in range(GAT.blocks):
                pe.wait_ge(w_in[b], 16)
                halves = w_rows[:, b % 2, :].rearrange("p (c e h) -> p c h e", c=2, h=H)
                for q in range(4):
                    i = 4 * b + q
                    if i >= 2:
                        pe.wait_ge(w_placed, i - 1)
                    for n in range(4):
                        c, h = divmod(4 * q + n, H)
                        last = pe.transpose(tr[i % 2][:, n * P:(n + 1) * P], halves[:, c, h, :], ident[:, :])
                    last.then_inc(w_turned, 1)

            def aggregate(a, weighted):
                c = a["cut"]
                per = 2 if weighted else 1

                def step(s):
                    w, u, bank = s.k, s.j % c.slots, s.j % BANKS
                    if weighted:
                        pe.wait_ge(a["onehot_set"], w + 1)
                        pe.wait_ge(a["msg_set"], w + 1)
                        hots = [onehot[:, s.j % 2, n, :] for n in range(2)]
                    else:
                        pe.wait_ge(a["onehot_set"], s.turn * (c.slots // 2) + (s.j // 2 + 1))
                        pe.wait_ge(a["rows_in"][u], (w - u) * 2 + 16)
                        hots = [onehot[:, s.j // 2 % 2, s.j % 2, :]]
                    if s.past(BANKS):
                        pe.wait_ge(a["acc_added"], per * (w - BANKS + 1))
                    if weighted:
                        for n, hot in enumerate(hots):
                            pe.matmul(den_ps[bank][:, 0:H], hot, w_step[:, w, n * H:(n + 1) * H],
                                      start=(n == 0), stop=(n == c.chunks - 1))
                    for n, hot in enumerate(hots):
                        last = pe.matmul(sum_ps[bank][:, :], hot, rows[:, c.chunks * u + n, :],
                                         start=(n == 0), stop=(n == c.chunks - 1))
                    last.then_inc(a["step_sum"], 1)
                pipelined(pe, c.steps, 8, 0, step)

            pe.wait_ge(w_placed, 4 * GAT.blocks)
            aggregate(agg[0], True)

            def dense_layer(m, lag):
                pe.wait_ge(m["w_in"], 16)

                def step(s):
                    if s.live(lag):
                        t, par = s.k - lag, (s.j - lag) % 2
                        pe.wait_ge(m["h_set"], t + 1)
                        if s.past(2, lag):
                            pe.wait_ge(m["hT_set"], t - 1)
                        turn(tr[par], 2 + par, m["turned"])
                    if s.live(lag + 1):
                        t, par = s.k - lag - 1, (s.j - lag - 1) % 2
                        pe.wait_ge(m["hT_set"], t + 1)
                        if s.past(2, lag + 1):
                            pe.wait_ge(m["tab_set"], t - 1)
                        product(mm[par][:, :], 4 + par, lambda k: wmat[:, k, :], m["summed"])
                pipelined(pe, TILES, 2, lag + 1, step)
            dense_layer(mids[0], 0)
            aggregate(agg[1], False)
            dense_layer(mids[1], 0)
            aggregate(agg[2], False)


_INS = ["x", "src", "dst", "L0_gnn_W_src", "L0_gnn_b_src", "L0_gnn_W_dst", "L0_gnn_b_dst", "L0_gnn_W_val", "L0_gnn_b_val",
        "L0_gnn_attn_l", "L0_gnn_attn_r", "L1_gnn_W1", "L1_gnn_b1", "L1_gnn_W2", "L1_gnn_b2"]


def kernel(**inputs):
    import concourse.bacc as bacc
    from concourse.bass_utils import run_bass_kernel_spmd as run

    nc = bacc.Bacc("TRN2", target_bir_lowering=False, num_devices=1)
    arrays, args = {}, []
    for name in _INS:
        a = np.ascontiguousarray(inputs[name])
        arrays[name] = a
        args.append(nc.dram_tensor(name, a.shape, mybir.dt.from_np(a.dtype), kind="ExternalInput").ap())
    out = nc.dram_tensor("out", [N, D], F32, kind="ExternalOutput").ap()
    build(nc, *args, out)
    return run(nc, [arrays], core_ids=[0]).results[0]["out"]
```

```python
import numpy as np
import concourse.bass as bass
from concourse import mybir
from contextlib import ExitStack

F32 = mybir.dt.float32
BF16 = mybir.dt.bfloat16
F16 = mybir.dt.float16
I32 = mybir.dt.int32
ALU = mybir.AluOpType
ACT = mybir.ActivationFunctionType
AX = mybir.AxisListType
ds = bass.ds

P = 128
N, E, D, H = 6250, 100000, 512, 8
F = D // H
KC = D // P
TILES = -(-N // P)
NP = TILES * P
LAST = N - (TILES - 1) * P
J = -(-E // P)
EP = J * P
SLOTS = 8
BANKS = 4
HALF = D // 2 + H
AW = D + H


class Cut:

    def __init__(self, chunks):
        self.chunks = chunks
        self.edges = chunks * P
        self.groups = EP // self.edges
        self.slots = SLOTS // chunks
        unroll = 2 * self.slots
        self.steps = -(-(self.groups + TILES - 1) // unroll) * unroll
        self.blocks = -(-self.steps // P)


GAT, GCN = Cut(2), Cut(1)
GE = GAT.edges
GROUPS = GAT.groups
SP = GAT.steps
XL = 8
OS = 8
EARLY_X1 = 2 * J * H // D // XL * XL
IDX = 16
LAG = 2
JB = 17
HB = J // JB
EB = 13
EL_BATCHES = 18
J0 = EL_BATCHES * EB
PCOLS = J - J0
PB = -(-PCOLS // P)
Q = 4
KT = 4
NA = -(-TILES // KT)
EARLY = 4
SB = 7
BIG = 1e38
EPS = 1e-5
SLOPE = 0.2


class Step:

    def __init__(self, k, j, count, inner, turn=None):
        self.k, self.j, self.count, self.inner, self.turn = k, j, count, inner, turn

    def live(self, lag=0):
        return self.inner or 0 <= self.k - lag < self.count

    def past(self, n, lag=0):
        return self.inner or self.k - lag >= n


def pipelined(eng, count, unroll, lag, body, tail=0):
    lo = -(-(lag + unroll) // unroll) * unroll
    hi = lo + (count - tail - lo) // unroll * unroll
    for k in range(lo):
        body(Step(k, k % unroll, count, False, k // unroll))
    with eng.Fori(0, (hi - lo) // unroll) as i:
        for j in range(unroll):
            body(Step(i * unroll + (lo + j), j, count, True, i + lo // unroll))
    for k in range(hi, count + lag):
        body(Step(k, k % unroll, count, False, k // unroll))


def build(nc, x, src, dst, W_src, b_src, W_dst, b_dst, W_val, b_val, attn_l, attn_r, W1, b1, W2, b2, out):
    ctx = ExitStack()
    with ctx:
        def sb(name, shape, dt=F32):
            return ctx.enter_context(nc.sbuf_tensor(name, shape, dt))

        def ps(name, shape):
            return ctx.enter_context(nc.psum_tensor(name, shape, F32))

        def sem(name):
            return ctx.enter_context(nc.semaphore(name))

        def dram(name, shape, dt=F32):
            return nc.dram_tensor(name, shape, dt, kind="Internal").ap()

        src_rows = dram("src_rows", [GROUPS, GE], I32)
        dst_rows = dram("dst_rows", [GROUPS, GE], I32)
        el_tab = dram("el_tab", [NP, H])
        er_tab = dram("er_tab", [EP + NP, H])
        w_tab = dram("w_tab", [GROUPS, GE * H])
        low_tab = dram("low_tab", [PB * P, P], F16)
        v_tab = dram("v_tab", [NP, D])
        x1_tab = dram("x1_tab", [NP, D])
        h2_tab = dram("h2_tab", [NP, D])
        h3_tab = dram("h3_tab", [NP, D])

        big = sb("big", [P, TILES * AW])
        edge = sb("edge", [P, 2 * J * H])
        rows_w = sb("rows_w", [P, SLOTS, AW])
        wmat = sb("wmat", [P, KC, D + 2 * H])
        bias = sb("bias", [P, D])
        ident = sb("ident", [P, P])
        ones = sb("ones", [P, P])
        tri = sb("tri", [P, P])
        iota = sb("iota", [P, P])
        node_i = sb("node_i", [P, TILES], I32)
        low_i4 = sb("low_i4", [P, KT], I32)
        low_id = sb("low_id", [P, KT])
        step_i = sb("step_i", [P, GCN.blocks], I32)
        stepf = sb("stepf", [P, GCN.blocks])
        gidx = [sb(f"gidx{c.chunks}", [P, c.blocks], I32) for c in (GAT, GCN)]
        tile0 = [sb(f"tile0_{c.chunks}", [P, c.blocks]) for c in (GAT, GCN)]
        pad_i = sb("pad_i", [1, 2, EP - E], I32)
        blr = sb("blr", [P, 2 * H])
        x1_stats = sb("x1_stats", [P, 2, 6])
        mv = sb("mv", [P, 2, 2])
        std = sb("std", [P, 2])
        rstd = sb("rstd", [P, 2])
        nmr = sb("nmr", [P, 2])
        epsc = sb("epsc", [P, 1])
        twoc = sb("twoc", [P, 1])
        eler_hots = sb("eler_hots", [P, TILES * 2 * H])
        src_flat = sb("src_flat", [P, J], I32)
        src_step = [sb(f"src_step{c.chunks}", [P, c.steps * c.chunks], I32) for c in (GAT, GCN)]
        ndrel = [sb(f"ndrel{c.chunks}", [P, c.steps * c.chunks]) for c in (GAT, GCN)]
        slot_i = [sb(f"slot_i{c.chunks}", [1, 8 + c.blocks * P], I32) for c in (GAT, GCN)]
        hist = sb("hist", [P, TILES])
        dinv = sb("dinv", [P, TILES])
        ind = sb("ind", [P, TILES])
        small = sb("small", [P, 8, TILES])
        er_idx = sb("er_idx", [P, TILES], I32)
        el_idx = sb("el_idx", [P, 2, EB], I32)
        el_rows = sb("el_rows", [P, 2, EB * H])
        sc_rows = sb("sc_rows", [P, SB, H])
        sc_idx = sb("sc_idx", [P, SB], I32)
        row_idx = sb("row_idx", [P, 2, IDX], I32)
        edgecols_i = sb("edgecols_i", [P, 2], I32)
        edgecols = sb("edgecols", [P, 2])
        stepcols = [sb(f"stepcols{c.chunks}", [P, 6, c.blocks]) for c in (GAT, GCN)]
        tail_st = sb("tail_st", [P, 2, H])
        carry = sb("carry", [P, H])

        el = edge[:, 0:J * H].rearrange("p (j h) -> p j h", h=H)
        top = edge[:, J * H:2 * J * H].rearrange("p (j h) -> p j h", h=H)
        w_step = edge[:, 0:SP * 2 * H].rearrange("p (w q) -> p w q", q=2 * H)
        w_rows = edge[:, SP * 2 * H:SP * 2 * H + 2 * GE * H].rearrange("p (b n) -> p b n", b=2)
        rden = edge[:, SP * 2 * H + 2 * GE * H:SP * 2 * H + 2 * GE * H + TILES * H].rearrange("p (t h) -> p t h", h=H)
        eler = eler_hots[:, :].rearrange("p (t q) -> p t q", q=2 * H)
        onehot = eler_hots[:, 0:4 * P].rearrange("p (b c n) -> p b c n", b=2, c=2)
        dist = eler_hots[:, 4 * P:6 * P].rearrange("p (c n) -> p c n", c=2)
        stat = big[:, TILES * D:TILES * (D + 6)].rearrange("p (t s) -> p t s", s=6)
        ln = small[:, 0:4, :]
        iota_i = small[:, 4:7, :].rearrange("p s t -> p (s t)")[:, 0:P].bitcast(I32)
        W_src_sb = wmat[:, :, 0:D]
        rows = rows_w[:, :, 0:D]
        W_dst_sb = rows[:, 0:KC, :]
        attn_sb = rows[:, KC:KC + 2, :]
        bsd_sb = rows[:, KC + 2:KC + 4, :]

        class Region:

            def __init__(self, ap):
                self.ap, self.at = ap, 0

            def __call__(self, n):
                self.at += n
                assert self.at <= self.ap.shape[1]
                return self.ap[:, self.at - n:self.at]

        part = Region(edge[:, :])
        fold = part(KC * D).rearrange("p (k n) -> p k n", k=KC)
        bfold = part(2 * D).rearrange("p (s n) -> p s n", s=2)
        g_i = [[src_step[1][0:1, 0:GAT.groups], src_step[1][0:1, GAT.groups:2 * GAT.groups]],
               [src_step[0][0:1, 0:GCN.groups], ndrel[0][0:1, 0:GCN.groups].bitcast(I32)]]
        g_row = [part(2 * c.blocks * P)[0:1, :].rearrange("p (s g) -> p s g", s=2) for c in (GAT, GCN)]
        assert part.at <= J * H
        flat_rows = rows_w[:, :, :].rearrange("p s n -> p (s n)")
        step_of = flat_rows[:, 0:GCN.blocks * P].bitcast(I32)
        g_from = [a.bitcast(BF16).rearrange("p (g n) -> p g n", n=c.blocks * P) for a, c in (
            (edge[:, 0:GAT.blocks ** 2 * P // 2], GAT),
            (flat_rows[:, GCN.blocks * P:GCN.blocks * P + GCN.blocks ** 2 * P // 2], GCN))]
        g_first = [a[:, 2, :] for a in stepcols]
        g_val = [a[:, 3, :].bitcast(BF16).rearrange("p (g v) -> p g v", v=2) for a in stepcols]
        part = Region(edge[:, J * H:2 * J * H])
        dst_i = part(J).bitcast(I32)
        blk_i = part(J).bitcast(I32)
        blk_f = part(J)
        low_i = part(J).bitcast(I32)
        low_f = part(J)
        hot_flat = part(JB * P).bitcast(BF16)
        hot_low = hot_flat.rearrange("p (b j n) -> p b j n", b=2, j=JB)
        src_hot = hot_flat[:, 0:2 * KT * Q * P].rearrange("p (b k n) -> p b k n", b=2, k=KT)
        part = Region(rows_w[:, 2:6, :].rearrange("p s n -> p (s n)"))
        b_f = part(2 * 2 * GE).rearrange("p (b s e) -> p b s e", b=2, s=2)
        part = Region(rows_w[:, 6:8, :].rearrange("p s n -> p (s n)"))
        hot_blk = part(JB * TILES).bitcast(BF16).rearrange("p (b j n) -> p b j n", b=2, j=JB)
        part = Region(rows_w[:, 2:6, :].rearrange("p s n -> p (s n)"))
        low_all = part(4 * Q * P // 2).bitcast(F16).rearrange("p (b n) -> p b n", b=4)
        picked = part(2 * Q * NA * H).rearrange("p (b q a h) -> p b q a h", b=2, q=Q, h=H)
        a_hot = part(2 * Q * NA).rearrange("p (b q a) -> p b q a", b=2, q=Q)
        part = Region(big[:, :])
        er = part(J * H).rearrange("p (j h) -> p j h", h=H)
        dst_f = part(J)
        cont = part(J + 1)
        pen = part(J + 1)
        carry_row = part(3 * (P + 1))[0:H, :].rearrange("p (s n) -> p s n", s=3)
        scanned = part.at
        halves = [slice(half * (J // 2), (half + 1) * (J // 2)) for half in range(2)]
        b_i = [part(c.blocks * 2 * c.edges).bitcast(I32).rearrange("p (b s e) -> p b s e", b=c.blocks, s=2)
               for c in (GAT, GCN)]
        el_parts = part(3 * NA * KT * H // 2).bitcast(BF16).rearrange("p (s t h) -> p s t h", s=3, h=H)
        el_rest = part(TILES * H).rearrange("p (t h) -> p t h", h=H)
        low_T = part(PB * P // 2).bitcast(F16).rearrange("p (b n) -> p b n", n=P)

        def acc(t):
            return big[:, ds(t * AW, D)]

        def first(t):
            return big[:, ds(t * D, D)]

        mm = [ps("mm0", [P, D]), ps("mm1", [P, D])]
        tr = [ps("tr0", [P, D]), ps("tr1", [P, D])]
        sm = [ps("sm0", [P, D]), ps("sm1", [P, D])]
        hist_ps = ps("hist_ps", [P, D])
        misc = ps("misc", [P, D])
        sum_ps, half_ps = mm + tr, sm + [hist_ps, misc]

        pad_set, const_set, ident_set, edges_kept, fold_in, edges_in, dst_in = map(sem, (
            "pad_set", "const_set", "ident_set", "edges_kept", "fold_in", "edges_in", "dst_in"))
        firsts_in = [sem("firsts_in0"), sem("firsts_in1")]
        borders_in, bval_in = sem("borders_in"), sem("bval_in")
        dve_setup, folded = sem("dve_setup"), sem("folded")
        x_in = [sem(f"x_in{c}") for c in range(TILES // XL + 1)]
        stat_set, ln_set, std_set, h_set, h_turned, hT_set, eler_set = map(sem, (
            "stat_set", "ln_set", "std_set", "h_set", "h_turned", "hT_set", "eler_set"))
        el_kept, er_zeroed, wval_in, v_sum, v_set, step_of_set = map(sem, (
            "el_kept", "er_zeroed", "wval_in", "v_sum", "v_set", "step_of_set"))
        v_kept = [sem("v_kept0"), sem("v_kept1")]
        el_in = [sem("el_in0"), sem("el_in1")]
        srcdst_in = [sem("srcdst_in0"), sem("srcdst_in1")]
        er_scattered, er_in, w_kept, el_idx_set, sc_idx_set = map(sem, (
            "er_scattered", "er_in", "w_kept", "el_idx_set", "sc_idx_set"))
        el_placed = sem("el_placed")
        w_in = [sem(f"w_in{k}") for k in range(GAT.blocks)]
        dve_prep, pe_prep, hot_set, hot_used, std_deg, er_idx_set, w_exp = map(sem, (
            "dve_prep", "pe_prep", "hot_set", "hot_used", "std_deg", "er_idx_set", "w_exp"))
        w_turned, w_placed, e_set, big_zeroed = map(sem, ("w_turned", "w_placed", "e_set", "big_zeroed"))
        low_kept, src_hot_set, el_summed, a_hot_set, el_masked, el_picked = map(sem, (
            "low_kept", "src_hot_set", "el_summed", "a_hot_set", "el_masked", "el_picked"))
        low_in = [sem(f"low_in{b}") for b in range(4)]
        agg = []
        for n, c in (("gat", 0), ("gcn1", 1), ("gcn2", 1)):
            agg.append(dict(
                cut=(GAT, GCN)[c], src=src_step[c], ndrel=ndrel[c], slot=slot_i[c],
                rows_in=[sem(f"{n}_rows_in{u}") for u in range((GAT, GCN)[c].slots)],
                idx_set=sem(f"{n}_idx_set"), dist_set=sem(f"{n}_dist_set"), onehot_set=sem(f"{n}_onehot_set"),
                msg_set=sem(f"{n}_msg_set"), step_sum=sem(f"{n}_step_sum"), acc_added=sem(f"{n}_acc_added")))
        xb_set = sem("xb_set")
        rden_set, xr_scaled, x1_set, x1_stat, x1_var, x1_std, x1_rstd, x1_nmr = map(sem, (
            "rden_set", "xr_scaled", "x1_set", "x1_stat", "x1_var", "x1_std", "x1_rstd", "x1_nmr"))
        xr_in = [sem("xr_in0"), sem("xr_in1")]
        x1_kept = [sem("x1_kept0"), sem("x1_kept1")]
        mids = []
        for n in ("gcn1", "gcn2"):
            mids.append(dict(
                w_in=sem(f"{n}_w_in"), y_set=sem(f"{n}_y_set"), h_set=sem(f"{n}_h_set"), turned=sem(f"{n}_turned"),
                hT_set=sem(f"{n}_hT_set"), summed=sem(f"{n}_summed"), tab_set=sem(f"{n}_tab_set"),
                seeded=sem(f"{n}_seeded"), kept=[sem(f"{n}_kept0"), sem(f"{n}_kept1")]))
        b_in = [sem("b1_in"), sem("b2_in")]
        y_set, out_set = sem("y_set"), sem("out_set")
        x1_in = [sem(f"x1_in{n}") for n in range(OS)]
        x1_early_in, out_kept = sem("x1_early_in"), sem("out_kept")

        def slot_total(t, par, per=16):
            return (t - par) * (per // 2) + per

        def all_kept(eng, pair, per=16):
            eng.wait_ge(pair[0], per * ((TILES + 1) // 2))
            eng.wait_ge(pair[1], per * (TILES // 2))

        waits_passed = {eng: sem(f"waits_passed_{eng}") for eng in ("pool", "dve")}

        def wait_alone(name, eng, which, value):
            eng.wait_ge(which, value)
            eng.sem_inc(waits_passed[name], 1)

        def on_all(vec):
            return vec.rearrange("(a n) -> a n", a=1).broadcast_to([P, D])

        block = ctx.enter_context(nc.Block())

        prep, pe_steps = [0], [0]
        marks = {}

        @block.vector
        def _(dve):
            def did(ins):
                prep[0] += 1
                ins.then_inc(dve_prep, 1)
                dve.wait_ge(dve_prep, prep[0])

            def issue(ins):
                prep[0] += 1
                ins.then_inc(dve_prep, 1)

            def settle():
                dve.wait_ge(dve_prep, prep[0])

            def turned():
                pe_steps[0] += 1
                dve.wait_ge(pe_prep, pe_steps[0])

            dve.wait_ge(const_set, 9)
            did(dve.tensor_copy(iota[:, :], iota_i[:, :]))
            did(dve.tensor_copy(stepf[:, :], step_i[:, :]))
            did(dve.tensor_copy(low_id[:, :], low_i4[:, :]))

            for n, c in enumerate((GAT, GCN)):
                dve.wait_ge(firsts_in[n], 32)
                G = c.groups
                (first_i, last_i), row = g_i[n], g_row[n]
                counted, summed = first_i.bitcast(F32), last_i.bitcast(F32)
                did(dve.memset(row[:, 0, :], 1e6))
                did(dve.memset(row[:, 1, :], 0.0))
                did(dve.tensor_scalar(first_i, first_i, 7, None, ALU.arith_shift_right))
                did(dve.tensor_scalar(last_i, last_i, 7, None, ALU.arith_shift_right))
                did(dve.tensor_copy(row[:, 1, 0:G], first_i))
                did(dve.tensor_copy(row[:, 0, 0:G], last_i))
                did(dve.scalar_tensor_tensor(counted, row[:, 0, 0:G], 1.0, row[:, 1, 0:G], ALU.add, ALU.subtract))
                did(dve.tensor_tensor_scan(summed, ones[0:1, 0:1].to_broadcast([1, G]), counted, 0.0, ALU.mult, ALU.add))
                did(dve.tensor_tensor(row[:, 0, 0:G], summed, counted, ALU.subtract))
                did(dve.tensor_tensor(summed, row[:, 1, 0:G], row[:, 0, 0:G], ALU.subtract))
                did(dve.tensor_copy(row[:, 1, 0:1], summed[:, 0:1]))
                did(dve.tensor_tensor(row[:, 1, 1:G], summed[:, 1:G], summed[:, 0:G - 1], ALU.subtract))
                marks[f"groups{n}"] = prep[0]

            dve.wait_ge(fold_in, 96)
            for s, w in enumerate((W_src_sb, W_dst_sb)):
                if s:
                    dve.wait_ge(folded, 5)
                dve.tensor_tensor(fold, w[:, :, :], attn_sb[:, s, :].unsqueeze(1).to_broadcast([P, KC, D]),
                                  ALU.mult).then_inc(dve_setup, 1)
                dve.tensor_tensor(bfold[:, s, :], bsd_sb[:, s, :], attn_sb[:, s, :], ALU.mult).then_inc(dve_setup, 1)
                dve.wait_ge(dve_setup, 2 * s + 2)
                for k in range(KC):
                    dve.tensor_reduce(wmat[:, k, D + s * H:D + (s + 1) * H], fold[:, k, :].rearrange("p (h f) -> p h f", f=F),
                                      AX.X, ALU.add).then_inc(folded, 1)
                dve.tensor_reduce(blr[:, s * H:(s + 1) * H], bfold[:, s, :].rearrange("p (h f) -> p h f", f=F),
                                  AX.X, ALU.add).then_inc(folded, 1)
            dve.wait_ge(folded, 10)

            dve.wait_ge(step_of_set, 1)
            for n, c in enumerate((GAT, GCN)):
                turned()
                did(dve.memset(g_val[n], 1.0))
                did(dve.tensor_copy(g_first[n], sm[0][:, 0:c.blocks]))
                did(dve.tensor_copy(g_val[n][:, :, 1], sm[0][:, c.blocks:2 * c.blocks]))
                for g in range(c.blocks):
                    did(dve.tensor_scalar(g_from[n][:, g, :], step_of[:, 0:c.blocks * P], g_first[n][:, g:g + 1], None, ALU.is_ge))
                marks[f"from{n}"] = prep[0]
                turned()
                cols = stepcols[n][:, :, :]
                did(dve.tensor_copy(cols[:, 0:2, :], sm[1][:, 0:2 * c.blocks].rearrange("p (b v) -> p v b", v=2)))
                did(dve.tensor_scalar(gidx[n][:, :], cols[:, 0, :], -1.0, None, ALU.add))
                marks[f"gidx{n}"] = prep[0]
                did(dve.tensor_tensor(cols[:, 4, :], cols[:, 1, :], stepf[:, 0:c.blocks], ALU.add))
                did(dve.tensor_scalar(tile0[n][:, :], cols[:, 4, :], float(P), None, ALU.mult))
                did(dve.tensor_scalar(cols[:, 5, :], cols[:, 4, :], float(TILES - 1), float(AW), ALU.min, ALU.mult))
                marks[f"slots{n}"] = prep[0]
                turned()
                did(dve.memset(slot_i[n][0:1, 0:LAG], 0))
                for lo in range(0, c.blocks * P, D):
                    hi = min(lo + D, c.blocks * P)
                    did(dve.tensor_copy(slot_i[n][0:1, LAG + lo:LAG + hi], mm[lo // D][0:1, 0:hi - lo]))
                marks[f"slots_out{n}"] = prep[0]

            for c in range(TILES // XL):
                dve.wait_ge(x_in[c], 16)
                with dve.Fori(0, 2) as i:
                    for n in range(XL // 2):
                        t = i * (XL // 2) + (c * XL + n)
                        dve.bn_stats(stat[:, t, :], first(t)).then_inc(stat_set, 1)
            dve.wait_ge(x_in[TILES // XL], 16)
            dve.bn_stats(stat[:, TILES - 1, :], first(TILES - 1)).then_inc(stat_set, 1)
            dve.wait_ge(stat_set, TILES)
            dve.tensor_tensor(ln[:, 0, :], stat[:, :, 1], stat[:, :, 4], ALU.add).then_inc(ln_set, 1)
            dve.tensor_tensor(ln[:, 1, :], stat[:, :, 1], stat[:, :, 4], ALU.subtract).then_inc(ln_set, 1)
            dve.tensor_tensor(ln[:, 2, :], stat[:, :, 2], stat[:, :, 5], ALU.add).then_inc(ln_set, 1)
            dve.wait_ge(ln_set, 3)
            dve.tensor_tensor(ln[:, 3, :], ln[:, 1, :], ln[:, 1, :], ALU.mult).then_inc(ln_set, 1)
            dve.tensor_scalar(ln[:, 0, :], ln[:, 0, :], 0.5, None, ALU.mult).then_inc(ln_set, 1)
            dve.tensor_scalar(ln[:, 2, :], ln[:, 2, :], 1.0 / D, None, ALU.mult).then_inc(ln_set, 1)
            dve.wait_ge(ln_set, 6)
            dve.scalar_tensor_tensor(ln[:, 1, :], ln[:, 3, :], 0.25, ln[:, 2, :], ALU.mult, ALU.add).then_inc(ln_set, 1)
            dve.wait_ge(std_set, 1)
            dve.reciprocal(ln[:, 2, :], ln[:, 3, :]).then_inc(ln_set, 1)
            dve.wait_ge(ln_set, 8)
            dve.scalar_tensor_tensor(ln[:, 1, :], ln[:, 0, :], -1.0, ln[:, 2, :], ALU.mult, ALU.mult).then_inc(ln_set, 1)

            dve.wait_ge(dst_in, 16)
            did(dve.tensor_scalar(blk_i, dst_i, 7, None, ALU.arith_shift_right))
            did(dve.tensor_scalar(low_i, dst_i, P - 1, None, ALU.bitwise_and))
            did(dve.tensor_copy(blk_f, blk_i))
            did(dve.tensor_copy(low_f, low_i))

            def first_layer(s):
                if s.live():
                    t, par = s.k, s.j
                    dve.wait_ge(h_turned, t + 1)
                    if s.past(2):
                        dve.wait_ge(v_sum, t - 1)
                    dve.tensor_copy(rows[:, 4 + par, :], tr[par][:, :]).then_inc(hT_set, 1)
                    if s.inner or t < HB:
                        b = t
                        if s.past(2):
                            dve.wait_ge(hot_used, b - 1)
                        dve.tensor_tensor(hot_low[:, par, :, :],
                                          low_f[:, ds(b * JB, JB)].unsqueeze(2).to_broadcast([P, JB, P]),
                                          iota[:, :].unsqueeze(1).to_broadcast([P, JB, P]), ALU.is_equal).then_inc(hot_set, 1)
                        dve.tensor_tensor(hot_blk[:, par, :, :],
                                          blk_f[:, ds(b * JB, JB)].unsqueeze(2).to_broadcast([P, JB, TILES]),
                                          iota[:, 0:TILES].unsqueeze(1).to_broadcast([P, JB, TILES]),
                                          ALU.is_equal).then_inc(hot_set, 1)
                if s.live(2):
                    t, par = s.k - 2, s.j
                    dve.wait_ge(v_set, 2 * t + 2)
                    dve.tensor_tensor(eler[:, t, :], sm[par][:, HALF - 2 * H:HALF], blr[:, :], ALU.add).then_inc(eler_set, 1)
            pipelined(dve, TILES, 2, 2, first_layer, tail=4)

            dve.wait_ge(hot_used, HB)
            did(dve.tensor_copy(hist[:, :], hist_ps[:, 0:TILES]))
            marks["hist"] = prep[0]
            did(dve.tensor_copy(small[:, 0, :], node_i[:, :]))
            turned()
            did(dve.tensor_copy(small[:, 1, :], misc[:, 0:TILES]))
            did(dve.tensor_tensor_scan(small[:, 2, :], ones[:, 0:TILES], small[:, 1, :], 0.0, ALU.mult, ALU.add))
            did(dve.tensor_tensor(small[:, 3, :], small[:, 2, :], small[:, 1, :], ALU.subtract))
            did(dve.tensor_tensor(small[:, 4, :], small[:, 3, :], sm[0][:, 0:TILES], ALU.add))
            did(dve.tensor_tensor(small[:, 3, :], small[:, 4, :], small[:, 0, :], ALU.subtract))
            did(dve.scalar_tensor_tensor(small[:, 5, :], hist[:, :], 0.0, small[:, 3, :], ALU.is_gt, ALU.mult))
            dve.tensor_tensor(er_idx[:, :], small[:, 5, :], small[:, 0, :], ALU.add).then_inc(er_idx_set, 1)
            dve.wait_ge(std_deg, 1)
            did(dve.reciprocal(dinv[:, :], small[:, 6, :]))
            did(dve.tensor_scalar(ind[:, :], hist[:, :], 0.0, None, ALU.is_gt))

            dve.wait_ge(h_set, TILES)
            did(dve.memset(er.rearrange("p j h -> p (j h)"), 0.0))
            marks["er_zero"] = prep[0]
            did(dve.tensor_copy(dst_f, dst_i))

            did(dve.tensor_scalar(low_i[:, 0:PCOLS], src_flat[:, J0:J], KT * P - 1, None, ALU.bitwise_and))
            did(dve.tensor_scalar(blk_i[:, 0:PCOLS], src_flat[:, J0:J], 9, None, ALU.arith_shift_right))
            did(dve.tensor_copy(low_f[:, 0:PCOLS], low_i[:, 0:PCOLS]))
            did(dve.tensor_copy(blk_f[:, 0:PCOLS], blk_i[:, 0:PCOLS]))
            marks["low"] = prep[0]
            did(dve.memset(el_parts[:, :, TILES:, :], 0.0))
            did(dve.tensor_copy(el_parts[:, 0, 0:TILES, :], eler[:, :, 0:H]))
            did(dve.tensor_tensor(el_rest, eler[:, :, 0:H], el_parts[:, 0, 0:TILES, :], ALU.subtract))
            did(dve.tensor_copy(el_parts[:, 1, 0:TILES, :], el_rest))
            did(dve.tensor_tensor(el_rest, el_rest, el_parts[:, 1, 0:TILES, :], ALU.subtract))
            did(dve.tensor_copy(el_parts[:, 2, 0:TILES, :], el_rest))
            marks["parts"] = prep[0]
            turned()
            for b in range(0, PB, 4):
                n = min(4, PB - b)
                did(dve.tensor_copy(low_T[:, b:b + n, :], (misc, hist_ps)[b // 4][:, 0:n * P].rearrange("p (b n) -> p b n", n=P)))
            marks["low_T"] = prep[0]

            def pick(s):
                if s.live(2):
                    g, par = s.k - 2, s.j % 2
                    dve.tensor_tensor(a_hot[:, par, :, :], blk_f[:, ds(g * Q, Q)].unsqueeze(2).to_broadcast([P, Q, NA]),
                                      iota[:, 0:NA].unsqueeze(1).to_broadcast([P, Q, NA]), ALU.is_equal).then_inc(a_hot_set, 1)
                if s.live():
                    g, par = s.k, s.j % 2
                    dve.wait_ge(low_in[s.j], (g - s.j) * 4 + 16)
                    if s.past(2):
                        dve.wait_ge(el_summed, g - 1)
                    for kt in range(KT):
                        dve.tensor_scalar(src_hot[:, par, kt, :], low_all[:, s.j, :], low_id[:, kt:kt + 1], None,
                                          ALU.is_equal).then_inc(src_hot_set, 1)
                if s.live(2):
                    g, par = s.k - 2, s.j % 2
                    dve.wait_ge(a_hot_set, g + 1)
                    dve.wait_ge(el_summed, g + 1)
                    dve.tensor_tensor(picked[:, par, :, :, :],
                                      sum_ps[(s.j - 2) % 4][:, 0:Q * NA * H].rearrange("p (q a h) -> p q a h", q=Q, h=H),
                                      a_hot[:, par, :, :].unsqueeze(3).to_broadcast([P, Q, NA, H]),
                                      ALU.mult).then_inc(el_masked, 1)
                if s.live(3):
                    g, par = s.k - 3, (s.j - 3) % 2
                    dve.wait_ge(el_masked, g + 1)
                    dve.tensor_reduce(edge[:, ds(g * (Q * H) + J0 * H, Q * H)].rearrange("p (q h) -> p q h", h=H),
                                      picked[:, par, :, :, :].rearrange("p q a h -> p q h a"), AX.X, ALU.add).then_inc(el_picked, 1)
            pipelined(dve, PCOLS // Q, 4, 3, pick)
            dve.wait_ge(el_picked, PCOLS // Q)

            blocks = [(n, c, b) for n, c in enumerate((GAT, GCN)) for b in range(c.blocks)]

            def to_turn(i):
                n, c, b = blocks[i]
                if b == 0:
                    dve.wait_ge(srcdst_in[n], 16 * 2 * c.blocks)
                half = b_f[:, i % 2, :, 0:c.edges]
                issue(dve.tensor_copy(half[:, 0, :], b_i[n][:, b, 0, :]))
                issue(dve.tensor_scalar(half[:, 1, :], b_i[n][:, b, 1, :], tile0[n][:, b:b + 1], -1.0,
                                        ALU.subtract, ALU.mult))
                marks[f"block{i}"] = prep[0]

            to_turn(0)
            for i, (n, c, b) in enumerate(blocks):
                if i + 1 < len(blocks):
                    to_turn(i + 1)
                n_w = min(P, c.steps - b * P)
                turned()
                got = tr[i % 2][:, 0:2 * c.edges].rearrange("p (s c w) -> p s w c", s=2, c=c.chunks)
                at = slice(b * P * c.chunks, (b * P + n_w) * c.chunks)
                issue(dve.tensor_copy(src_step[n][:, at].rearrange("p (w c) -> p w c", c=c.chunks), got[:, 0, 0:n_w, :]))
                issue(dve.tensor_copy(ndrel[n][:, at].rearrange("p (w c) -> p w c", c=c.chunks), got[:, 1, 0:n_w, :]))
            settle()
            marks["tables"] = prep[0]

            dve.wait_ge(borders_in, 32)
            did(dve.tensor_copy(edgecols[:, :], edgecols_i[:, :]))
            did(dve.tensor_tensor(cont[:, 1:J], dst_f[:, 1:J], dst_f[:, 0:J - 1], ALU.is_equal))
            did(dve.tensor_tensor(cont[:, 0:1], dst_f[:, 0:1], edgecols[:, 0:1], ALU.is_equal))
            did(dve.tensor_tensor(cont[:, J:J + 1], dst_f[:, J - 1:J], edgecols[:, 1:2], ALU.is_equal))
            did(dve.tensor_scalar(pen, cont, -1.0, BIG, ALU.add, ALU.mult))

            def carries(local, is_max, back):
                flags = cont[:, 1:J + 1] if back else cont[:, 0:J]
                for h in range(H):
                    local(h)
                settle()
                issue(dve.tensor_copy(tail_st[:, 0, :], top[:, 0 if back else J - 1, :]))
                did(dve.tensor_reduce(carry[:, 0:1], flags, AX.X, ALU.min))
                if is_max:
                    did(dve.tensor_scalar(carry[:, 0:1], carry[:, 0:1], -1.0, BIG, ALU.add, ALU.mult))
                did(dve.tensor_copy(tail_st[:, 1, :], carry[:, 0:1].to_broadcast([P, H])))
                marks.setdefault("ends", []).append(prep[0])
                turned()
                did(dve.tensor_copy(carry_row[:, 0:2, 0:P], misc[0:H, 0:2 * P].rearrange("p (s n) -> p s n", s=2)))
                start = -BIG if is_max else 0.0
                edge_col = P if back else 0
                did(dve.memset(carry_row[:, 2, edge_col:edge_col + 1], start))
                ops = (ALU.add, ALU.max) if is_max else (ALU.mult, ALU.add)
                if back:
                    did(dve.tensor_tensor_scan(carry_row[:, 2, 0:P][:, ::-1], carry_row[:, 1, 0:P][:, ::-1],
                                               carry_row[:, 0, 0:P][:, ::-1], start, *ops))
                else:
                    did(dve.tensor_tensor_scan(carry_row[:, 2, 1:P + 1], carry_row[:, 1, 0:P],
                                               carry_row[:, 0, 0:P], start, *ops))
                marks.setdefault("carried", []).append(prep[0])
                turned()
                did(dve.tensor_copy(carry[:, :], sm[1][:, 0:H]))

            dve.wait_ge(er_in, 16)

            def er_local(h):
                issue(dve.tensor_tensor_scan(top[:, :, h], cont[:, 0:J], er[:, :, h], 0.0, ALU.mult, ALU.add))
            carries(er_local, False, False)
            for h in range(H):
                issue(dve.tensor_tensor_scan(er[:, :, h], cont[:, 0:J], er[:, :, h], carry[:, h:h + 1], ALU.mult, ALU.add))
            settle()

            dve.wait_ge(el_placed, EL_BATCHES)

            def top_local(h):
                issue(dve.tensor_tensor_scan(top[:, :, h], pen[:, 0:J], el[:, :, h], -BIG, ALU.add, ALU.max))
            carries(top_local, True, False)
            for h in range(H):
                issue(dve.tensor_tensor_scan(top[:, :, h], pen[:, 0:J], el[:, :, h], carry[:, h:h + 1], ALU.add, ALU.max))
            settle()
            marks["top"] = prep[0]

            def back_local(h):
                issue(dve.tensor_tensor_scan(top[:, ::-1, h], pen[:, 1:J + 1][:, ::-1], top[:, ::-1, h], -BIG,
                                             ALU.add, ALU.max))
            carries(back_local, True, True)
            for h in range(H):
                issue(dve.tensor_tensor_scan(top[:, ::-1, h], pen[:, 1:J + 1][:, ::-1], top[:, ::-1, h],
                                             carry[:, h:h + 1], ALU.add, ALU.max))
            settle()
            for at in halves:
                issue(dve.tensor_tensor(top[:, at, :], top[:, at, :], er[:, at, :], ALU.add))
            settle()
            dve.wait_ge(e_set, 2)
            for half, at in enumerate(halves):
                did(dve.scalar_tensor_tensor(el[:, at, :], el[:, at, :], SLOPE, el[:, at, :], ALU.mult, ALU.max))
                did(dve.scalar_tensor_tensor(top[:, at, :], top[:, at, :], SLOPE, top[:, at, :], ALU.mult, ALU.max))
                did(dve.tensor_tensor(el[:, at, :], el[:, at, :], top[:, at, :], ALU.subtract))
                marks[f"arg{half}"] = prep[0]
            did(dve.memset(big[:, 0:scanned], 0.0))
            dve.wait_ge(w_kept, 32)
            for b in range(GAT.blocks):
                n_w = min(P, SP - b * P)
                for q in range(4):
                    i = 4 * b + q
                    dve.wait_ge(w_turned, i + 1)
                    dve.tensor_copy(w_step[:, b * P:b * P + n_w, 4 * q:4 * q + 4],
                                    tr[i % 2][:, :].rearrange("p (q w) -> p w q", q=4)[:, 0:n_w, :]).then_inc(w_placed, 1)
            dve.wait_ge(w_placed, 4 * GAT.blocks)

            def aggregate(a, weighted):
                per = 2 if weighted else 1
                c, offs = a["cut"], [None]

                def step(s):
                    if weighted and s.live():
                        w, u = s.k, s.j % c.slots
                        dve.wait_ge(a["rows_in"][u], (w - u) * 8 + 32)
                        view = rows[:, 2 * u:2 * u + 2, :].rearrange("p c (h f) -> p c h f", f=F)
                        weights = w_step[:, w, :].rearrange("p (c h) -> p c h", c=2)
                        dve.tensor_tensor(view, view, weights.unsqueeze(3).to_broadcast([P, 2, H, F]),
                                          ALU.mult).then_inc(a["msg_set"], 1)
                        dve.tensor_copy(rows_w[:, 2 * u:2 * u + 2, D:AW], weights).then_inc(a["msg_set"], 1)
                    if s.j % BANKS == 0:
                        _, offs[0] = nc.values_load_multi_w_load_instructions(
                            a["slot"][0:1, ds(s.k, BANKS)], engines=(mybir.EngineType.DVE,), min_val=0,
                            max_val=(TILES - 1) * AW, skip_runtime_bounds_check_because="clamped when the table is made")
                    if s.live(LAG):
                        w, bank = s.k - LAG, (s.j - LAG) % BANKS
                        dve.wait_ge(a["step_sum"], w + 1)
                        if s.past(1, LAG):
                            dve.wait_ge(a["acc_added"], per * w)
                        o = offs[0][s.j % BANKS]
                        if weighted:
                            for half, bank_ps in enumerate((sum_ps[bank], half_ps[bank])):
                                part = big[:, ds(o + half * (AW // 2), AW // 2)]
                                dve.tensor_tensor(part, part, bank_ps[:, 0:AW // 2], ALU.add).then_inc(a["acc_added"], 1)
                        else:
                            dve.tensor_tensor(big[:, ds(o, D)], big[:, ds(o, D)], sum_ps[bank][:, :], ALU.add).then_inc(a["acc_added"], 1)
                pipelined(dve, c.steps, 2 * BANKS, LAG, step)
            dve.wait_ge(big_zeroed, 1)
            aggregate(agg[0], True)

            def bank_out(m, s, lag):
                if s.live(lag):
                    t, par = s.k - lag, (s.j - lag) % 2
                    dve.wait_ge(m["turned"], t + 1)
                    if s.past(2, lag):
                        dve.wait_ge(m["summed"], t - 1)
                    dve.tensor_copy(rows[:, 4 + par, :], tr[par][:, :]).then_inc(m["hT_set"], 1)

            dve.wait_ge(bval_in, 16)
            dve.wait_ge(agg[0]["acc_added"], 2 * SP)
            den = big[:, :].rearrange("p (t n) -> p t n", n=AW)[:, :, D:AW]
            dve.tensor_scalar(rden[:, :, :], den, 1e-16, None, ALU.max).then_inc(rden_set, 1)
            dve.wait_ge(rden_set, 1)
            dve.reciprocal(rden[:, :, :], rden[:, :, :]).then_inc(rden_set, 1)
            dve.wait_ge(rden_set, 2)

            def residual(s):
                if s.live():
                    t = s.k
                    a_t = acc(t).rearrange("p (h f) -> p h f", f=F)
                    dve.tensor_tensor(a_t, a_t, rden[:, t, :].unsqueeze(2).to_broadcast([P, H, F]),
                                      ALU.mult).then_inc(xr_scaled, 1)
                    t, par = s.k, s.j
                    dve.wait_ge(xr_in[par], slot_total(t, par))
                    dve.scalar_tensor_tensor(rows[:, par, :], bias[:, :], ind[:, ds(t, 1)], rows[:, par, :],
                                             ALU.mult, ALU.add).then_inc(xb_set, 1)
                if s.live(2):
                    t, par = s.k - 2, s.j
                    dve.wait_ge(x1_set, t + 1)
                    dve.bn_stats(x1_stats[:, par, :], acc(t)).then_inc(x1_stat, 1)
                    wait_alone("dve", dve, x1_stat, t + 1)
                    dve.bn_aggr(mv[:, par, :], x1_stats[:, par, :]).then_inc(x1_var, 1)
                if s.live(3):
                    t, par = s.k - 3, (s.j - 1) % 2
                    dve.wait_ge(x1_std, t + 1)
                    if s.past(2, 3):
                        dve.wait_ge(mids[0]["h_set"], t - 1)
                    dve.reciprocal(small[:, 7, par:par + 1], std[:, par:par + 1]).then_inc(x1_rstd, 1)
                    dve.wait_ge(x1_rstd, 2 * t + 1)
                    dve.tensor_tensor(rstd[:, par:par + 1], small[:, 7, par:par + 1], dinv[:, ds(t, 1)],
                                      ALU.mult).then_inc(x1_rstd, 1)
                    dve.wait_ge(x1_rstd, 2 * t + 2)
                    dve.tensor_scalar(nmr[:, par:par + 1], mv[:, par, 0:1], rstd[:, par:par + 1], -1.0,
                                      ALU.mult, ALU.mult).then_inc(x1_nmr, 1)
                bank_out(mids[0], s, 4)
            pipelined(dve, TILES, 2, 4, residual)

            dve.wait_ge(mids[0]["seeded"], TILES)
            aggregate(agg[1], False)

            dve.wait_ge(b_in[0], 16)
            dve.wait_ge(agg[1]["acc_added"], GCN.steps)

            def between(s):
                if s.live():
                    t = s.k
                    dve.scalar_tensor_tensor(acc(t), acc(t), dinv[:, ds(t, 1)], bias[:, :],
                                             ALU.mult, ALU.add).then_inc(mids[1]["y_set"], 1)
                bank_out(mids[1], s, 2)
            pipelined(dve, TILES, 2, 2, between)

            dve.wait_ge(mids[1]["seeded"], TILES)
            aggregate(agg[2], False)

            dve.wait_ge(b_in[1], 16)
            dve.wait_ge(agg[2]["acc_added"], GCN.steps)

            def finish(s, base, x1):
                if s.live():
                    t = s.k + base
                    dve.scalar_tensor_tensor(acc(t), acc(t), dinv[:, ds(t, 1)], bias[:, :],
                                             ALU.mult, ALU.add).then_inc(y_set, 1)
                if s.live(1):
                    t = s.k - 1 + base
                    dve.wait_ge(y_set, t + 1)
                    dve.scalar_tensor_tensor(acc(t), acc(t), 0.0, x1(s.k - 1, (s.j - 1) % OS),
                                             ALU.max, ALU.add).then_inc(out_set, 1)

            dve.wait_ge(x1_early_in, 16 * EARLY_X1)
            pipelined(dve, EARLY_X1, OS, 1, lambda s: finish(s, 0, lambda k, slot: edge[:, ds(k * D, D)]))

            def loaded(k, slot):
                dve.wait_ge(x1_in[slot], (k - slot) * (16 // OS) + 16)
                return rows[:, slot, :]
            pipelined(dve, TILES - EARLY_X1, OS, 1, lambda s: finish(s, EARLY_X1, loaded))

        @block.sync
        def _(sp):
            sp.dma_start(src_rows.rearrange("g e -> (g e)")[0:E].rearrange("(a n) -> a n", a=16),
                         src.rearrange("(a n) -> a n", a=16)).then_inc(edges_kept, 16)
            sp.dma_start(dst_rows.rearrange("g e -> (g e)")[0:E].rearrange("(a n) -> a n", a=16),
                         dst.rearrange("(a n) -> a n", a=16)).then_inc(edges_kept, 16)
            sp.wait_ge(pad_set, 2)
            sp.dma_start(src_rows.rearrange("g e -> (g e)")[E:EP].rearrange("(a n) -> a n", a=1),
                         pad_i[:, 0, :]).then_inc(edges_kept, 16)
            sp.dma_start(dst_rows.rearrange("g e -> (g e)")[E:EP].rearrange("(a n) -> a n", a=1),
                         pad_i[:, 1, :]).then_inc(edges_kept, 16)
            sp.wait_ge(edges_kept, 64)
            dst_line = dst_rows.rearrange("g e -> (g e)")

            def load_firsts(n, c):
                by_group = dst_line.rearrange("(g e) -> g e", e=c.edges)
                with nc.allow_non_contiguous_dma(reason="first and last dst of every group"):
                    for s in range(2):
                        sp.dma_start(g_i[n][s], by_group[:, s * (c.edges - 1):s * (c.edges - 1) + 1].rearrange(
                            "g e -> e g")).then_inc(firsts_in[n], 16)
            load_firsts(0, GAT)
            load_firsts(1, GCN)
            sp.dma_start(W_src_sb[:, :, :], W_src.rearrange("(k p) n -> p k n", p=P)).then_inc(fold_in, 16)
            sp.dma_start(W_dst_sb, W_dst.rearrange("(k p) n -> p k n", p=P)).then_inc(fold_in, 16)
            sp.dma_start(attn_sb[:, 0, :], on_all(attn_l.rearrange("h f -> (h f)"))).then_inc(fold_in, 16)
            sp.dma_start(attn_sb[:, 1, :], on_all(attn_r.rearrange("h f -> (h f)"))).then_inc(fold_in, 16)
            sp.dma_start(bsd_sb[:, 0, :], on_all(b_src)).then_inc(fold_in, 16)
            sp.dma_start(bsd_sb[:, 1, :], on_all(b_dst)).then_inc(fold_in, 16)
            sp.dma_start(bias[:, :], on_all(b_val)).then_inc(bval_in, 16)
            dst_flat = dst_line.rearrange("(p j) -> p j", j=J)
            sp.dma_start(dst_i, dst_flat).then_inc(dst_in, 16)
            sp.wait_ge(pad_set, 4)
            for c in range(TILES // XL):
                sp.dma_start(big[:, c * XL * D:(c + 1) * XL * D].rearrange("p (t d) -> p t d", d=D),
                             x[c * XL * P:(c + 1) * XL * P, :].rearrange("(t p) d -> p t d", p=P)).then_inc(x_in[c], 16)
            sp.dma_start(first(TILES - 1)[0:LAST, :], x[(TILES - 1) * P:N, :]).then_inc(x_in[TILES // XL], 16)
            sp.dma_start(src_flat[:, :], src_rows.rearrange("g e -> (g e)").rearrange("(p j) -> p j", j=J)).then_inc(edges_in, 16)
            sp.wait_ge(folded, 10)
            sp.dma_start(wmat[:, :, 0:D], W_val.rearrange("(k p) n -> p k n", p=P)).then_inc(wval_in, 16)
            with nc.allow_non_contiguous_dma(reason="single dst at the borders of partitions"):
                sp.dma_start(edgecols_i[1:P, 0:1], dst_flat[0:P - 1, J - 1:J]).then_inc(borders_in, 16)
                sp.dma_start(edgecols_i[0:P - 1, 1:2], dst_flat[1:P, 0:1]).then_inc(borders_in, 16)
            def keep_v(s):
                t, par = s.k, s.j
                sp.wait_ge(v_set, 2 * t + 2)
                sp.dma_start(v_tab[ds(t * P, P), :], rows[:, par, :]).then_inc(v_kept[par], 16)
            pipelined(sp, TILES, 2, 0, keep_v)
            sp.wait_ge(eler_set, TILES)
            sp.dma_start(el_tab.rearrange("(t p) h -> p t h", p=P), eler[:, :, 0:H]).then_inc(el_kept, 16)
            sp.dma_start(wmat[:, :, 0:D], W1.rearrange("(k p) n -> p k n", p=P)).then_inc(mids[0]["w_in"], 16)
            sp.wait_ge(dve_prep, marks["er_zero"])
            sp.dma_start(er_tab[0:EP, :].rearrange("(p j) h -> p (j h)", j=J),
                         er.rearrange("p j h -> p (j h)")).then_inc(er_zeroed, 16)
            sp.wait_ge(dve_prep, marks["low_T"])
            sp.dma_start(low_tab.rearrange("(b r) n -> r b n", r=P), low_T[:, :, :]).then_inc(low_kept, 16)
            sp.wait_ge(low_kept, 16)

            def load_low(s):
                if s.past(4):
                    sp.wait_ge(src_hot_set, (s.k - 3) * KT)
                sp.dma_start(low_all[:, s.j, :], low_tab[ds(s.k * Q, Q), :].rearrange("q n -> (q n)").rearrange(
                    "(a n) -> a n", a=1).broadcast_to([P, Q * P])).then_inc(low_in[s.j], 16)
            pipelined(sp, PCOLS // Q, 4, 0, load_low)
            sp.wait_ge(er_scattered, 16 * TILES)
            sp.dma_start(er.rearrange("p j h -> p (j h)"),
                         er_tab[0:EP, :].rearrange("(p j) h -> p (j h)", j=J)).then_inc(er_in, 16)
            by_part = w_tab.rearrange("g n -> (g n)").rearrange("(p n) -> p n", p=P)
            for half, at in enumerate(halves):
                at = slice(at.start * H, at.stop * H)
                sp.wait_ge(w_exp, half + 1)
                sp.dma_start(by_part[:, at], edge[:, at]).then_inc(w_kept, 16)

            sp.wait_ge(rden_set, 2)

            def keep_table(m, tab, s, lag):
                if s.live(lag):
                    t, par = s.k - lag, (s.j - lag) % 2
                    sp.wait_ge(m["tab_set"], t + 1)
                    sp.dma_start(tab[ds(t * P, P), :], rows[:, 6 + par, :]).then_inc(m["kept"][par], 16)

            def residual(s):
                t, par = s.k, s.j
                if s.live():
                    if s.past(2):
                        sp.wait_ge(x1_set, t - 1)
                    if s.inner or t < TILES - 1:
                        sp.dma_start(rows[:, par, :], x[ds(t * P, P), :]).then_inc(xr_in[par], 16)
                    else:
                        sp.dma_start(rows[0:LAST, par, :], x[t * P:N, :]).then_inc(xr_in[par], 16)
                if s.live(2):
                    t = s.k - 2
                    sp.wait_ge(x1_set, t + 1)
                    sp.dma_start(x1_tab[ds(t * P, P), :], acc(t)).then_inc(x1_kept[par], 16)
                keep_table(mids[0], h2_tab, s, 6)
            pipelined(sp, TILES, 2, 6, residual, tail=1)
            sp.wait_ge(xb_set, TILES)
            sp.dma_start(bias[:, :], on_all(b1)).then_inc(b_in[0], 16)
            sp.wait_ge(mids[0]["summed"], TILES)
            sp.dma_start(wmat[:, :, 0:D], W2.rearrange("(k p) n -> p k n", p=P)).then_inc(mids[1]["w_in"], 16)

            all_kept(sp, x1_kept)

            def fetch_early(s):
                sp.wait_ge(agg[1]["acc_added"], s.k * 32 + 32)
                sp.dma_start(edge[:, ds(s.k * D, D)], x1_tab[ds(s.k * P, P), :]).then_inc(x1_early_in, 16)
            assert 32 * EARLY_X1 <= GCN.steps
            pipelined(sp, EARLY_X1, 2, 0, fetch_early)

            def between(s):
                keep_table(mids[1], h3_tab, s, 0)
            pipelined(sp, TILES, 2, 0, between)
            sp.wait_ge(mids[1]["y_set"], TILES)
            sp.dma_start(bias[:, :], on_all(b2)).then_inc(b_in[1], 16)

            sp.wait_ge(agg[2]["acc_added"], GCN.steps)

            def load_x1(k, slot):
                sp.dma_start(rows[:, slot, :], x1_tab[ds((k + EARLY_X1) * P, P), :]).then_inc(x1_in[slot], 16)
            for slot in range(OS):
                load_x1(slot, slot)

            def keep_early(s):
                t = s.k
                sp.wait_ge(out_set, t + 1)
                sp.dma_start(out[ds(t * P, P), :], acc(t)).then_inc(out_kept, 16)
            pipelined(sp, EARLY_X1, OS, 0, keep_early)

            def keep_late(s):
                t = s.k + EARLY_X1
                sp.wait_ge(out_set, t + 1)
                if s.inner or t < TILES - 1:
                    sp.dma_start(out[ds(t * P, P), :], acc(t)).then_inc(out_kept, 16)
                else:
                    sp.dma_start(out[t * P:N, :], acc(t)[0:LAST, :]).then_inc(out_kept, 16)
                if s.inner or t + OS < TILES:
                    load_x1(s.k + OS, s.j)
            pipelined(sp, TILES - EARLY_X1, OS, 0, keep_late, tail=OS + 1)
            sp.wait_ge(out_kept, 16 * TILES)

        @block.gpsimd
        def _(pool):
            pool.memset(pad_i[:, 0, :], 0).then_inc(pad_set, 1)
            pool.memset(pad_i[:, 1, :], NP - 1).then_inc(pad_set, 1)
            pool.memset(first(TILES - 1), 0.0).then_inc(pad_set, 1)
            pool.memset(edgecols_i[:, :], -1).then_inc(pad_set, 1)
            pool.memset(ident[:, :], 0.0).then_inc(const_set, 1)
            pool.memset(ones[:, :], 1.0).then_inc(const_set, 1)
            pool.memset(tri[:, :], 1.0).then_inc(const_set, 1)
            pool.memset(epsc[:, :], EPS).then_inc(const_set, 1)
            pool.memset(twoc[:, :], 2.0).then_inc(const_set, 1)
            pool.iota(iota_i[:, :], pattern=[[1, P]], base=0, channel_multiplier=0).then_inc(const_set, 1)
            pool.iota(node_i[:, :], pattern=[[P, TILES]], base=EP, channel_multiplier=1).then_inc(const_set, 1)
            pool.iota(low_i4[:, :], pattern=[[P, KT]], base=0, channel_multiplier=1).then_inc(const_set, 1)
            pool.iota(step_i[:, :], pattern=[[P, GCN.blocks]], base=0, channel_multiplier=1).then_inc(const_set, 1)
            pool.wait_ge(const_set, 5)
            pool.affine_select(out=ident[:, :], in_=ident[:, :], compare_op=ALU.not_equal, fill=1.0, base=0,
                               pattern=[[-1, P]], channel_multiplier=1).then_inc(ident_set, 1)
            pool.affine_select(out=tri[:, :], in_=tri[:, :], compare_op=ALU.is_gt, fill=0.0, base=0,
                               pattern=[[1, P]], channel_multiplier=-1).then_inc(ident_set, 1)

            pool.wait_ge(folded, 10)
            pool.iota(step_of, pattern=[[1, GCN.blocks * P]], base=0, channel_multiplier=0).then_inc(step_of_set, 1)

            pool.wait_ge(h_set, TILES)
            for n, c in enumerate((GAT, GCN)):
                pool.wait_ge(dve_prep, marks[f"gidx{n}"])
                for b in range(c.blocks):
                    for s, tab in enumerate((src_rows, dst_rows)):
                        by_group = tab if c.chunks == 2 else tab.rearrange("g (c e) -> (g c) e", e=c.edges)
                        pool.indirect_dma_start(b_i[n][:, b, s, :], None, by_group,
                                                bass.IndirectOffsetOnAxis(ap=gidx[n][:, b:b + 1], axis=0)).then_inc(srcdst_in[n], 16)

            pool.wait_ge(el_kept, 16)
            pool.wait_ge(edges_in, 16)

            def batch(s):
                g, b = s.k, s.j
                if s.live():
                    pool.tensor_copy(el_idx[:, b, :], src_flat[:, ds(g * EB, EB)]).then_inc(el_idx_set, 1)
                    wait_alone("pool", pool, el_idx_set, g + 1)
                    for n in range(EB):
                        pool.indirect_dma_start(
                            el_rows[:, b, n * H:(n + 1) * H], None, el_tab,
                            bass.IndirectOffsetOnAxis(ap=el_idx[:, b, n:n + 1], axis=0)).then_inc(el_in[b], 16)
                if s.live(1):
                    g, b = s.k - 1, (s.j - 1) % 2
                    wait_alone("pool", pool, el_in[b], (g - b) * (8 * EB) + 16 * EB)
                    pool.tensor_copy(edge[:, ds(g * (EB * H), EB * H)], el_rows[:, b, :]).then_inc(el_placed, 1)
                    wait_alone("pool", pool, el_placed, g + 1)
            for k in range(2):
                batch(Step(k, k, EL_BATCHES, False))
            with pool.Fori(0, (EARLY - 2) // 2) as i:
                for j in range(2):
                    batch(Step(i * 2 + (2 + j), j, EL_BATCHES, True))
            pool.wait_ge(er_idx_set, 1)
            pool.wait_ge(er_zeroed, 16)
            with pool.Fori(0, TILES // SB) as i:
                pool.tensor_copy(sc_idx[:, :], er_idx[:, ds(i * SB, SB)]).then_inc(sc_idx_set, 1)
                pool.tensor_copy(sc_rows[:, :, :], eler[:, ds(i * SB, SB), H:2 * H]).then_inc(sc_idx_set, 1)
                wait_alone("pool", pool, sc_idx_set, i * 2 + 2)
                for n in range(SB):
                    pool.indirect_dma_start(er_tab, bass.IndirectOffsetOnAxis(ap=sc_idx[:, n:n + 1], axis=0),
                                            sc_rows[:, n, :], None).then_inc(er_scattered, 16)
                wait_alone("pool", pool, er_scattered, (i + 1) * (16 * SB))
            with pool.Fori(0, (EL_BATCHES - EARLY) // 2) as i:
                for j in range(2):
                    batch(Step(i * 2 + (EARLY + j), j, EL_BATCHES, True))
            batch(Step(EL_BATCHES, 0, EL_BATCHES, False))
            pool.wait_ge(dve_prep, marks["top"])
            for at in halves:
                pool.tensor_tensor(el[:, at, :], el[:, at, :], er[:, at, :], ALU.add).then_inc(e_set, 1)
            pool.memset(big[:, scanned:], 0.0).then_inc(big_zeroed, 1)
            pool.wait_ge(w_kept, 32)
            for b in range(GAT.blocks):
                if b >= 2:
                    pool.wait_ge(w_turned, 4 * (b - 1))
                pool.indirect_dma_start(w_rows[:, b % 2, :], None, w_tab,
                                        bass.IndirectOffsetOnAxis(ap=gidx[0][:, b:b + 1], axis=0)).then_inc(w_in[b], 16)

            def gather(tab, a):
                c = a["cut"]
                per = IDX // c.chunks

                def step(s):
                    w, u, b = s.k, s.j % c.slots, s.j // per
                    if s.past(c.slots):
                        wait_alone("pool", pool, a["step_sum"], w - c.slots + 1)
                    if s.j % per == 0:
                        pool.tensor_copy(row_idx[:, b, :], a["src"][:, ds(w * c.chunks, IDX)]).then_inc(a["idx_set"], 1)
                        wait_alone("pool", pool, a["idx_set"], s.turn * 2 + (b + 1))
                    for i in range(c.chunks):
                        slot, n = u * c.chunks + i, (s.j % per) * c.chunks + i
                        pool.indirect_dma_start(
                            rows[:, slot, :], None, tab,
                            bass.IndirectOffsetOnAxis(ap=row_idx[:, b, n:n + 1], axis=0)).then_inc(a["rows_in"][u], 16)
                pipelined(pool, c.steps, 2 * per, 0, step)

            pool.wait_ge(dve_prep, marks["tables"])
            all_kept(pool, v_kept)
            gather(v_tab, agg[0])

            def seed(m, s, lag):
                if s.live(lag):
                    t, par = s.k - lag, (s.j - lag) % 2
                    wait_alone("pool", pool, m["tab_set"], t + 1)
                    pool.tensor_tensor(acc(t), rows[:, 6 + par, :], rows[:, 6 + par, :], ALU.add).then_inc(m["seeded"], 1)

            def residual(s):
                if s.live():
                    t, par = s.k, s.j
                    wait_alone("pool", pool, xr_scaled, t + 1)
                    wait_alone("pool", pool, xb_set, t + 1)
                    pool.tensor_tensor(acc(t), acc(t), rows[:, par, :], ALU.add).then_inc(x1_set, 1)
                if s.live(5):
                    t, par = s.k - 5, (s.j - 5) % 2
                    wait_alone("pool", pool, x1_kept[par], slot_total(t, par))
                seed(mids[0], s, 5)
            pipelined(pool, TILES, 2, 5, residual)
            all_kept(pool, mids[0]["kept"])
            all_kept(pool, x1_kept)
            gather(h2_tab, agg[1])

            def between(s):
                seed(mids[1], s, 3)
            pipelined(pool, TILES, 2, 3, between)
            all_kept(pool, mids[1]["kept"])
            gather(h3_tab, agg[2])

        @block.scalar
        def _(act):
            act.wait_ge(const_set, 9)

            act.wait_ge(ln_set, 7)
            act.activation(ln[:, 3, :], ln[:, 1, :], ACT.Sqrt, bias=epsc[:, 0:1]).then_inc(std_set, 1)
            act.wait_ge(ln_set, 9)

            def first_layer(s):
                if s.live():
                    t, par = s.k, s.j
                    if s.past(2):
                        act.wait_ge(h_turned, t - 1)
                    act.activation(rows[:, 2 + par, :], first(t), ACT.Relu,
                                   bias=ln[:, 1, ds(t, 1)], scale=ln[:, 2, ds(t, 1)]).then_inc(h_set, 1)
                if s.live(2):
                    t, par = s.k - 2, s.j
                    act.wait_ge(v_sum, t + 1)
                    if s.past(2, 2):
                        act.wait_ge(v_kept[par], slot_total(t - 2, par))
                    act.activation(rows[:, par, 0:HALF], mm[par][:, 0:HALF], ACT.Copy).then_inc(v_set, 1)
                    act.activation(rows[:, par, HALF:D], sm[par][:, 0:D - HALF], ACT.Copy).then_inc(v_set, 1)
            pipelined(act, TILES, 2, 2, first_layer)

            act.wait_ge(dve_prep, marks["hist"])
            act.activation(small[:, 6, :], hist[:, :], ACT.Sqrt, bias=twoc[:, 0:1]).then_inc(std_deg, 1)
            for half, at in enumerate(halves):
                act.wait_ge(dve_prep, marks[f"arg{half}"])
                act.activation(el[:, at, :], el[:, at, :], ACT.Exp).then_inc(w_exp, 1)

            def make_onehots(a):
                per = 2 // a["cut"].chunks

                def pair(s):
                    n = s.k
                    if s.past(1):
                        act.wait_ge(a["onehot_set"], n)
                    for c in range(2):
                        act.activation(dist[:, c, :], iota[:, :], ACT.Abs,
                                       bias=a["ndrel"][:, ds(n * 2 + c, 1)]).then_inc(a["dist_set"], 1)
                    act.wait_ge(a["dist_set"], 2 * n + 2)
                    if s.past(2):
                        act.wait_ge(a["step_sum"], per * (n - 1))
                    act.activation(onehot[:, s.j % 2, :, :], dist[:, :, :], ACT.Relu,
                                   bias=ones[:, 0:1], scale=-1.0).then_inc(a["onehot_set"], 1)
                pipelined(act, a["cut"].steps // per, 4, 0, pair)

            act.wait_ge(dve_prep, marks["tables"])
            make_onehots(agg[0])

            def table_out(m, s, lag):
                if s.live(lag):
                    t, par = s.k - lag, (s.j - lag) % 2
                    act.wait_ge(m["summed"], t + 1)
                    if s.past(2, lag):
                        act.wait_ge(m["seeded"], t - 1)
                        act.wait_ge(m["kept"][par], slot_total(t - 2, par))
                    act.activation(rows[:, 6 + par, :], mm[par][:, :], ACT.Copy).then_inc(m["tab_set"], 1)

            def residual(s):
                if s.live(2):
                    t, par = s.k - 2, s.j
                    act.wait_ge(x1_var, t + 1)
                    act.activation(std[:, par:par + 1], mv[:, par, 1:2], ACT.Sqrt, bias=epsc[:, 0:1]).then_inc(x1_std, 1)
                if s.live(3):
                    t, par = s.k - 3, (s.j - 3) % 2
                    act.wait_ge(x1_nmr, t + 1)
                    if s.past(2, 3):
                        act.wait_ge(mids[0]["turned"], t - 1)
                    act.activation(rows[:, 2 + par, :], acc(t), ACT.Relu,
                                   bias=nmr[:, par:par + 1], scale=rstd[:, par:par + 1]).then_inc(mids[0]["h_set"], 1)
                table_out(mids[0], s, 5)
            pipelined(act, TILES, 2, 5, residual)

            make_onehots(agg[1])

            def between(s):
                if s.live(1):
                    t, par = s.k - 1, (s.j - 1) % 2
                    act.wait_ge(mids[1]["y_set"], t + 1)
                    if s.past(2, 1):
                        act.wait_ge(mids[1]["turned"], t - 1)
                    act.activation(rows[:, 2 + par, :], acc(t), ACT.Relu,
                                   scale=dinv[:, ds(t, 1)]).then_inc(mids[1]["h_set"], 1)
                table_out(mids[1], s, 3)
            pipelined(act, TILES, 2, 3, between)
            make_onehots(agg[2])

        @block.tensor
        def _(pe):
            pe.wait_ge(ident_set, 2)
            pe.wait_ge(dve_prep, marks["groups1"])
            for n, c in enumerate((GAT, GCN)):
                for v in range(2):
                    for g in range(c.blocks):
                        last = pe.matmul(sm[0][:, v * c.blocks + g:v * c.blocks + g + 1], g_row[n][:, v, g * P:(g + 1) * P],
                                         ones[0:1, 0:1], start=True, stop=True)
                last.then_inc(pe_prep, 1)
                pe.wait_ge(dve_prep, marks[f"from{n}"])
                for b in range(c.blocks):
                    for g in range(c.blocks):
                        last = pe.matmul(sm[1][:, 2 * b:2 * b + 2], g_from[n][:, g, b * P:(b + 1) * P], g_val[n][:, g, :],
                                         start=(g == 0), stop=(g == c.blocks - 1))
                last.then_inc(pe_prep, 1)
                pe.wait_ge(dve_prep, marks[f"slots{n}"])
                for b in range(c.blocks):
                    last = pe.matmul(mm[b // BANKS][0:1, b % BANKS * P:(b % BANKS + 1) * P],
                                     stepcols[n][:, 5, b:b + 1], ident[:, :], start=True, stop=True)
                last.then_inc(pe_prep, 1)
            pe.wait_ge(dve_prep, marks["slots_out1"])
            pe.wait_ge(folded, 10)
            pe.wait_ge(wval_in, 16)

            def turn(bank, slot, done):
                for k in range(KC):
                    last = nc.tensor.transpose(bank[:, k * P:(k + 1) * P], rows[:, slot, k * P:(k + 1) * P], ident[:, :])
                last.then_inc(done, 1)

            def product(bank, slot, rhs, done):
                for k in range(KC):
                    last = nc.tensor.matmul(bank, rows[:, slot, k * P:(k + 1) * P], rhs(k), start=(k == 0), stop=(k == KC - 1))
                last.then_inc(done, 1)

            def first_layer(s):
                if s.live():
                    t, par = s.k, s.j
                    pe.wait_ge(h_set, t + 1)
                    if s.past(2):
                        pe.wait_ge(hT_set, t - 1)
                    turn(tr[par], 2 + par, h_turned)
                if s.live(1):
                    t, par = s.k - 1, (s.j - 1) % 2
                    pe.wait_ge(hT_set, t + 1)
                    if s.past(2, 1):
                        pe.wait_ge(eler_set, t - 1)
                        pe.wait_ge(v_set, 2 * (t - 1))
                    for k in range(KC):
                        for half, bank in enumerate((mm[par], sm[par])):
                            last = pe.matmul(bank[:, 0:HALF], rows[:, 4 + par, k * P:(k + 1) * P],
                                             wmat[:, k, half * HALF:(half + 1) * HALF], start=(k == 0), stop=(k == KC - 1))
                    last.then_inc(v_sum, 1)
                if s.inner or s.k < HB:
                    b, par = s.k, s.j
                    pe.wait_ge(hot_set, 2 * b + 2)
                    for j in range(JB):
                        last = pe.matmul(hist_ps[:, 0:TILES], hot_low[:, par, j, :], hot_blk[:, par, j, :],
                                         start=(not s.inner and b == 0 and j == 0),
                                         stop=(not s.inner and b == HB - 1 and j == JB - 1))
                    last.then_inc(hot_used, 1)
            pipelined(pe, TILES, 2, 1, first_layer, tail=4)

            pe.wait_ge(dve_prep, marks["hist"])
            pe.matmul(misc[:, 0:TILES], ones[:, :], hist[:, :], start=True, stop=True)
            pe.matmul(sm[0][:, 0:TILES], tri[:, :], hist[:, :], start=True, stop=True).then_inc(pe_prep, 1)

            pe.wait_ge(dve_prep, marks["low"])
            for b in range(PB):
                last = pe.transpose((misc, hist_ps)[b // 4][:, b % 4 * P:(b % 4 + 1) * P], low_f[:, b * P:(b + 1) * P], ident[:, :])
            last.then_inc(pe_prep, 1)

            def pick(s):
                g, par, bank = s.k, s.j % 2, s.j
                pe.wait_ge(src_hot_set, (g + 1) * KT)
                if s.past(4):
                    pe.wait_ge(el_masked, g - 3)
                for q in range(Q):
                    for kt in range(KT):
                        for part in range(3):
                            last = pe.matmul(sum_ps[bank][:, q * NA * H:(q + 1) * NA * H],
                                             src_hot[:, par, kt, q * P:(q + 1) * P], el_parts[:, part, kt::KT, :],
                                             start=(kt == 0 and part == 0), stop=(kt == KT - 1 and part == 2))
                last.then_inc(el_summed, 1)
            pipelined(pe, PCOLS // Q, 4, 0, pick)

            i = 0
            for c in (GAT, GCN):
                for b in range(c.blocks):
                    pe.wait_ge(dve_prep, marks[f"block{i}"])
                    for s in range(2):
                        for h in range(c.chunks):
                            last = pe.transpose(tr[i % 2][:, (c.chunks * s + h) * P:(c.chunks * s + h + 1) * P],
                                                b_f[:, i % 2, s, h * P:(h + 1) * P], ident[:, :])
                    last.then_inc(pe_prep, 1)
                    i += 1

            for n in range(3):
                pe.wait_ge(dve_prep, marks["ends"][n])
                for i in range(2):
                    last = pe.transpose(misc[0:H, i * P:(i + 1) * P], tail_st[:, i, :], ident[:, :])
                last.then_inc(pe_prep, 1)
                pe.wait_ge(dve_prep, marks["carried"][n])
                lo = 1 if n == 2 else 0
                pe.transpose(sm[1][:, 0:H], carry_row[:, 2, lo:lo + P], ident[0:H, 0:H]).then_inc(pe_prep, 1)

            for b in range(GAT.blocks):
                pe.wait_ge(w_in[b], 16)
                halves = w_rows[:, b % 2, :].rearrange("p (c e h) -> p c h e", c=2, h=H)
                for q in range(4):
                    i = 4 * b + q
                    if i >= 2:
                        pe.wait_ge(w_placed, i - 1)
                    for n in range(4):
                        c, h = divmod(4 * q + n, H)
                        last = pe.transpose(tr[i % 2][:, n * P:(n + 1) * P], halves[:, c, h, :], ident[:, :])
                    last.then_inc(w_turned, 1)

            def aggregate(a, weighted):
                c = a["cut"]
                per = 2 if weighted else 1

                def step(s):
                    w, u, bank = s.k, s.j % c.slots, s.j % BANKS
                    if weighted:
                        pe.wait_ge(a["onehot_set"], w + 1)
                        pe.wait_ge(a["msg_set"], 2 * w + 2)
                        hots = [onehot[:, s.j % 2, n, :] for n in range(2)]
                    else:
                        pe.wait_ge(a["onehot_set"], s.turn * (c.slots // 2) + (s.j // 2 + 1))
                        pe.wait_ge(a["rows_in"][u], (w - u) * 2 + 16)
                        hots = [onehot[:, s.j // 2 % 2, s.j % 2, :]]
                    if s.past(BANKS):
                        pe.wait_ge(a["acc_added"], per * (w - BANKS + 1))
                    halves = ((sum_ps[bank], 0, AW // 2), (half_ps[bank], AW // 2, AW)) if weighted else ((sum_ps[bank], 0, D),)
                    for n, hot in enumerate(hots):
                        for bank_ps, lo, hi in halves:
                            last = pe.matmul(bank_ps[:, 0:hi - lo], hot, rows_w[:, c.chunks * u + n, lo:hi],
                                             start=(n == 0), stop=(n == c.chunks - 1))
                    last.then_inc(a["step_sum"], 1)
                pipelined(pe, c.steps, 8, 0, step)

            pe.wait_ge(w_placed, 4 * GAT.blocks)
            aggregate(agg[0], True)

            def dense_layer(m, lag):
                pe.wait_ge(m["w_in"], 16)

                def step(s):
                    if s.live(lag):
                        t, par = s.k - lag, (s.j - lag) % 2
                        pe.wait_ge(m["h_set"], t + 1)
                        if s.past(2, lag):
                            pe.wait_ge(m["hT_set"], t - 1)
                        turn(tr[par], 2 + par, m["turned"])
                    if s.live(lag + 1):
                        t, par = s.k - lag - 1, (s.j - lag - 1) % 2
                        pe.wait_ge(m["hT_set"], t + 1)
                        if s.past(2, lag + 1):
                            pe.wait_ge(m["tab_set"], t - 1)
                        product(mm[par][:, :], 4 + par, lambda k: wmat[:, k, 0:D], m["summed"])
                pipelined(pe, TILES, 2, lag + 1, step)
            dense_layer(mids[0], 0)
            aggregate(agg[1], False)
            dense_layer(mids[1], 0)
            aggregate(agg[2], False)


_INS = ["x", "src", "dst", "L0_gnn_W_src", "L0_gnn_b_src", "L0_gnn_W_dst", "L0_gnn_b_dst", "L0_gnn_W_val", "L0_gnn_b_val",
        "L0_gnn_attn_l", "L0_gnn_attn_r", "L1_gnn_W1", "L1_gnn_b1", "L1_gnn_W2", "L1_gnn_b2"]


def kernel(**inputs):
    import concourse.bacc as bacc
    from concourse.bass_utils import run_bass_kernel_spmd as run

    nc = bacc.Bacc("TRN2", target_bir_lowering=False, num_devices=1)
    arrays, args = {}, []
    for name in _INS:
        a = np.ascontiguousarray(inputs[name])
        arrays[name] = a
        args.append(nc.dram_tensor(name, a.shape, mybir.dt.from_np(a.dtype), kind="ExternalInput").ap())
    out = nc.dram_tensor("out", [N, D], F32, kind="ExternalOutput").ap()
    build(nc, *args, out)
    return run(nc, [arrays], core_ids=[0]).results[0]["out"]
```
